# Optimizing a Trainium2 kernel written in Bass

```python
import numpy as np
import jax
import jax.numpy as jnp

def _softmax(x, axis=-1):
    return jax.nn.softmax(x, axis=axis)

def _gelu(x):
    return jax.nn.gelu(x, approximate=True)

def _silu(x):
    return jax.nn.silu(x)

def _sigmoid(x):
    return jax.nn.sigmoid(x)

def _layernorm(x, axis=-1, eps=1e-05):
    m = jnp.mean(x, axis=axis, keepdims=True)
    v = jnp.var(x, axis=axis, keepdims=True)
    return (x - m) / jnp.sqrt(v + eps)

def _scatter_add(tgt, idx, src, axis=0):
    return tgt.at[idx].add(src)

def _segment_sum(src, seg, n):
    return jax.ops.segment_sum(src, seg, n)
kernel_name = 'mk_macaron_d2_jaxref_r8_b8900c'

def setup_inputs(seed: int=0):
    np.random.seed(seed)
    _w = jnp.asarray

    def _L0_attn_setup():
        import jax, jax.numpy as jnp
        import numpy as np
        HEADS = 16
        key = jax.random.key(seed)
        ks = jax.random.split(key, 5)
        B, T, D = (2, 256, 256)
        s = 0.02
        return {'x': jax.random.normal(ks[0], (B, T, D), dtype=jnp.float32), 'Wq': jax.random.normal(ks[1], (D, D), dtype=jnp.float32) * s, 'Wk': jax.random.normal(ks[2], (D, D), dtype=jnp.float32) * s, 'Wv': jax.random.normal(ks[3], (D, D), dtype=jnp.float32) * s, 'Wo': jax.random.normal(ks[4], (D, D), dtype=jnp.float32) * s}
    _L0_attn_in = _L0_attn_setup()

    def _L0_ffn_setup():
        import jax, jax.numpy as jnp
        import numpy as np
        NUM_EXPERTS = 16
        TOP_K = 2
        HIDDEN = 256
        D_FF = 512
        BATCH, SEQ = (4, 256)

        def _moe_forward(hidden, router_w, W1, W2):
            B, S, D = hidden.shape
            x = hidden.reshape(-1, D)
            T = x.shape[0]
            logits = x @ router_w
            top_vals, top_ids = jax.lax.top_k(logits, TOP_K)
            probs = jax.nn.softmax(top_vals, axis=-1)
            combine = jnp.zeros((T, NUM_EXPERTS), dtype=x.dtype)
            combine = combine.at[jnp.arange(T)[:, None], top_ids].add(probs)
            out = jnp.zeros_like(x)
            for e in range(NUM_EXPERTS):
                h = jax.nn.silu(x @ W1[e]) @ W2[e]
                out = out + combine[:, e:e + 1] * h
            return out.reshape(B, S, D)
        key = jax.random.key(seed)
        k_h, k_r, k_w1, k_w2 = jax.random.split(key, 4)
        hidden = jax.random.normal(k_h, (BATCH, SEQ, HIDDEN), dtype=jnp.float32)
        router_w = jax.random.normal(k_r, (HIDDEN, NUM_EXPERTS), dtype=jnp.float32) * HIDDEN ** (-0.5)
        W1 = jax.random.normal(k_w1, (NUM_EXPERTS, HIDDEN, D_FF), dtype=jnp.float32) * HIDDEN ** (-0.5)
        W2 = jax.random.normal(k_w2, (NUM_EXPERTS, D_FF, HIDDEN), dtype=jnp.float32) * D_FF ** (-0.5)
        return {'hidden': hidden, 'router_w': router_w, 'W1': W1, 'W2': W2}
    _L0_ffn_in = _L0_ffn_setup()

    def _L1_attn_setup():
        import jax, jax.numpy as jnp
        import numpy as np
        B, S, DM = (2, 128, 256)
        H, HD, RD = (16, 128, 64)
        DQL, DKVL = (48, 64)
        THETA = 10000.0
        EPS = 1e-06

        def _rope_tables(seq, dim, theta):
            freqs = 1.0 / theta ** (jnp.arange(0, dim, 2, dtype=jnp.float32) / dim)
            t = jnp.arange(seq, dtype=jnp.float32)
            ang = jnp.outer(t, freqs)
            return (jnp.cos(ang), jnp.sin(ang))

        def _apply_rope(x, cos, sin):
            xr = x.reshape(x.shape[:-1] + (-1, 2))
            xe, xo = (xr[..., 0], xr[..., 1])
            c = cos[None, :, None, :]
            s = sin[None, :, None, :]
            return jnp.stack([xe * c - xo * s, xe * s + xo * c], axis=-1).reshape(x.shape)

        def _rmsnorm(x, w):
            return x * jax.lax.rsqrt(jnp.mean(x * x, axis=-1, keepdims=True) + EPS) * w

        def _reference_tuple_inner(x, Wq_down, q_norm_w, Wq_up, Wq_rope, Wkv_down, kv_norm_w, Wk_up, Wv_up, Wk_rope, Wout):
            b, s, _ = x.shape
            cos, sin = _rope_tables(s, RD, THETA)
            c_q = _rmsnorm(x @ Wq_down, q_norm_w)
            q = (c_q @ Wq_up).reshape(b, s, H, HD).transpose(0, 2, 1, 3)
            q_rope = _apply_rope((x @ Wq_rope).reshape(b, s, H, RD), cos, sin)
            q_rope = q_rope.transpose(0, 2, 1, 3)
            c_kv = _rmsnorm(x @ Wkv_down, kv_norm_w)
            k = (c_kv @ Wk_up).reshape(b, s, H, HD).transpose(0, 2, 1, 3)
            v = (c_kv @ Wv_up).reshape(b, s, H, HD).transpose(0, 2, 1, 3)
            k_rope = _apply_rope((x @ Wk_rope).reshape(b, s, H, RD), cos, sin)
            k_rope = k_rope.transpose(0, 2, 1, 3)
            scale = (HD + RD) ** (-0.5)
            scores = (jnp.einsum('bhqd,bhkd->bhqk', q, k) + jnp.einsum('bhqd,bhkd->bhqk', q_rope, k_rope)) * scale
            attn = jax.nn.softmax(scores, axis=-1)
            out = jnp.einsum('bhqk,bhkd->bhqd', attn, v)
            out = out.transpose(0, 2, 1, 3).reshape(b, s, H * HD) @ Wout
            return (out, attn)
        key = jax.random.key(seed)
        ks = jax.random.split(key, 9)
        sc = 0.02
        return {'x': jax.random.normal(ks[0], (B, S, DM), dtype=jnp.float32), 'Wq_down': jax.random.normal(ks[1], (DM, DQL), dtype=jnp.float32) * sc, 'q_norm_w': jnp.ones((DQL,), dtype=jnp.float32), 'Wq_up': jax.random.normal(ks[2], (DQL, H * HD), dtype=jnp.float32) * sc, 'Wq_rope': jax.random.normal(ks[3], (DM, H * RD), dtype=jnp.float32) * sc, 'Wkv_down': jax.random.normal(ks[4], (DM, DKVL), dtype=jnp.float32) * sc, 'kv_norm_w': jnp.ones((DKVL,), dtype=jnp.float32), 'Wk_up': jax.random.normal(ks[5], (DKVL, H * HD), dtype=jnp.float32) * sc, 'Wv_up': jax.random.normal(ks[6], (DKVL, H * HD), dtype=jnp.float32) * sc, 'Wk_rope': jax.random.normal(ks[7], (DM, H * RD), dtype=jnp.float32) * sc, 'Wout': jax.random.normal(ks[8], (H * HD, DM), dtype=jnp.float32) * sc}
    _L1_attn_in = _L1_attn_setup()

    def _L1_ffn_setup():
        import jax, jax.numpy as jnp
        import numpy as np
        B, S, D_IN, D_OUT, E, R = (4, 256, 256, 256, 8, 16)
        SCALING = 32.0 / 16.0
        key = jax.random.key(seed)
        ks = jax.random.split(key, 7)
        return {'x': jax.random.normal(ks[0], (B, S, D_IN), jnp.float32), 'base_w': jax.random.normal(ks[1], (D_OUT, D_IN), jnp.float32) * 0.02, 'base_b': jax.random.normal(ks[2], (D_OUT,), jnp.float32) * 0.02, 'router_w': jax.random.normal(ks[3], (E, D_IN), jnp.float32) * 0.02, 'router_b': jax.random.normal(ks[4], (E,), jnp.float32) * 0.02, 'lora_A': jax.random.normal(ks[5], (E, D_IN, R), jnp.float32) * 0.02, 'lora_B': jax.random.normal(ks[6], (E, R, D_OUT), jnp.float32) * 0.02}
    _L1_ffn_in = _L1_ffn_setup()
    _d = {'L0_attn_x': _L0_attn_in['x'], 'L0_attn_Wq': _L0_attn_in['Wq'], 'L0_attn_Wk': _L0_attn_in['Wk'], 'L0_attn_Wv': _L0_attn_in['Wv'], 'L0_attn_Wo': _L0_attn_in['Wo'], 'L0_ffn_router_w': _L0_ffn_in['router_w'], 'L0_ffn_W1': _L0_ffn_in['W1'], 'L0_ffn_W2': _L0_ffn_in['W2'], 'L1_attn_Wq_down': _L1_attn_in['Wq_down'], 'L1_attn_q_norm_w': _L1_attn_in['q_norm_w'], 'L1_attn_Wq_up': _L1_attn_in['Wq_up'], 'L1_attn_Wq_rope': _L1_attn_in['Wq_rope'], 'L1_attn_Wkv_down': _L1_attn_in['Wkv_down'], 'L1_attn_kv_norm_w': _L1_attn_in['kv_norm_w'], 'L1_attn_Wk_up': _L1_attn_in['Wk_up'], 'L1_attn_Wv_up': _L1_attn_in['Wv_up'], 'L1_attn_Wk_rope': _L1_attn_in['Wk_rope'], 'L1_attn_Wout': _L1_attn_in['Wout'], 'L1_ffn_base_w': _L1_ffn_in['base_w'], 'L1_ffn_base_b': _L1_ffn_in['base_b'], 'L1_ffn_router_w': _L1_ffn_in['router_w'], 'L1_ffn_router_b': _L1_ffn_in['router_b'], 'L1_ffn_lora_A': _L1_ffn_in['lora_A'], 'L1_ffn_lora_B': _L1_ffn_in['lora_B']}
    _x0 = _d['L0_attn_x']
    _d['L0_attn_x'] = jax.random.normal(jax.random.fold_in(jax.random.key(seed), 1), (2, 1024, 256), dtype=_x0.dtype)
    del _x0
    return _d

def reference(L0_attn_x, L0_attn_Wq, L0_attn_Wk, L0_attn_Wv, L0_attn_Wo, L0_ffn_router_w, L0_ffn_W1, L0_ffn_W2, L1_attn_Wq_down, L1_attn_q_norm_w, L1_attn_Wq_up, L1_attn_Wq_rope, L1_attn_Wkv_down, L1_attn_kv_norm_w, L1_attn_Wk_up, L1_attn_Wv_up, L1_attn_Wk_rope, L1_attn_Wout, L1_ffn_base_w, L1_ffn_base_b, L1_ffn_router_w, L1_ffn_router_b, L1_ffn_lora_A, L1_ffn_lora_B):

    def _L0_attn_ref(x, Wq, Wk, Wv, Wo):
        import jax, jax.numpy as jnp
        import numpy as np
        HEADS = 16
        B, T, _ = x.shape
        H = HEADS
        Dh = Wq.shape[1] // H
        q = (x @ Wq).reshape(B, T, H, Dh)
        k = (x @ Wk).reshape(B, T, H, Dh)
        v = (x @ Wv).reshape(B, T, H, Dh)
        scores = jnp.einsum('bthd,bshd->bhts', q, k)
        mask = jnp.tril(jnp.ones((T, T), dtype=scores.dtype))
        scores = scores * mask
        attn = jax.nn.softmax(scores / T ** 0.5, axis=-1)
        out = jnp.einsum('bhts,bshd->bthd', attn, v).reshape(B, T, H * Dh)
        return out @ Wo

    def _L0_ffn_ref(hidden, router_w, W1, W2):
        import jax, jax.numpy as jnp
        import numpy as np
        NUM_EXPERTS = 16
        TOP_K = 2
        HIDDEN = 256
        D_FF = 512
        BATCH, SEQ = (4, 256)

        def _moe_forward(hidden, router_w, W1, W2):
            B, S, D = hidden.shape
            x = hidden.reshape(-1, D)
            T = x.shape[0]
            logits = x @ router_w
            top_vals, top_ids = jax.lax.top_k(logits, TOP_K)
            probs = jax.nn.softmax(top_vals, axis=-1)
            combine = jnp.zeros((T, NUM_EXPERTS), dtype=x.dtype)
            combine = combine.at[jnp.arange(T)[:, None], top_ids].add(probs)
            out = jnp.zeros_like(x)
            for e in range(NUM_EXPERTS):
                h = jax.nn.silu(x @ W1[e]) @ W2[e]
                out = out + combine[:, e:e + 1] * h
            return out.reshape(B, S, D)
        return _moe_forward(hidden, router_w, W1, W2)

    def _L1_attn_ref(x, Wq_down, q_norm_w, Wq_up, Wq_rope, Wkv_down, kv_norm_w, Wk_up, Wv_up, Wk_rope, Wout):
        import jax, jax.numpy as jnp
        import numpy as np
        B, S, DM = (2, 128, 256)
        H, HD, RD = (16, 128, 64)
        DQL, DKVL = (48, 64)
        THETA = 10000.0
        EPS = 1e-06

        def _rope_tables(seq, dim, theta):
            freqs = 1.0 / theta ** (jnp.arange(0, dim, 2, dtype=jnp.float32) / dim)
            t = jnp.arange(seq, dtype=jnp.float32)
            ang = jnp.outer(t, freqs)
            return (jnp.cos(ang), jnp.sin(ang))

        def _apply_rope(x, cos, sin):
            xr = x.reshape(x.shape[:-1] + (-1, 2))
            xe, xo = (xr[..., 0], xr[..., 1])
            c = cos[None, :, None, :]
            s = sin[None, :, None, :]
            return jnp.stack([xe * c - xo * s, xe * s + xo * c], axis=-1).reshape(x.shape)

        def _rmsnorm(x, w):
            return x * jax.lax.rsqrt(jnp.mean(x * x, axis=-1, keepdims=True) + EPS) * w

        def _reference_tuple_inner(x, Wq_down, q_norm_w, Wq_up, Wq_rope, Wkv_down, kv_norm_w, Wk_up, Wv_up, Wk_rope, Wout):
            b, s, _ = x.shape
            cos, sin = _rope_tables(s, RD, THETA)
            c_q = _rmsnorm(x @ Wq_down, q_norm_w)
            q = (c_q @ Wq_up).reshape(b, s, H, HD).transpose(0, 2, 1, 3)
            q_rope = _apply_rope((x @ Wq_rope).reshape(b, s, H, RD), cos, sin)
            q_rope = q_rope.transpose(0, 2, 1, 3)
            c_kv = _rmsnorm(x @ Wkv_down, kv_norm_w)
            k = (c_kv @ Wk_up).reshape(b, s, H, HD).transpose(0, 2, 1, 3)
            v = (c_kv @ Wv_up).reshape(b, s, H, HD).transpose(0, 2, 1, 3)
            k_rope = _apply_rope((x @ Wk_rope).reshape(b, s, H, RD), cos, sin)
            k_rope = k_rope.transpose(0, 2, 1, 3)
            scale = (HD + RD) ** (-0.5)
            scores = (jnp.einsum('bhqd,bhkd->bhqk', q, k) + jnp.einsum('bhqd,bhkd->bhqk', q_rope, k_rope)) * scale
            attn = jax.nn.softmax(scores, axis=-1)
            out = jnp.einsum('bhqk,bhkd->bhqd', attn, v)
            out = out.transpose(0, 2, 1, 3).reshape(b, s, H * HD) @ Wout
            return (out, attn)
        return _reference_tuple_inner(x, Wq_down, q_norm_w, Wq_up, Wq_rope, Wkv_down, kv_norm_w, Wk_up, Wv_up, Wk_rope, Wout)[0]

    def _L1_ffn_ref(x, base_w, base_b, router_w, router_b, lora_A, lora_B):
        import jax, jax.numpy as jnp
        import numpy as np
        B, S, D_IN, D_OUT, E, R = (4, 256, 256, 256, 8, 16)
        SCALING = 32.0 / 16.0
        b, s, d_in = x.shape
        n = b * s
        e = lora_A.shape[0]
        d_out = lora_B.shape[-1]
        result = jnp.einsum('bsd,od->bso', x, base_w) + base_b
        logits = jnp.einsum('bsd,ed->bse', x, router_w) + router_b
        probs = jax.nn.softmax(logits.astype(jnp.float32), axis=-1)
        top_vals, top_idx = jax.lax.top_k(probs, 2)
        top_vals = top_vals / jnp.sum(top_vals, axis=-1, keepdims=True)
        top_vals = top_vals.astype(x.dtype)
        flat_idx = top_idx.reshape(n, 2)
        flat_val = top_vals.reshape(n, 2)
        gate = jnp.zeros((n, e), x.dtype).at[jnp.arange(n)[:, None], flat_idx].set(flat_val)
        xf = x.reshape(n, d_in)
        mid = jnp.einsum('nd,edr->ner', xf, lora_A)
        mid = mid * gate[:, :, None]
        lora_out = jnp.einsum('ner,erd->nd', mid, lora_B)
        return result + SCALING * lora_out.reshape(b, s, d_out)
    x = L0_attn_x
    x = x + 0.5 * _L0_ffn_ref(_layernorm(x, axis=-1), L0_ffn_router_w, L0_ffn_W1, L0_ffn_W2)
    x = x + _L0_attn_ref(_layernorm(x, axis=-1), L0_attn_Wq, L0_attn_Wk, L0_attn_Wv, L0_attn_Wo)
    x = x + 0.5 * _L0_ffn_ref(_layernorm(x, axis=-1), L0_ffn_router_w, L0_ffn_W1, L0_ffn_W2)
    x = x + 0.5 * _L1_ffn_ref(_layernorm(x, axis=-1), L1_ffn_base_w, L1_ffn_base_b, L1_ffn_router_w, L1_ffn_router_b, L1_ffn_lora_A, L1_ffn_lora_B)
    x = x + _L1_attn_ref(_layernorm(x, axis=-1), L1_attn_Wq_down, L1_attn_q_norm_w, L1_attn_Wq_up, L1_attn_Wq_rope, L1_attn_Wkv_down, L1_attn_kv_norm_w, L1_attn_Wk_up, L1_attn_Wv_up, L1_attn_Wk_rope, L1_attn_Wout)
    x = x + 0.5 * _L1_ffn_ref(_layernorm(x, axis=-1), L1_ffn_base_w, L1_ffn_base_b, L1_ffn_router_w, L1_ffn_router_b, L1_ffn_lora_A, L1_ffn_lora_B)
    return x

_drawn_inputs = setup_inputs


def setup_inputs(seed=0):
    import zlib

    import numpy as np

    out = dict(_drawn_inputs(seed))
    spreads = {'L1_attn_q_norm_w': (1.0, 0.6), 'L1_attn_kv_norm_w': (1.0, 0.6)}
    factors = {'L0_attn_Wq': 8.0,
     'L0_attn_Wk': 8.0,
     'L0_attn_Wv': 4.241,
     'L0_attn_Wo': 3.904,
     'L1_attn_Wq_down': 8.0,
     'L1_attn_Wq_up': 8.0,
     'L1_attn_Wq_rope': 8.0,
     'L1_attn_Wkv_down': 8.0,
     'L1_attn_Wk_up': 8.0,
     'L1_attn_Wv_up': 7.507,
     'L1_attn_Wk_rope': 8.0,
     'L1_attn_Wout': 6.836,
     'L1_ffn_base_b': 3.13,
     'L1_ffn_router_b': 8.0}
    for name, (base, spread) in spreads.items():
        noise = np.random.default_rng([zlib.crc32(name.encode()), seed]).standard_normal(out[name].shape)
        drawn = base * np.exp(spread * noise) if base else spread * noise
        out[name] = jnp.asarray(drawn.astype(out[name].dtype))
    for name, factor in factors.items():
        out[name] = (out[name] * factor).astype(out[name].dtype)
    return out
```

```python
from contextlib import ExitStack

import numpy as np

import concourse.bass as bass
from concourse import mybir

F32 = mybir.dt.float32
F32R = mybir.dt.float32r
I32 = mybir.dt.int32
U32 = mybir.dt.uint32
ALU = mybir.AluOpType
ACT = mybir.ActivationFunctionType
AX_X = mybir.AxisListType.X
AX_XY = mybir.AxisListType.XY

P = 128
BATCH, SEQ, D = 2, 1024, 256
NT = BATCH * SEQ // P
TB = SEQ // P
KD = D // P
LN_EPS = 1e-5

NE, FF, TOP = 16, 512, 2
KF = FF // P
NTILE = 48
assert NTILE >= NT * TOP + NE - 1 and NTILE % 2 == 0

H0, DH0 = 16, 16
HG = 4
NG0 = H0 // HG
VW = 32

H1, RD, HD1, DQL, DKVL = 16, 64, 128, 48, 64
NP1 = H1 // 2
MLA_SCALE = float(HD1 + RD) ** -0.5
RMS_EPS = 1e-6

LE, LR = 8, 16
LORA_SCALE = 2.0

MOE_STEPS = 54
LORA_STEPS = 14

C_ID, C_ONE, C_TRI, C_LOW, C_IOTA, C_TILE = 0, 128, 256, 384, 512, 528
C_EPS = C_TILE + NTILE
C_END = C_EPS + 2


class Sem:

    def __init__(self, handle, each, rep):
        self.handle, self.base = handle, each * rep

    def at(self, n):
        return self.base + n


def bcast(ap, axis, n):
    ap = ap.unsqueeze(axis)
    shape = list(ap.shape)
    shape[axis] = n
    return ap.to_broadcast(shape)


class Core:

    def __init__(self, nc, ctx):
        self.nc, self.ctx = nc, ctx
        self.handles = {}

    def sb(self, ctx, name, shape, dt=F32):
        return ctx.enter_context(self.nc.sbuf_tensor(name, shape, dt))

    def sem(self, name, each=0, rep=0):
        if name not in self.handles:
            self.handles[name] = self.ctx.enter_context(self.nc.semaphore(name))
        return Sem(self.handles[name], each, rep)


def norm_stats_dve(dve, g, s_stat, s_mv):
    with dve.Fori(0, NT) as t:
        dve.bn_stats(g.ST[:, t, :], g.X[:, t, :]).then_inc(s_stat.handle, 1)
    dve.wait_ge(s_stat.handle, s_stat.at(NT))
    for t in range(NT):
        dve.bn_aggr(g.MV[:, t, :], g.ST[:, t, :]).then_inc(s_mv.handle, 1)


def norm_sd_act(act, g, s_mv, s_sd):
    act.wait_ge(s_mv.handle, s_mv.at(NT))
    act.activation(g.SD[:, :], g.MV[:, :, 1], ACT.Sqrt, bias=g.C[:, C_EPS:C_EPS + 1]).then_inc(s_sd.handle, 1)


def norm_rs_dve(dve, g, s_sd, s_rs):
    dve.wait_ge(s_sd.handle, s_sd.at(1))
    dve.reciprocal(g.RS[:, :], g.SD[:, :]).then_inc(s_rs.handle, 1)
    dve.wait_ge(s_rs.handle, s_rs.at(1))


def normalize(dve, g, out, t):
    return dve.tensor_scalar(out, g.X[:, t, :], g.MV[:, t, 0:1], g.RS[:, bass.ds(t, 1)], ALU.subtract, ALU.mult)


def load_stage(nc, g, dram):
    s_in = g.sem("loaded_x")
    s_c = g.sem("loaded_constants")
    s_z = g.sem("zeros_made")
    s_zd = g.sem("slots_zeroed")
    with nc.Block() as block:
        @block.sync
        def _(sp):
            sp.dma_start(g.X[:, :, :], dram["x"].rearrange("(t p) d -> p t d", p=P)).then_inc(s_in.handle, 16)
            sp.dma_start(g.C[:, :], dram["const"]).then_inc(s_c.handle, 16)
            for e in range(0, NE, 4):
                sp.dma_start(g.W1[:, e:e + 4], dram["W1"][:, e:e + 4]).then_inc(g.s_w1.handle, 16)
            sp.wait_ge(s_in.handle, 16)
            sp.wait_ge(s_c.handle, 16)

        @block.vector
        def _(dve):
            dve.memset(g.XN[:, 0, :], 0.0).then_inc(s_z.handle, 1)

        @block.gpsimd
        def _(pool):
            pool.wait_ge(s_z.handle, 1)
            pool.dma_start(g.XG.rearrange("(n p) d -> p n d", p=P), bcast(g.XN[:, 0, :], 1, NTILE + 2)).then_inc(s_zd.handle, 16)
            pool.wait_ge(s_zd.handle, 16)


def moe_stage(nc, g, dram, rep):
    S = lambda name, each: g.sem("moe_" + name, each, rep)
    s_w2 = S("loaded_W2", 64)
    s_rw = S("loaded_router", 16)
    s_stat, s_mv, s_sd, s_rs = S("partial_stats", NT), S("stats", NT), S("deviations", 1), S("reciprocals", 1)
    s_xn, s_save, s_xtp, s_xtc = S("xn_tile", NT), S("xn_saved", NT), S("xnT_in_psum", NT), S("xnT_copied", NT)
    s_lgp, s_lgc = S("logits_in_psum", NT), S("logits_copied", NT)
    s_max, s_idx = S("top_values", NT), S("top_experts", NT)
    s_dve = S("routing_step", MOE_STEPS)
    s_gap, s_exp = S("gap", 1), S("gap_exp", 1)
    s_msk, s_cnt = S("mask", 1), S("counts_in_psum", 1)
    s_pos, s_ei = S("slots", 1), S("tile_experts", 1)
    s_sc = S("rows_scattered", 32 * NT)
    s_xs = [S(f"slots_loaded{u}", 16 * (NTILE // 2 + 1)) for u in range(2)]
    s_tap, s_tac = S("slotsT_in_psum", NTILE + 2), S("slotsT_copied", NTILE + 2)
    s_h, s_hs = S("hidden_in_psum", NTILE), S("hidden", NTILE)
    s_thp, s_thc = S("hiddenT_in_psum", NTILE), S("hiddenT_copied", NTILE)
    s_y, s_yc = S("expert_out_in_psum", NTILE), S("expert_out_copied", NTILE)
    s_yd = S("expert_out_stored", 16 * NTILE)
    NQ = 4
    s_ga = [S(f"rows_gathered{q}", 32 * NT // NQ) for q in range(NQ)]
    s_add = S("first_added", NT)

    with ExitStack() as ctx:
        sb = lambda name, shape, dt=F32: g.sb(ctx, f"moe{rep}_{name}", shape, dt)
        W2 = sb("W2", [P, NE, KF, D])
        RW = sb("RW", [P, KD, NE])
        XNS = sb("XNS", [P, 2, D])
        XT = sb("XT", [P, 2, KD, P])
        LG = sb("LG", [P, NT, NE])
        M8 = sb("M8", [P, NT, 8])
        I8 = sb("I8", [P, NT, 8], U32)
        IF = sb("IF", [P, NT, 8])
        OH = sb("OH", [P, 2, NT, NE])
        MK = sb("MK", [P, NT, NE])
        EXC = sb("EXC", [P, NT + 1, NE])
        NI = sb("NI", [P, NE], I32)
        NI2 = sb("NI2", [P, NE], I32)
        TE = sb("TE", [P, NE])
        TI = sb("TI", [P, NE + 1])
        BS = sb("BS", [P, NE])
        PB = sb("PB", [P, NT, NE])
        PT = sb("PT", [P, 2, NT, NE])
        PF = sb("PF", [P, 2, NT])
        PI = sb("PI", [P, 2, NT], I32)
        CM = sb("CM", [1, NTILE, NE])
        EF = sb("EF", [1, NTILE])
        EC = sb("EC", [1, NTILE])
        EI = sb("EI", [1, NTILE], I32)
        GP = sb("GP", [P, NT])
        GE = sb("GE", [P, NT])
        GS = sb("GS", [P, NT])
        GH = sb("GH", [P, 2, NT])
        GR = sb("GR", [P, NT])
        XS = sb("XS", [P, 2, D])
        ST = sb("ST", [P, 2, KD, P])
        HS = sb("HS", [P, 2, FF])
        HT = sb("HT", [P, 2, KF, P])
        YS = sb("YS", [P, 2, D])
        Y2 = sb("Y2", [P, 8, D])
        bank = g.bank

        with nc.Block() as block:
            @block.sync
            def _(sp):
                sp.dma_start(RW[:, :, :], dram["router_w"]).then_inc(s_rw.handle, 16)
                for e in range(0, NE, 4):
                    sp.dma_start(W2[:, e:e + 4], dram["W2"][:, e:e + 4]).then_inc(s_w2.handle, 16)
                sp.wait_ge(s_sc.handle, s_sc.at(32 * NT))
                for u in range(2):
                    sp.dma_start(XS[:, u, :], g.XG[u * P:(u + 1) * P, :]).then_inc(s_xs[u].handle, 16)
                with sp.Fori(0, NTILE // 2) as i:
                    for u in range(2):
                        sp.wait_ge(s_tap.handle, s_tap.at(2 * i + u + 1))
                        sp.dma_start(XS[:, u, :], g.XG[bass.ds((2 * i + u + 2) * P, P), :]).then_inc(s_xs[u].handle, 16)

            @block.vector
            def _(dve):
                norm_stats_dve(dve, g, s_stat, s_mv)
                norm_rs_dve(dve, g, s_sd, s_rs)
                with dve.Fori(0, NT // 2) as i:
                    for u in range(2):
                        dve.wait_ge(s_xtp.handle, s_xtp.at(2 * i))
                        dve.wait_ge(s_save.handle, s_save.at(2 * i))
                        normalize(dve, g, XNS[:, u, :], 2 * i + u).then_inc(s_xn.handle, 1)

                for t in range(NT):
                    dve.wait_ge(s_lgc.handle, s_lgc.at(t + 1))
                    dve.max(M8[:, t, :], LG[:, t, :]).then_inc(s_max.handle, 1)
                for t in range(NT):
                    dve.wait_ge(s_max.handle, s_max.at(t + 1))
                    dve.max_index(I8[:, t, :], M8[:, t, :], LG[:, t, :]).then_inc(s_idx.handle, 1)
                dve.tensor_tensor(GP[:, :], M8[:, :, 1], M8[:, :, 0], ALU.subtract).then_inc(s_gap.handle, 1)
                dve.wait_ge(s_idx.handle, s_idx.at(NT))
                n = [0]

                def then_wait(ins):
                    n[0] += 1
                    ins.then_inc(s_dve.handle, 1)
                    dve.wait_ge(s_dve.handle, s_dve.at(n[0]))

                then_wait(dve.tensor_copy(IF[:, :, :], I8[:, :, :]))
                iota = bcast(g.C[:, C_IOTA:C_IOTA + NE], 1, NT)
                for k in range(2):
                    ins = dve.tensor_tensor(OH[:, k], iota, bcast(IF[:, :, k], 2, NE), ALU.is_equal)
                    then_wait(ins)
                dve.tensor_tensor(MK[:, :, :], OH[:, 0], OH[:, 1], ALU.add).then_inc(s_msk.handle, 1)
                then_wait(dve.memset(EXC[:, 0, :], 0.0))
                dve.wait_ge(s_cnt.handle, s_cnt.at(1))
                with dve.Fori(0, NT) as t:
                    dve.wait_ge(s_dve.handle, s_dve.at(n[0] + t))
                    dve.tensor_tensor(EXC[:, t + 1, :], bank(5)[:, bass.ds(t * NE, NE)], EXC[:, t, :],
                                      ALU.add).then_inc(s_dve.handle, 1)
                n[0] += NT
                dve.wait_ge(s_dve.handle, s_dve.at(n[0]))
                then_wait(dve.tensor_scalar(NI[:, :], EXC[:, NT, :], float(P - 1), None, ALU.add))
                then_wait(dve.tensor_scalar(NI2[:, :], NI[:, :], 7, None, ALU.arith_shift_right))
                then_wait(dve.tensor_copy(TE[:, :], NI2[:, :]))
                then_wait(dve.memset(TI[:, 0:1], 0.0))
                with dve.Fori(0, NE) as e:
                    dve.wait_ge(s_dve.handle, s_dve.at(n[0] + e))
                    dve.tensor_tensor(TI[:, bass.ds(e + 1, 1)], TI[:, bass.ds(e, 1)], TE[:, bass.ds(e, 1)],
                                      ALU.add).then_inc(s_dve.handle, 1)
                n[0] += NE
                dve.wait_ge(s_dve.handle, s_dve.at(n[0]))
                then_wait(dve.tensor_scalar(BS[:, :], TI[:, 0:NE], float(P), None, ALU.mult))
                then_wait(dve.tensor_tensor(PB[:, :, :], EXC[:, 0:NT, :], bcast(BS[:, :], 1, NT), ALU.add))
                then_wait(dve.tensor_tensor(MK[:, :, :], bank(4)[:, 0:NT * NE].rearrange("p (t e) -> p t e", e=NE),
                                            PB[:, :, :], ALU.add))
                for k in range(2):
                    then_wait(dve.tensor_tensor(PT[:, k], OH[:, k], MK[:, :, :], ALU.mult))
                    then_wait(dve.tensor_reduce(PF[:, k, :], PT[:, k], AX_X, ALU.add))
                dve.tensor_copy(PI[:, :, :], PF[:, :, :]).then_inc(s_pos.handle, 1)
                then_wait(dve.tensor_tensor(CM[:, :, :], bcast(TI[0:1, 1:NE + 1], 1, NTILE),
                                            bcast(g.C[0:1, C_TILE:C_TILE + NTILE], 2, NE), ALU.is_le))
                then_wait(dve.tensor_reduce(EF[:, :], CM[:, :, :], AX_X, ALU.add))
                then_wait(dve.tensor_scalar(EC[:, :], EF[:, :], float(NE - 1), None, ALU.min))
                dve.tensor_copy(EI[:, :], EC[:, :]).then_inc(s_ei.handle, 1)
                dve.wait_ge(s_exp.handle, s_exp.at(1))
                then_wait(dve.tensor_scalar(GS[:, :], GE[:, :], 1.0, None, ALU.add))
                then_wait(dve.reciprocal(GR[:, :], GS[:, :]))
                then_wait(dve.tensor_scalar(GH[:, 0, :], GR[:, :], 0.5, None, ALU.mult))
                then_wait(dve.tensor_tensor(GH[:, 1, :], GH[:, 0, :], GE[:, :], ALU.mult))
                assert n[0] == MOE_STEPS

                for u in range(2):
                    dve.wait_ge(s_tap.handle, s_tap.at(u + 1))
                    dve.tensor_copy(ST[:, u], bank(u)[:, 0:KD * P].rearrange("p (k s) -> p k s", s=P)).then_inc(s_tac.handle, 1)
                with dve.Fori(0, NTILE // 2) as i:
                    for u in range(2):
                        dve.wait_ge(s_thp.handle, s_thp.at(2 * i + u + 1))
                        dve.wait_ge(s_y.handle, s_y.at(2 * i))
                        dve.tensor_copy(HT[:, u], bank(4 + u)[:, :].rearrange("p (k s) -> p k s", s=P)).then_inc(s_thc.handle, 1)
                    for u in range(2):
                        dve.wait_ge(s_tap.handle, s_tap.at(2 * i + u + 3))
                        dve.wait_ge(s_h.handle, s_h.at(2 * i + u + 1))
                        dve.tensor_copy(ST[:, u], bank(u)[:, 0:KD * P].rearrange("p (k s) -> p k s", s=P)).then_inc(s_tac.handle, 1)
                per = NT // NQ
                for q in range(NQ):
                    dve.wait_ge(s_ga[q].handle, s_ga[q].at(32 * per))
                    with dve.Fori(q * per, (q + 1) * per) as t:
                        dve.scalar_tensor_tensor(g.X[:, t, :], g.XN[:, t, :], GH[:, 0, bass.ds(t, 1)], g.X[:, t, :],
                                                 ALU.mult, ALU.add).then_inc(s_add.handle, 1)
                    with dve.Fori(q * per, (q + 1) * per) as t:
                        dve.wait_ge(s_add.handle, s_add.at(t + 1))
                        ins = dve.scalar_tensor_tensor(g.X[:, t, :], Y2[:, t - (q // 2) * 2 * per, :], GH[:, 1, bass.ds(t, 1)],
                                                       g.X[:, t, :], ALU.mult, ALU.add)
                        ins.then_inc(g.s_second[rep].handle, 1)

            @block.scalar
            def _(act):
                norm_sd_act(act, g, s_mv, s_sd)
                with act.Fori(0, NT // 2) as i:
                    for u in range(2):
                        act.wait_ge(s_xn.handle, s_xn.at(2 * i + u + 1))
                        act.copy(g.XN[:, 2 * i + u, :], XNS[:, u, :]).then_inc(s_save.handle, 1)
                        act.wait_ge(s_xtp.handle, s_xtp.at(2 * i + u + 1))
                        act.wait_ge(s_lgp.handle, s_lgp.at(2 * i))
                        act.copy(XT[:, u], bank(u)[:, 0:KD * P].rearrange("p (k s) -> p k s", s=P)).then_inc(s_xtc.handle, 1)
                    for u in range(2):
                        act.wait_ge(s_lgp.handle, s_lgp.at(2 * i + u + 1))
                        act.copy(LG[:, 2 * i + u, :], bank(2 + u)[:, 0:NE]).then_inc(s_lgc.handle, 1)
                act.wait_ge(s_gap.handle, s_gap.at(1))
                act.activation(GE[:, :], GP[:, :], ACT.Exp).then_inc(s_exp.handle, 1)
                with act.Fori(0, NTILE // 2) as i:
                    for u in range(2):
                        act.wait_ge(s_h.handle, s_h.at(2 * i + u + 1))
                        act.wait_ge(s_thp.handle, s_thp.at(2 * i))
                        act.activation(HS[:, u, :], bank(2 + u)[:, :], ACT.Silu).then_inc(s_hs.handle, 1)
                    for u in range(2):
                        act.wait_ge(s_y.handle, s_y.at(2 * i + u + 1))
                        act.wait_ge(s_yd.handle, s_yd.at(32 * i))
                        act.copy(YS[:, u, :], bank(6 + u)[:, 0:D]).then_inc(s_yc.handle, 1)

            @block.tensor
            def _(pe):
                ident = g.C[:, C_ID:C_ID + P]
                pe.wait_ge(s_rw.handle, s_rw.at(16))
                with pe.Fori(0, NT // 2) as i:
                    for u in range(2):
                        pe.wait_ge(s_xn.handle, s_xn.at(2 * i + u + 1))
                        pe.wait_ge(s_xtc.handle, s_xtc.at(2 * i))
                        for k in range(KD):
                            ins = pe.transpose(bank(u)[:, k * P:(k + 1) * P], XNS[:, u, k * P:(k + 1) * P], ident)
                        ins.then_inc(s_xtp.handle, 1)
                    for u in range(2):
                        pe.wait_ge(s_xtc.handle, s_xtc.at(2 * i + u + 1))
                        pe.wait_ge(s_lgc.handle, s_lgc.at(2 * i))
                        for k in range(KD):
                            ins = pe.matmul(bank(2 + u)[:, 0:NE], XT[:, u, k, :], RW[:, k, :], start=(k == 0), stop=(k == KD - 1))
                        ins.then_inc(s_lgp.handle, 1)
                pe.wait_ge(s_msk.handle, s_msk.at(1))
                mask = MK[:, :, :].rearrange("p t e -> p (t e)")
                pe.matmul(bank(4)[:, 0:NT * NE], g.C[:, C_TRI:C_TRI + P], mask, start=True, stop=True)
                pe.matmul(bank(5)[:, 0:NT * NE], g.C[:, C_ONE:C_ONE + P], mask, start=True, stop=True).then_inc(s_cnt.handle, 1)

                pe.wait_ge(g.s_w1.handle, 64)
                pe.wait_ge(s_w2.handle, s_w2.at(64))
                pe.wait_ge(s_ei.handle, s_ei.at(1))

                def slots_t(u, j, loads):
                    pe.wait_ge(s_xs[u].handle, s_xs[u].at(16 * loads))
                    for k in range(KD):
                        ins = pe.transpose(bank(u)[:, k * P:(k + 1) * P], XS[:, u, k * P:(k + 1) * P], ident)
                    ins.then_inc(s_tap.handle, 1)

                slots_t(0, 0, 1)
                slots_t(1, 1, 1)
                with pe.Fori(0, NTILE // 2) as i:
                    experts = [pe.value_load(EI[0:1, bass.ds(2 * i + u, 1)], min_val=0, max_val=NE - 1) for u in range(2)]
                    for u in range(2):
                        pe.wait_ge(s_tac.handle, s_tac.at(2 * i + u + 1))
                        pe.wait_ge(s_hs.handle, s_hs.at(2 * i))
                        for k in range(KD):
                            ins = pe.matmul(bank(2 + u)[:, :], ST[:, u, k, :], g.W1[:, experts[u], k, :], start=(k == 0), stop=(k == KD - 1))
                        ins.then_inc(s_h.handle, 1)
                    for u in range(2):
                        pe.wait_ge(s_hs.handle, s_hs.at(2 * i + u + 1))
                        pe.wait_ge(s_thc.handle, s_thc.at(2 * i))
                        for k in range(KF):
                            ins = pe.transpose(bank(4 + u)[:, k * P:(k + 1) * P], HS[:, u, k * P:(k + 1) * P], ident)
                        ins.then_inc(s_thp.handle, 1)
                    for u in range(2):
                        slots_t(u, 2 * i + u + 2, i + 2)
                    for u in range(2):
                        pe.wait_ge(s_thc.handle, s_thc.at(2 * i + u + 1))
                        pe.wait_ge(s_yc.handle, s_yc.at(2 * i))
                        for k in range(KF):
                            ins = pe.matmul(bank(6 + u)[:, 0:D], HT[:, u, k, :], W2[:, experts[u], k, :], start=(k == 0), stop=(k == KF - 1))
                        ins.then_inc(s_y.handle, 1)

            @block.gpsimd
            def _(pool):
                pool.wait_ge(s_pos.handle, s_pos.at(1))
                pool.wait_ge(s_save.handle, s_save.at(NT))
                for t in range(NT):
                    for k in range(2):
                        pool.indirect_dma_start(g.XG, bass.IndirectOffsetOnAxis(PI[:, k, t:t + 1], 0),
                                                g.XN[:, t, :], None).then_inc(s_sc.handle, 16)
                with pool.Fori(0, NTILE // 2) as i:
                    for u in range(2):
                        pool.wait_ge(s_yc.handle, s_yc.at(2 * i + u + 1))
                        pool.dma_start(g.YG[bass.ds((2 * i + u) * P, P), :], YS[:, u, :]).then_inc(s_yd.handle, 16)
                pool.wait_ge(s_yd.handle, s_yd.at(16 * NTILE))
                per = NT // NQ
                for t in range(NT):
                    if t >= NT // 2:
                        pool.wait_ge(g.s_second[rep].handle, t - NT // 2 + 1)
                    q = t // per
                    pool.indirect_dma_start(g.XN[:, t, :], None, g.YG, bass.IndirectOffsetOnAxis(PI[:, 0, t:t + 1], 0)).then_inc(s_ga[q].handle, 16)
                    pool.indirect_dma_start(Y2[:, t % 8, :], None, g.YG, bass.IndirectOffsetOnAxis(PI[:, 1, t:t + 1], 0)).then_inc(s_ga[q].handle, 16)


def attention_stage(nc, g, dram):
    S = lambda name: g.sem("att_" + name).handle
    s_w, s_fill = S("weights"), S("filled")
    s_stat, s_mv, s_sd, s_rs = (g.sem("att_" + n) for n in ("partial_stats", "stats", "deviations", "reciprocals"))
    s_xn, s_xtp, s_xtc = S("xn_tile"), S("xnT_in_psum"), S("xnT_copied")
    s_pr, s_hi, s_rows = S("qkv_in_psum"), S("high_parts"), S("low_parts")
    s_qkp, s_qc, s_kc = S("qkT_in_psum"), S("qT_copied"), S("kT_copied")
    s_cs, s_suf = S("tile_sums_in_psum"), S("later_sums")
    s_sc, s_mask, s_mx, s_nb = S("scores"), S("masked"), S("row_max"), S("negative_max")
    s_p, s_e0 = S("probs"), S("later_weight")
    s_ptp, s_ptc = S("probsT_in_psum"), S("probsT_copied")
    s_ot, s_otc, s_bt = S("outT_in_psum"), S("outT_copied"), S("out_in_psum")
    s_f = [S(n) for n in ("later_part", "out_sum", "out_denominator", "out_rows")]
    s_aop, s_aoc, s_wo, s_x = S("outrowsT_in_psum"), S("outrowsT_copied"), S("projected"), S("x_updated")

    NU = TB * HG
    chunks = []
    for n in range(NU):
        nk = n // HG + 1
        chunks += [(n, c, min(4, nk - c)) for c in range(0, nk, 4)]
    NC = len(chunks)
    first_chunk = [next(c for c, ch in enumerate(chunks) if ch[0] == n) for n in range(NU)] + [NC]

    with ExitStack() as ctx:
        sb = lambda name, shape, dt=F32: g.sb(ctx, "att_" + name, shape, dt)
        WQ = sb("Wqkv", [P, KD, NG0 * 3 * HG * DH0])
        WO = sb("Wo", [P, KD, D])
        XNS = sb("XNS", [P, 2, D])
        XT = sb("XT", [P, KD, SEQ])
        QS = sb("QS", [P, 2, HG * 64])
        KS = sb("KS", [P, 2, HG * 64])
        QT = sb("QT", [P, 2, 2, SEQ], F32R)
        KT = sb("KT", [P, 2, SEQ], F32R)
        VV = sb("VV", [P, TB, HG * VW])
        SF = sb("SF", [P, TB, HG * VW])
        PR = sb("PR", [P, 2, SEQ])
        PT = sb("PT", [P, 2, HG, TB, P])
        MX = sb("MX", [P, NU])
        NB = sb("NB", [P, NU])
        E0 = sb("E0", [P, 2, HG])
        OT = sb("OT", [P, P])
        F1 = sb("F1", [P, HG * VW])
        F2 = sb("F2", [P, HG * VW])
        F3 = sb("F3", [P, HG])
        AO = sb("AO", [P, TB, D])
        AT = sb("AT", [P, 2, KD, P])
        bank, banks = g.bank, g.banks
        ident = g.C[:, C_ID:C_ID + P]
        sc_bank = lambda n: 2 * (n % 2)
        scores = lambda n, w: banks(sc_bank(n), 2)[:, 0:w]
        slots = lambda rows, j: rows[:, j % 2, :].rearrange("p (h s d) -> p h s d", h=HG, s=4)
        part = lambda j, m: bank(j % 2)[:, m * 64:(m + 1) * 64].rearrange("p (h d) -> p h d", h=HG)
        v4 = lambda ap: ap.rearrange("p (h d) -> p h d", h=HG)

        with nc.Block() as block:
            @block.sync
            def _(sp):
                sp.dma_start(WQ[:, :, :], dram["Wqkv"]).then_inc(s_w, 16)
                sp.dma_start(WO[:, :, :], dram["Wo"]).then_inc(s_w, 16)
                sp.wait_ge(s_w, 32)

            @block.gpsimd
            def _(pool):
                pool.memset(QT[:, :, :, :].bitcast(F32), 0.0).then_inc(s_fill, 1)
                pool.memset(VV[:, :, :], 0.0).then_inc(s_fill, 1)
                pool.wait_ge(s_fill, 2)
                pool.memset(VV[:, :, :].rearrange("p j (h d) -> p (j h) d", d=VW)[:, :, DH0:DH0 + 1], 1.0).then_inc(s_fill, 1)

            @block.tensor
            def _(pe):
                pe.wait_ge(s_w, 32)
                pe.wait_ge(s_fill, 3)
                with pe.Fori(0, BATCH) as b:
                    for j in range(TB):
                        pe.wait_ge(s_xn, TB * b + j + 1)
                        if j >= 2:
                            pe.wait_ge(s_xtc, TB * b + j - 1)
                        for k in range(KD):
                            ins = pe.transpose(bank(j % 2)[:, k * P:(k + 1) * P], XNS[:, j % 2, k * P:(k + 1) * P], ident)
                        ins.then_inc(s_xtp, 1)
                    with pe.Fori(0, NG0) as gg:
                        it = b * NG0 + gg
                        pe.wait_ge(s_xtc, TB * b + TB)

                        def qk_transposes(j):
                            pe.wait_ge(s_rows, 2 * (TB * it + j + 1))
                            if j >= 2:
                                pe.wait_ge(s_qc, 2 * (TB * it + j - 1))
                                pe.wait_ge(s_kc, TB * it + j - 1)
                            for r in range(2):
                                pe.transpose(bank(2 + j % 2)[:, r * P:(r + 1) * P], QS[:, j % 2, r * P:(r + 1) * P], ident)
                            for r in range(2):
                                ins = pe.transpose(bank(4 + j % 2)[:, r * P:(r + 1) * P], KS[:, j % 2, r * P:(r + 1) * P], ident)
                            ins.then_inc(s_qkp, 1)

                        for j in range(TB):
                            if j >= 2:
                                pe.wait_ge(s_rows, 2 * (TB * it + j - 1))
                            for k in range(KD):
                                ins = pe.matmul(bank(j % 2)[:, 0:3 * HG * DH0], XT[:, k, j * P:(j + 1) * P],
                                                WQ[:, k, bass.ds(gg * (3 * HG * DH0), 3 * HG * DH0)], start=(k == 0), stop=(k == KD - 1))
                            ins.then_inc(s_pr, 1)
                            if j:
                                qk_transposes(j - 1)
                        qk_transposes(TB - 1)
                        for m in range(2):
                            ins = pe.matmul(bank(6 + m)[:, :], g.C[:, C_ONE:C_ONE + P],
                                            VV[:, 4 * m:4 * m + 4, :].rearrange("p j c -> p (j c)"), start=True, stop=True)
                        ins.then_inc(s_cs, 1)
                        pe.wait_ge(s_qc, 2 * TB * (it + 1))
                        pe.wait_ge(s_kc, TB * (it + 1))

                        def scores_of(n):
                            i, h = n // HG, n % HG
                            if n >= 2:
                                pe.wait_ge(s_p, NU * it + n - 1)
                            width = (i // 2 + 1) * 2 * P
                            for c in range(0, width, 512):
                                w = min(512, width - c)
                                ins = pe.matmul(bank(sc_bank(n) + c // 512)[:, 0:w], QT[:, h // 2, h % 2, i * P:(i + 1) * P],
                                                KT[:, h // 2, c:c + w], start=True, stop=True)
                            ins.then_inc(s_sc, 1)

                        def transposes_of(n):
                            pe.wait_ge(s_p, NU * it + n + 1)
                            for c in range(first_chunk[n], first_chunk[n + 1]):
                                _, k0, nk = chunks[c]
                                if c >= 2:
                                    pe.wait_ge(s_ptc, NC * it + c - 1)
                                for k in range(nk):
                                    ins = pe.transpose(bank(4 + c % 2)[:, k * P:(k + 1) * P], PR[:, n % 2, (k0 + k) * P:(k0 + k + 1) * P], ident)
                                ins.then_inc(s_ptp, 1)

                        def values_of(i):
                            pe.wait_ge(s_ptc, NC * it + first_chunk[HG * (i + 1)])
                            if i:
                                pe.wait_ge(s_otc, TB * it + i)
                            else:
                                pe.wait_ge(s_suf, TB * (it + 1))
                            for k in range(i + 1):
                                for h in range(HG):
                                    ins = pe.matmul(bank(6)[h * VW:(h + 1) * VW, 0:P], VV[:, k, h * VW:(h + 1) * VW],
                                                    PT[:, i % 2, h, k, :], start=(k == 0), stop=(k == i))
                            ins.then_inc(s_ot, 1)

                        def out_rows_of(i):
                            pe.wait_ge(s_otc, TB * it + i + 1)
                            if i:
                                pe.wait_ge(s_f[1], TB * it + i)
                            pe.transpose(bank(7)[:, 0:P], OT[:, :], ident).then_inc(s_bt, 1)

                        scores_of(0)
                        for n in range(NU):
                            if n + 1 < NU:
                                scores_of(n + 1)
                            transposes_of(n)
                            if n >= HG and n % HG == 0:
                                values_of(n // HG - 1)
                            if n >= HG and n % HG == 3:
                                out_rows_of(n // HG - 1)
                        values_of(TB - 1)
                        out_rows_of(TB - 1)
                    for i in range(TB):
                        pe.wait_ge(s_f[3], TB * NG0 * (b + 1))
                        if i >= 2:
                            pe.wait_ge(s_aoc, TB * b + i - 1)
                        for k in range(KD):
                            ins = pe.transpose(bank(4 + i % 2)[:, k * P:(k + 1) * P], AO[:, i, k * P:(k + 1) * P], ident)
                        ins.then_inc(s_aop, 1)
                        pe.wait_ge(s_aoc, TB * b + i + 1)
                        if i >= 2:
                            pe.wait_ge(s_x, TB * b + i - 1)
                        for k in range(KD):
                            ins = pe.matmul(bank(i % 2)[:, 0:D], AT[:, i % 2, k, :], WO[:, k, :], start=(k == 0), stop=(k == KD - 1))
                        ins.then_inc(s_wo, 1)
                    pe.wait_ge(s_x, TB * (b + 1))

            @block.scalar
            def _(act):
                norm_sd_act(act, g, s_mv, s_sd)
                act.wait_ge(s_fill, 3)
                with act.Fori(0, BATCH) as b:
                    for j in range(TB):
                        act.wait_ge(s_xtp, TB * b + j + 1)
                        act.copy(XT[:, :, j * P:(j + 1) * P], bank(j % 2)[:, 0:KD * P].rearrange("p (k s) -> p k s", s=P)).then_inc(s_xtc, 1)
                    with act.Fori(0, NG0) as gg:
                        it = b * NG0 + gg

                        def q_copies(j):
                            act.wait_ge(s_qkp, TB * it + j + 1)
                            for m in range(2):
                                act.copy(QT[m * 64:(m + 1) * 64, :, m, j * P:(j + 1) * P],
                                         bank(2 + j % 2)[m * 64:(m + 1) * 64, 0:2 * P].rearrange("p (r s) -> p r s", r=2)).then_inc(s_qc, 1)

                        for j in range(TB):
                            act.wait_ge(s_pr, TB * it + j + 1)
                            if j >= 2:
                                act.wait_ge(s_qkp, TB * it + j - 1)
                            act.copy(slots(QS, j)[:, :, 0:4:2, :].bitcast(F32R), bcast(part(j, 0), 2, 2)).then_inc(s_hi, 1)
                            act.copy(slots(KS, j)[:, :, 0:2, :].bitcast(F32R), bcast(part(j, 1), 2, 2)).then_inc(s_hi, 1)
                            if j == 0:
                                act.wait_ge(s_bt, TB * it)
                            act.copy(v4(VV[:, j, :])[:, :, 0:DH0], part(j, 2)).then_inc(s_hi, 1)
                            if j:
                                q_copies(j - 1)
                        q_copies(TB - 1)

                        def copies_of(n):
                            for c in range(first_chunk[n], first_chunk[n + 1]):
                                _, k0, nk = chunks[c]
                                i, h = n // HG, n % HG
                                act.wait_ge(s_ptp, NC * it + c + 1)
                                if i >= 2 and n % HG == 0 and k0 == 0:
                                    act.wait_ge(s_ot, TB * it + i - 1)
                                act.copy(PT[:, i % 2, h, k0:k0 + nk, :], bank(4 + c % 2)[:, 0:nk * P].rearrange("p (k s) -> p k s", s=P)).then_inc(s_ptc, 1)

                        for n in range(NU):
                            i, w = n // HG, (n // HG + 1) * P
                            act.wait_ge(s_nb, NU * it + n + 1)
                            if n >= 2:
                                act.wait_ge(s_ptp, NC * it + first_chunk[n - 1])
                            act.activation(PR[:, n % 2, 0:w], scores(n, w), ACT.Exp, bias=NB[:, n:n + 1], scale=SEQ ** -0.5).then_inc(s_p, 1)
                            if n % HG == 3:
                                if i >= 2:
                                    act.wait_ge(s_f[0], (TB - 1) * it + i - 1)
                                act.activation(E0[:, i % 2, :], NB[:, HG * i:HG * i + HG], ACT.Exp).then_inc(s_e0, 1)
                            if n:
                                copies_of(n - 1)
                        copies_of(NU - 1)
                    for i in range(TB):
                        act.wait_ge(s_aop, TB * b + i + 1)
                        if i >= 2:
                            act.wait_ge(s_wo, TB * b + i - 1)
                        act.copy(AT[:, i % 2], bank(4 + i % 2)[:, 0:KD * P].rearrange("p (k s) -> p k s", s=P)).then_inc(s_aoc, 1)

            @block.vector
            def _(dve):
                norm_stats_dve(dve, g, s_stat, s_mv)
                norm_rs_dve(dve, g, s_sd, s_rs)
                with dve.Fori(0, BATCH) as b:
                    for j in range(TB):
                        if j >= 2:
                            dve.wait_ge(s_xtp, TB * b + j - 1)
                        normalize(dve, g, XNS[:, j % 2, :], b * TB + j).then_inc(s_xn, 1)
                    with dve.Fori(0, NG0) as gg:
                        it = b * NG0 + gg

                        def k_copy(j):
                            dve.wait_ge(s_qkp, TB * it + j + 1)
                            dve.tensor_copy(KT[:, :, j * P:(j + 1) * P], bank(4 + j % 2)[:, 0:2 * P].rearrange("p (r s) -> p r s", r=2)).then_inc(s_kc, 1)

                        for j in range(TB):
                            dve.wait_ge(s_hi, 3 * (TB * it + j + 1))
                            qs, ks = slots(QS, j), slots(KS, j)
                            dve.tensor_tensor(qs[:, :, 1:4:2, :], bcast(part(j, 0), 2, 2), qs[:, :, 0:4:2, :], ALU.subtract).then_inc(s_rows, 1)
                            dve.tensor_tensor(ks[:, :, 2:4, :], bcast(part(j, 1), 2, 2), ks[:, :, 0:2, :], ALU.subtract).then_inc(s_rows, 1)
                            if j:
                                k_copy(j - 1)
                        k_copy(TB - 1)
                        dve.wait_ge(s_cs, it + 1)
                        dve.wait_ge(s_f[0], (TB - 1) * it)
                        dve.memset(SF[:, TB - 1, :], 0.0).then_inc(s_suf, 1)
                        for i in range(TB - 2, -1, -1):
                            dve.wait_ge(s_suf, TB * it + TB - 1 - i)
                            dve.tensor_tensor(SF[:, i, :], bank(6 + (i + 1) // 4)[:, (i + 1) % 4 * P:((i + 1) % 4 + 1) * P], SF[:, i + 1, :],
                                              ALU.add).then_inc(s_suf, 1)
                        dve.wait_ge(s_suf, TB * (it + 1))

                        def finish(i):
                            dve.wait_ge(s_bt, TB * it + i + 1)
                            if i < TB - 1:
                                dve.wait_ge(s_e0, TB * it + i + 1)
                                dve.tensor_tensor(v4(F1[:, :]), v4(SF[:, i, :]), bcast(E0[:, i % 2, :], 2, VW), ALU.mult).then_inc(s_f[0], 1)
                                dve.wait_ge(s_f[0], (TB - 1) * it + i + 1)
                                dve.tensor_tensor(F2[:, :], bank(7)[:, 0:P], F1[:, :], ALU.add).then_inc(s_f[1], 1)
                            else:
                                dve.tensor_copy(F2[:, :], bank(7)[:, 0:P]).then_inc(s_f[1], 1)
                            dve.wait_ge(s_f[1], TB * it + i + 1)
                            dve.reciprocal(F3[:, :], v4(F2[:, :])[:, :, DH0]).then_inc(s_f[2], 1)
                            dve.wait_ge(s_f[2], TB * it + i + 1)
                            out = AO[:, i, bass.ds(gg * (HG * DH0), HG * DH0)]
                            dve.tensor_tensor(v4(out), v4(F2[:, :])[:, :, 0:DH0], bcast(F3[:, :], 2, DH0), ALU.mult).then_inc(s_f[3], 1)

                        def out_copy(i):
                            dve.wait_ge(s_ot, TB * it + i + 1)
                            if i:
                                dve.wait_ge(s_bt, TB * it + i)
                            dve.tensor_copy(OT[:, :], bank(6)[:, 0:P]).then_inc(s_otc, 1)

                        for n in range(NU):
                            i, h = n // HG, n % HG
                            w = (i + 1) * P
                            dve.wait_ge(s_sc, NU * it + n + 1)
                            diag = scores(n, w)[:, i * P:w]
                            dve.tensor_tensor(diag, diag, g.C[:, C_LOW:C_LOW + P], ALU.mult).then_inc(s_mask, 1)
                            dve.wait_ge(s_mask, NU * it + n + 1)
                            dve.tensor_reduce(MX[:, n:n + 1], scores(n, w), AX_X, ALU.max).then_inc(s_mx, 1)
                            dve.wait_ge(s_mx, NU * it + n + 1)
                            if i < TB - 1:
                                ins = dve.tensor_scalar(NB[:, n:n + 1], MX[:, n:n + 1], 0.0, -(SEQ ** -0.5), ALU.max, ALU.mult)
                            else:
                                ins = dve.tensor_scalar(NB[:, n:n + 1], MX[:, n:n + 1], -(SEQ ** -0.5), None, ALU.mult)
                            ins.then_inc(s_nb, 1)
                            if n >= HG and n % HG == 2:
                                out_copy(n // HG - 1)
                            if n >= 2 * HG and n % HG == 0:
                                finish(n // HG - 2)
                        finish(TB - 2)
                        out_copy(TB - 1)
                        finish(TB - 1)
                    for i in range(TB):
                        dve.wait_ge(s_wo, TB * b + i + 1)
                        xt = g.X[:, b * TB + i, :]
                        dve.tensor_tensor(xt, bank(i % 2)[:, 0:D], xt, ALU.add).then_inc(s_x, 1)


def lora_stage(nc, g, dram, rep):
    S = lambda name, each: g.sem("lora_" + name, each, rep)
    s_w = S("weights", 64)
    s_stat, s_mv, s_sd, s_rs = S("partial_stats", NT), S("stats", NT), S("deviations", 1), S("reciprocals", 1)
    s_xn, s_xtp, s_xtc = S("xn_tile", NT), S("xnT_in_psum", NT), S("xnT_copied", NT)
    s_pr, s_mid, s_lg, s_b1, s_b2 = S("projected", NT), S("mids_copied", NT), S("logits", NT), S("biased", NT), S("base_added", NT)
    s_step, s_max, s_idx, s_e = S("routing_step", LORA_STEPS), S("top_probs", NT), S("top_experts", NT), S("exps", 1)
    s_gm, s_mtp, s_mtc, s_lo, s_x = S("gated", NT), S("midsT_in_psum", NT), S("midsT_copied", NT), S("lora_out", NT), S("lora_added", NT)
    NL = LE * LR + LE
    with ExitStack() as ctx:
        sb = lambda name, shape, dt=F32: g.sb(ctx, f"lora{rep}_{name}", shape, dt)
        WB, WL, BL, BI = sb("Wbase", [P, KD, D]), sb("Wlora", [P, KD, NL]), sb("B", [P, D]), sb("biases", [P, D + LE])
        XNS, XT = sb("XNS", [P, 2, D]), sb("XT", [P, 2, KD, P])
        MID, LG, BB = sb("MID", [P, NT, LE * LR]), sb("LG", [P, NT, LE]), sb("BB", [P, 2, D])
        MX, SH, EX, SM, RC, PB = sb("MX", [P, NT]), sb("SH", [P, NT, LE]), sb("EX", [P, NT, LE]), sb("SM", [P, NT]), sb("RC", [P, NT]), sb("PB", [P, NT, LE])
        M8, I8, IF = sb("M8", [P, NT, 8]), sb("I8", [P, NT, 8], U32), sb("IF", [P, NT, 8])
        OH, G1, G2, TS, TR, GT = sb("OH", [P, 2, NT, LE]), sb("G1", [P, NT, LE]), sb("G2", [P, NT, LE]), sb("TS", [P, NT]), sb("TR", [P, NT]), sb("GT", [P, NT, LE])
        GM, MT = sb("GM", [P, 2, LE * LR]), sb("MT", [P, 2, P])
        bank = g.bank
        ident = g.C[:, C_ID:C_ID + P]
        with nc.Block() as block:
            @block.sync
            def _(sp):
                sp.dma_start(WB[:, :, :], dram["Wbase"]).then_inc(s_w.handle, 16)
                sp.dma_start(WL[:, :, :], dram["Wlora"]).then_inc(s_w.handle, 16)
                sp.dma_start(BL[:, :], dram["Blora"]).then_inc(s_w.handle, 16)
                sp.dma_start(BI[:, :], dram["biases"].to_broadcast([P, D + LE])).then_inc(s_w.handle, 16)
                sp.wait_ge(s_w.handle, s_w.at(64))

            @block.tensor
            def _(pe):
                pe.wait_ge(s_w.handle, s_w.at(64))
                with pe.Fori(0, NT // 2) as i:
                    for u in range(2):
                        pe.wait_ge(s_xn.handle, s_xn.at(2 * i + u + 1))
                        pe.wait_ge(s_xtc.handle, s_xtc.at(2 * i))
                        for k in range(KD):
                            ins = pe.transpose(bank(u)[:, k * P:(k + 1) * P], XNS[:, u, k * P:(k + 1) * P], ident)
                        ins.then_inc(s_xtp.handle, 1)
                    for u in range(2):
                        pe.wait_ge(s_xtc.handle, s_xtc.at(2 * i + u + 1))
                        pe.wait_ge(s_b1.handle, s_b1.at(2 * i))
                        pe.wait_ge(s_lg.handle, s_lg.at(2 * i))
                        for k in range(KD):
                            pe.matmul(bank(2 + u)[:, 0:D], XT[:, u, k, :], WB[:, k, :], start=(k == 0), stop=(k == KD - 1))
                        for k in range(KD):
                            ins = pe.matmul(bank(4 + u)[:, 0:NL], XT[:, u, k, :], WL[:, k, :], start=(k == 0), stop=(k == KD - 1))
                        ins.then_inc(s_pr.handle, 1)
                with pe.Fori(0, NT // 2) as i:
                    for u in range(2):
                        pe.wait_ge(s_gm.handle, s_gm.at(2 * i + u + 1))
                        pe.wait_ge(s_mtc.handle, s_mtc.at(2 * i))
                        pe.transpose(bank(u)[:, 0:P], GM[:, u, :], ident).then_inc(s_mtp.handle, 1)
                    for u in range(2):
                        pe.wait_ge(s_mtc.handle, s_mtc.at(2 * i + u + 1))
                        pe.wait_ge(s_x.handle, s_x.at(2 * i))
                        pe.matmul(bank(2 + u)[:, 0:D], MT[:, u, :], BL[:, :], start=True, stop=True).then_inc(s_lo.handle, 1)

            @block.scalar
            def _(act):
                norm_sd_act(act, g, s_mv, s_sd)
                act.wait_ge(s_w.handle, s_w.at(64))
                with act.Fori(0, NT // 2) as i:
                    for u in range(2):
                        act.wait_ge(s_xtp.handle, s_xtp.at(2 * i + u + 1))
                        act.wait_ge(s_pr.handle, s_pr.at(2 * i))
                        act.copy(XT[:, u], bank(u)[:, 0:KD * P].rearrange("p (k s) -> p k s", s=P)).then_inc(s_xtc.handle, 1)
                    for u in range(2):
                        act.wait_ge(s_pr.handle, s_pr.at(2 * i + u + 1))
                        act.copy(MID[:, 2 * i + u, :], bank(4 + u)[:, 0:LE * LR]).then_inc(s_mid.handle, 1)
                act.wait_ge(s_step.handle, s_step.at(2))
                act.activation(EX[:, :, :], SH[:, :, :], ACT.Exp).then_inc(s_e.handle, 1)
                with act.Fori(0, NT // 2) as i:
                    for u in range(2):
                        act.wait_ge(s_mtp.handle, s_mtp.at(2 * i + u + 1))
                        act.wait_ge(s_lo.handle, s_lo.at(2 * i))
                        act.copy(MT[:, u, :], bank(u)[:, 0:P]).then_inc(s_mtc.handle, 1)

            @block.vector
            def _(dve):
                norm_stats_dve(dve, g, s_stat, s_mv)
                norm_rs_dve(dve, g, s_sd, s_rs)
                dve.wait_ge(s_w.handle, s_w.at(64))
                for u in range(2):
                    normalize(dve, g, XNS[:, u, :], u).then_inc(s_xn.handle, 1)
                def base_outputs(i, more):
                    for u in range(2):
                        dve.wait_ge(s_pr.handle, s_pr.at(2 * i + u + 1))
                        dve.wait_ge(s_mid.handle, s_mid.at(2 * i + u + 1))
                        dve.tensor_tensor(LG[:, 2 * i + u, :], bank(4 + u)[:, LE * LR:NL], BI[:, D:D + LE], ALU.add).then_inc(s_lg.handle, 1)
                        dve.wait_ge(s_b2.handle, s_b2.at(2 * i))
                        dve.tensor_tensor(BB[:, u, :], bank(2 + u)[:, 0:D], BI[:, 0:D], ALU.add).then_inc(s_b1.handle, 1)
                        dve.wait_ge(s_b1.handle, s_b1.at(2 * i + u + 1))
                        dve.scalar_tensor_tensor(g.X[:, 2 * i + u, :], BB[:, u, :], 0.5, g.X[:, 2 * i + u, :],
                                                 ALU.mult, ALU.add).then_inc(s_b2.handle, 1)
                    for u in range(2 if more else 0):
                        normalize(dve, g, XNS[:, u, :], 2 * i + 2 + u).then_inc(s_xn.handle, 1)

                with dve.Fori(0, NT // 2 - 1) as i:
                    base_outputs(i, True)
                base_outputs(NT // 2 - 1, False)
                dve.wait_ge(s_lg.handle, s_lg.at(NT))
                n = [0]

                def then_wait(ins):
                    n[0] += 1
                    ins.then_inc(s_step.handle, 1)
                    dve.wait_ge(s_step.handle, s_step.at(n[0]))

                then_wait(dve.tensor_reduce(MX[:, :], LG[:, :, :], AX_X, ALU.max))
                then_wait(dve.tensor_tensor(SH[:, :, :], LG[:, :, :], bcast(MX[:, :], 2, LE), ALU.subtract))
                dve.wait_ge(s_e.handle, s_e.at(1))
                then_wait(dve.tensor_reduce(SM[:, :], EX[:, :, :], AX_X, ALU.add))
                then_wait(dve.reciprocal(RC[:, :], SM[:, :]))
                then_wait(dve.tensor_tensor(PB[:, :, :], EX[:, :, :], bcast(RC[:, :], 2, LE), ALU.mult))
                for t in range(NT):
                    dve.max(M8[:, t, :], PB[:, t, :]).then_inc(s_max.handle, 1)
                for t in range(NT):
                    dve.wait_ge(s_max.handle, s_max.at(t + 1))
                    dve.max_index(I8[:, t, :], M8[:, t, :], PB[:, t, :]).then_inc(s_idx.handle, 1)
                dve.wait_ge(s_idx.handle, s_idx.at(NT))
                then_wait(dve.tensor_copy(IF[:, :, :], I8[:, :, :]))
                iota = bcast(g.C[:, C_IOTA:C_IOTA + LE], 1, NT)
                for k in range(2):
                    then_wait(dve.tensor_tensor(OH[:, k], iota, bcast(IF[:, :, k], 2, LE), ALU.is_equal))
                then_wait(dve.tensor_tensor(G1[:, :, :], OH[:, 0], bcast(M8[:, :, 0], 2, LE), ALU.mult))
                then_wait(dve.tensor_tensor(G2[:, :, :], OH[:, 1], bcast(M8[:, :, 1], 2, LE), ALU.mult))
                then_wait(dve.tensor_tensor(SH[:, :, :], G1[:, :, :], G2[:, :, :], ALU.add))
                then_wait(dve.tensor_tensor(TS[:, :], M8[:, :, 0], M8[:, :, 1], ALU.add))
                then_wait(dve.reciprocal(TR[:, :], TS[:, :]))
                then_wait(dve.tensor_tensor(GT[:, :, :], SH[:, :, :], bcast(TR[:, :], 2, LE), ALU.mult))
                assert n[0] == LORA_STEPS
                dve.wait_ge(s_mid.handle, s_mid.at(NT))
                dve.wait_ge(s_b2.handle, s_b2.at(NT))

                def gated(u, t):
                    mid = MID[:, t, :].rearrange("p (e r) -> p e r", r=LR)
                    dve.tensor_tensor(GM[:, u, :].rearrange("p (e r) -> p e r", r=LR), mid, bcast(GT[:, t, :], 2, LR), ALU.mult).then_inc(s_gm.handle, 1)

                gated(0, 0)
                gated(1, 1)

                def lora_outputs(i, more):
                    for u in range(2 if more else 0):
                        dve.wait_ge(s_mtp.handle, s_mtp.at(2 * i + u + 1))
                        gated(u, 2 * i + 2 + u)
                    for u in range(2):
                        dve.wait_ge(s_lo.handle, s_lo.at(2 * i + u + 1))
                        dve.scalar_tensor_tensor(g.X[:, 2 * i + u, :], bank(2 + u)[:, 0:D], 0.5 * LORA_SCALE, g.X[:, 2 * i + u, :],
                                                 ALU.mult, ALU.add).then_inc(s_x.handle, 1)

                with dve.Fori(0, NT // 2 - 1) as i:
                    lora_outputs(i, True)
                lora_outputs(NT // 2 - 1, False)


def mla_stage(nc, g, dram):
    S = lambda name: g.sem("mla_" + name).handle
    s_w, s_w2 = S("weights"), S("up_weights")
    s_stat, s_mv, s_sd, s_rs = (g.sem("mla_" + n) for n in ("partial_stats", "stats", "deviations", "reciprocals"))
    s_gp, s_gc, s_up, s_uc = S("absorbed_q_in_psum"), S("absorbed_q"), S("absorbed_v_in_psum"), S("absorbed_v")
    s_xn, s_xtp, s_xtc, s_cp, s_cc, s_sq = S("xn_tile"), S("xnT_in_psum"), S("xnT_copied"), S("latents_in_psum"), S("latents_copied"), S("squares")
    s_rd, s_rr, s_re, s_xb, s_xs = S("latent_deviations"), S("latent_scales"), S("latent_mean_squares"), S("sequence_xnT"), S("xnT_saved")
    s_cn, s_cn2, s_ctp, s_cq, s_ckh, s_ckl = S("latents"), S("latent_twice"), S("latentsT_in_psum"), S("cqT_copied"), S("latent_keys_high"), S("latent_keys_low")
    s_pr, s_ab, s_ro, s_rows = S("projected"), S("latent_queries"), S("rotary_products"), S("rotary_rows")
    s_qkp, s_hi, s_lo = S("qkT_in_psum"), S("high_parts"), S("low_parts")
    s_sc, s_mx, s_nb, s_p = S("scores"), S("row_max"), S("negative_max"), S("probs")
    s_ptp, s_ptc, s_ot, s_otc, s_bt = S("probsT_in_psum"), S("probsT_copied"), S("outT_in_psum"), S("outT_copied"), S("out_in_psum")
    s_dn, s_la = S("denominators"), S("latent_rows")
    s_lp, s_lc, s_o, s_x = S("latent_rowsT_in_psum"), S("latent_rowsT_copied"), S("outputs"), S("x_updated")
    NL = DQL + DKVL
    NU = 2 * TB
    with ExitStack() as ctx:
        sb = lambda name, shape, dt=F32: g.sb(ctx, "mla_" + name, shape, dt)
        WR = sb("Wrope", [P, KD, NP1 * 4 * RD])
        WD, WN = sb("Wdown", [P, KD, NL]), sb("norms", [P, NL])
        RO = sb("rope", [P, 2, TB, RD])
        GQ, UV = sb("GQ", [DQL, H1 * DKVL]), sb("UV", [P, NP1, D])
        bank, banks = g.bank, g.banks
        ident = g.C[:, C_ID:C_ID + P]
        kv = slice(DQL, NL)

        with ExitStack() as up:
            WQT, WKT, WVT = (g.sb(up, "mla_" + n, [P, H1, m]) for n, m in (("WqT", DQL), ("WkT", DKVL), ("WvT", DKVL)))
            WOU = g.sb(up, "mla_Wout", [P, H1, D])
            with nc.Block() as block:
                @block.sync
                def _(sp):
                    for dst, name in ((WQT, "WqT"), (WKT, "WkT"), (WVT, "WvT"), (WOU, "Wout")):
                        sp.dma_start(dst[:, :, :], dram[name]).then_inc(s_w2, 16)
                    sp.dma_start(WD[:, :, :], dram["Wdown"]).then_inc(s_w, 16)
                    sp.dma_start(WN[:, :], dram["norms"].to_broadcast([P, NL])).then_inc(s_w, 16)
                    sp.dma_start(RO[:, :, :, :], dram["rope"].rearrange("p c t d -> p c t d")).then_inc(s_w, 16)
                    sp.dma_start(WR[:, :, :], dram["Wrope"]).then_inc(s_w, 16)
                    sp.wait_ge(s_w, 64)
                    sp.wait_ge(s_w2, 64)

                @block.tensor
                def _(pe):
                    pe.wait_ge(s_w2, 64)
                    for h in range(H1):
                        ins = pe.matmul(bank(h // 8)[0:DQL, h % 8 * DKVL:(h % 8 + 1) * DKVL], WQT[:, h, :], WKT[:, h, :], start=True, stop=True)
                    ins.then_inc(s_gp, 1)
                    for h in range(H1):
                        ins = pe.matmul(bank(2 + h // 4)[h % 2 * DKVL:(h % 2 + 1) * DKVL, h // 2 % 2 * D:(h // 2 % 2 + 1) * D],
                                        WVT[:, h, :], WOU[:, h, :], start=True, stop=True)
                    ins.then_inc(s_up, 1)

                @block.scalar
                def _(act):
                    act.wait_ge(s_gp, 1)
                    act.copy(GQ[:, :], banks(0, 2)[0:DQL, :]).then_inc(s_gc, 1)
                    act.wait_ge(s_up, 1)
                    for m in range(4):
                        act.copy(UV[:, 2 * m:2 * m + 2, :].rearrange("p a d -> p (a d)"), bank(2 + m)[:, :]).then_inc(s_uc, 1)

        XNS, XTS = sb("XNS", [P, 2, D]), sb("XTS", [P, 2, KD, P])
        XTA, XT = sb("XTA", [P, KD, NT * P]), sb("XT", [P, KD, SEQ])
        CR, SQ, SS = sb("CR", [P, NT, NL]), sb("SQ", [P, 2, NL]), sb("SS", [P, 2, NT])
        SE, SD2, RS2 = sb("SE", [P, 2, NT]), sb("SD2", [P, 2, NT]), sb("RS2", [P, 2, NT])
        CN = sb("CN", [P, TB, DQL + 2 * DKVL])
        CQ = sb("CQ", [DQL, SEQ])
        QH, QL, KH, KL = (sb(n, [P, 2, SEQ], F32R) for n in ("QH", "QL", "KH", "KL"))
        T1, T2 = sb("T1", [P, 2, 4 * RD]), sb("T2", [P, 2, 4 * RD])
        QR, KR = sb("QR", [P, 2, 6 * RD]), sb("KR", [P, 2, 2 * RD])
        PR, PT = sb("PR", [P, 2, SEQ]), sb("PT", [P, 2, 2, TB, P])
        MX, NB, DN, RD_ = sb("MX", [P, NU]), sb("NB", [P, NU]), sb("DN", [P, NU]), sb("RD", [P, NU])
        OT, LA, LT = sb("OT", [P, P]), sb("LA", [P, TB, NP1 * P]), sb("LT", [P, 2, NP1, P])

        with nc.Block() as block:
            @block.tensor
            def _(pe):
                with pe.Fori(0, NT // 2) as i:
                    for u in range(2):
                        pe.wait_ge(s_xn, 2 * i + u + 1)
                        pe.wait_ge(s_xtc, 2 * i)
                        for k in range(KD):
                            ins = pe.transpose(bank(u)[:, k * P:(k + 1) * P], XNS[:, u, k * P:(k + 1) * P], ident)
                        ins.then_inc(s_xtp, 1)
                    for u in range(2):
                        pe.wait_ge(s_xtc, 2 * i + u + 1)
                        pe.wait_ge(s_cc, 2 * i)
                        for k in range(KD):
                            ins = pe.matmul(bank(2 + u)[:, 0:NL], XTS[:, u, k, :], WD[:, k, :], start=(k == 0), stop=(k == KD - 1))
                        ins.then_inc(s_cp, 1)
                with pe.Fori(0, BATCH) as b:
                    for j in range(TB):
                        pe.wait_ge(s_cn2, TB * b + j + 1)
                        if j >= 2:
                            pe.wait_ge(s_cq, TB * b + j - 1)
                            pe.wait_ge(s_ckl, 2 * (TB * b + j - 1))
                        pe.transpose(bank(j % 2)[:, 0:P], CN[:, j, 0:P], ident)
                        pe.transpose(bank(j % 2)[:, P:2 * P], CN[:, j, DQL:DQL + 2 * DKVL], ident).then_inc(s_ctp, 1)
                    with pe.Fori(0, NP1) as r:
                        it = b * NP1 + r
                        pe.wait_ge(s_cq, TB * (b + 1))
                        pe.wait_ge(s_ckl, 2 * TB * (b + 1))
                        pe.wait_ge(s_xb, b + 1)

                        def qk_transposes(j):
                            pe.wait_ge(s_rows, 2 * (TB * it + j + 1))
                            if j >= 2:
                                pe.wait_ge(s_lo, 3 * (TB * it + j - 1))
                            for m in range(2):
                                pe.transpose(bank(2 + j % 2)[:, m * P:(m + 1) * P], QR[:, j % 2, m * P:(m + 1) * P], ident)
                            pe.transpose(bank(2 + j % 2)[:, 2 * P:3 * P], KR[:, j % 2, :], ident).then_inc(s_qkp, 1)

                        for j in range(TB):
                            if j >= 2:
                                pe.wait_ge(s_ro, 3 * (TB * it + j - 1))
                            for k in range(KD):
                                pe.matmul(bank(j % 2)[:, 0:4 * RD], XT[:, k, j * P:(j + 1) * P], WR[:, k, bass.ds(r * (4 * RD), 4 * RD)],
                                          start=(k == 0), stop=(k == KD - 1))
                            pe.matmul(bank(j % 2)[:, 4 * RD:6 * RD], CQ[:, j * P:(j + 1) * P], GQ[:, bass.ds(r * (2 * RD), 2 * RD)],
                                      start=True, stop=True).then_inc(s_pr, 1)
                            if j:
                                qk_transposes(j - 1)
                        qk_transposes(TB - 1)
                        pe.wait_ge(s_lo, 3 * TB * (it + 1))

                        def scores_of(n):
                            i, h = n // 2, n % 2
                            if n >= 2:
                                pe.wait_ge(s_p, NU * it + n - 1)
                            qs = slice(i * P, (i + 1) * P)
                            for c in range(2):
                                ks = slice(c * 512, (c + 1) * 512)
                                for m, (q, k) in enumerate(((QH, KH), (QL, KH), (QH, KL))):
                                    ins = pe.matmul(bank(2 * h + c)[:, :], q[:, h, qs], k[:, h, ks], start=(m == 0), stop=(m == 2))
                            ins.then_inc(s_sc, 1)

                        def transposes_of(n):
                            pe.wait_ge(s_p, NU * it + n + 1)
                            for c in range(2):
                                if n:
                                    pe.wait_ge(s_ptc, 2 * (NU * it + n) + c - 1)
                                for k in range(4):
                                    ins = pe.transpose(bank(4 + c)[:, k * P:(k + 1) * P], PR[:, n % 2, (4 * c + k) * P:(4 * c + k + 1) * P], ident)
                                ins.then_inc(s_ptp, 1)

                        def values_of(i):
                            pe.wait_ge(s_ptc, 2 * NU * it + 4 * (i + 1))
                            if i:
                                pe.wait_ge(s_otc, TB * it + i)
                            for k in range(TB):
                                for h in range(2):
                                    ins = pe.matmul(bank(6)[h * DKVL:(h + 1) * DKVL, 0:P], CN[:, k, DQL:DQL + DKVL], PT[:, i % 2, h, k, :],
                                                    start=(k == 0), stop=(k == TB - 1))
                            ins.then_inc(s_ot, 1)

                        def out_rows_of(i):
                            pe.wait_ge(s_otc, TB * it + i + 1)
                            if i:
                                pe.wait_ge(s_la, TB * it + i)
                            pe.transpose(bank(7)[:, 0:P], OT[:, :], ident).then_inc(s_bt, 1)

                        scores_of(0)
                        for n in range(NU):
                            if n + 1 < NU:
                                scores_of(n + 1)
                            transposes_of(n)
                            if n >= 2 and n % 2 == 0:
                                values_of(n // 2 - 1)
                            if n >= 2 and n % 2 == 1:
                                out_rows_of(n // 2 - 1)
                        values_of(TB - 1)
                        out_rows_of(TB - 1)
                    for i in range(TB):
                        pe.wait_ge(s_la, TB * NP1 * (b + 1))
                        for c in range(2):
                            if i:
                                pe.wait_ge(s_lc, 2 * (TB * b + i) + c - 1)
                            for k in range(4):
                                ins = pe.transpose(bank(4 + c)[:, k * P:(k + 1) * P], LA[:, i, (4 * c + k) * P:(4 * c + k + 1) * P], ident)
                            ins.then_inc(s_lp, 1)
                        pe.wait_ge(s_lc, 2 * (TB * b + i + 1))
                        if i >= 2:
                            pe.wait_ge(s_x, TB * b + i - 1)
                        for k in range(NP1):
                            ins = pe.matmul(bank(6 + i % 2)[:, 0:D], LT[:, i % 2, k, :], UV[:, k, :], start=(k == 0), stop=(k == NP1 - 1))
                        ins.then_inc(s_o, 1)
                    pe.wait_ge(s_x, TB * (b + 1))

            @block.scalar
            def _(act):
                norm_sd_act(act, g, s_mv, s_sd)
                with act.Fori(0, NT // 2) as i:
                    for u in range(2):
                        t = 2 * i + u
                        act.wait_ge(s_xtp, t + 1)
                        act.wait_ge(s_cp, 2 * i)
                        act.copy(XTS[:, u], bank(u)[:, 0:KD * P].rearrange("p (k s) -> p k s", s=P)).then_inc(s_xtc, 1)
                        act.wait_ge(s_xtc, t + 1)
                        act.copy(XTA[:, :, bass.ds(t * P, P)], XTS[:, u]).then_inc(s_xs, 1)
                    for u in range(2):
                        t = 2 * i + u
                        act.wait_ge(s_cp, t + 1)
                        act.wait_ge(s_sq, 4 * i)
                        for m, cols in enumerate((slice(0, DQL), kv)):
                            act.activation(SQ[:, u, cols], bank(2 + u)[:, cols], ACT.Square, accum_out=SS[:, m, bass.ds(t, 1)]).then_inc(s_sq, 1)
                        act.copy(CR[:, t, :], bank(2 + u)[:, 0:NL]).then_inc(s_cc, 1)
                act.wait_ge(s_re, 1)
                act.activation(SD2[:, :, :], SE[:, :, :], ACT.Sqrt, bias=g.C[:, C_EPS + 1:C_EPS + 2]).then_inc(s_rd, 1)
                with act.Fori(0, BATCH) as b:
                    act.wait_ge(s_xs, NT)
                    act.wait_ge(s_pr, TB * NP1 * b)
                    act.copy(XT[:, :, :], XTA[:, :, bass.ds(b * SEQ, SEQ)]).then_inc(s_xb, 1)
                    for j in range(TB):
                        tok = slice(j * P, (j + 1) * P)
                        act.wait_ge(s_ctp, TB * b + j + 1)
                        act.copy(CQ[:, tok], bank(j % 2)[0:DQL, 0:P]).then_inc(s_cq, 1)
                        act.copy(KH[DKVL:P, 0, tok], bank(j % 2)[DKVL:P, P:2 * P]).then_inc(s_ckh, 1)
                        act.copy(KH[0:DKVL, 1, tok], bank(j % 2)[0:DKVL, P:2 * P]).then_inc(s_ckh, 1)
                    with act.Fori(0, NP1) as r:
                        it = b * NP1 + r

                        def highs(j):
                            tok = slice(j * P, (j + 1) * P)
                            act.wait_ge(s_qkp, TB * it + j + 1)
                            act.copy(QH[:, :, tok], bank(2 + j % 2)[:, 0:2 * P].rearrange("p (m s) -> p m s", m=2)).then_inc(s_hi, 1)
                            act.copy(KH[0:RD, 0, tok], bank(2 + j % 2)[0:RD, 2 * P:3 * P]).then_inc(s_hi, 1)
                            act.copy(KH[RD:P, 1, tok], bank(2 + j % 2)[RD:P, 2 * P:3 * P]).then_inc(s_hi, 1)

                        for j in range(TB):
                            act.wait_ge(s_pr, TB * it + j + 1)
                            if j >= 2:
                                act.wait_ge(s_qkp, TB * it + j - 1)
                            act.copy(QR[:, j % 2, RD:3 * RD], bank(j % 2)[:, 4 * RD:6 * RD]).then_inc(s_ab, 1)
                            if j:
                                highs(j - 1)
                        highs(TB - 1)

                        def copies_of(n):
                            i, h = n // 2, n % 2
                            for c in range(2):
                                act.wait_ge(s_ptp, 2 * (NU * it + n) + c + 1)
                                if i >= 2 and h == 0 and c == 0:
                                    act.wait_ge(s_ot, TB * it + i - 1)
                                act.copy(PT[:, i % 2, h, 4 * c:4 * c + 4, :], bank(4 + c)[:, :].rearrange("p (k s) -> p k s", s=P)).then_inc(s_ptc, 1)

                        for n in range(NU):
                            act.wait_ge(s_nb, NU * it + n + 1)
                            if n >= 2:
                                act.wait_ge(s_ptp, 2 * (NU * it + n - 1))
                            act.activation(PR[:, n % 2, :], banks(2 * (n % 2), 2)[:, :], ACT.Exp, bias=NB[:, n:n + 1], scale=MLA_SCALE,
                                           accum_out=DN[:, n:n + 1]).then_inc(s_p, 1)
                            if n:
                                copies_of(n - 1)
                        copies_of(NU - 1)
                    for i in range(TB):
                        for c in range(2):
                            act.wait_ge(s_lp, 2 * (TB * b + i) + c + 1)
                            if i >= 2 and c == 0:
                                act.wait_ge(s_o, TB * b + i - 1)
                            act.copy(LT[:, i % 2, 4 * c:4 * c + 4, :], bank(4 + c)[:, :].rearrange("p (k s) -> p k s", s=P)).then_inc(s_lc, 1)

            @block.gpsimd
            def _(pool):
                with pool.Fori(0, BATCH * NP1) as it:
                    for j in range(TB):
                        u = j % 2
                        pool.wait_ge(s_ro, 3 * (TB * it + j + 1))
                        if j >= 2:
                            pool.wait_ge(s_qkp, TB * it + j - 1)
                        heads = lambda ap: ap.rearrange("p (m d) -> p m d", m=2)
                        qr = QR[:, u, :].rearrange("p (m d) -> p m d", m=2)[:, :, 0:RD]
                        pool.tensor_tensor(qr, heads(T1[:, u, 0:2 * RD]), heads(T2[:, u, 0:2 * RD]), ALU.add).then_inc(s_rows, 1)
                        pool.tensor_tensor(KR[:, u, :], T1[:, u, 2 * RD:4 * RD], T2[:, u, 2 * RD:4 * RD], ALU.add).then_inc(s_rows, 1)

            @block.vector
            def _(dve):
                norm_stats_dve(dve, g, s_stat, s_mv)
                norm_rs_dve(dve, g, s_sd, s_rs)
                with dve.Fori(0, NT // 2) as i:
                    for u in range(2):
                        dve.wait_ge(s_xtp, 2 * i)
                        normalize(dve, g, XNS[:, u, :], 2 * i + u).then_inc(s_xn, 1)
                dve.wait_ge(s_sq, 2 * NT)
                for m, n in enumerate((DQL, DKVL)):
                    ins = dve.tensor_scalar(SE[:, m, :], SS[:, m, :], 1.0 / n, None, ALU.mult)
                ins.then_inc(s_re, 1)
                dve.wait_ge(s_rd, 1)
                dve.reciprocal(RS2[:, :, :], SD2[:, :, :]).then_inc(s_rr, 1)
                dve.wait_ge(s_rr, 1)
                with dve.Fori(0, BATCH) as b:
                    for j in range(TB):
                        t = TB * b + j
                        dve.scalar_tensor_tensor(CN[:, j, 0:DQL], CR[:, t, 0:DQL], RS2[:, 0, bass.ds(t, 1)], WN[:, 0:DQL], ALU.mult, ALU.mult)
                        for m in range(2):
                            ins = dve.scalar_tensor_tensor(CN[:, j, DQL + m * DKVL:DQL + (m + 1) * DKVL], CR[:, t, kv], RS2[:, 1, bass.ds(t, 1)],
                                                           WN[:, kv], ALU.mult, ALU.mult)
                        ins.then_inc(s_cn2, 1)
                    for j in range(TB):
                        tok = slice(j * P, (j + 1) * P)
                        dve.wait_ge(s_ckh, 2 * (TB * b + j + 1))
                        dve.tensor_tensor(KL[DKVL:P, 0, tok], bank(j % 2)[DKVL:P, P:2 * P], KH[DKVL:P, 0, tok].bitcast(F32), ALU.subtract).then_inc(s_ckl, 1)
                        dve.tensor_tensor(KL[0:DKVL, 1, tok], bank(j % 2)[0:DKVL, P:2 * P], KH[0:DKVL, 1, tok].bitcast(F32), ALU.subtract).then_inc(s_ckl, 1)
                    with dve.Fori(0, NP1) as r:
                        it = b * NP1 + r

                        def lows(j):
                            tok = slice(j * P, (j + 1) * P)
                            dve.wait_ge(s_hi, 3 * (TB * it + j + 1))
                            dve.tensor_tensor(QL[:, :, tok], bank(2 + j % 2)[:, 0:2 * P].rearrange("p (m s) -> p m s", m=2),
                                              QH[:, :, tok].bitcast(F32), ALU.subtract).then_inc(s_lo, 1)
                            dve.tensor_tensor(KL[0:RD, 0, tok], bank(2 + j % 2)[0:RD, 2 * P:3 * P], KH[0:RD, 0, tok].bitcast(F32), ALU.subtract).then_inc(s_lo, 1)
                            dve.tensor_tensor(KL[RD:P, 1, tok], bank(2 + j % 2)[RD:P, 2 * P:3 * P], KH[RD:P, 1, tok].bitcast(F32), ALU.subtract).then_inc(s_lo, 1)

                        for j in range(TB):
                            u = j % 2
                            dve.wait_ge(s_ab, TB * it + j + 1)
                            if j >= 2:
                                dve.wait_ge(s_rows, 2 * (TB * it + j - 1))
                            rot = bank(u)[:, 0:4 * RD].rearrange("p (m d) -> p m d", d=RD)
                            t1, t2 = (t[:, u, :].rearrange("p (m d) -> p m d", d=RD) for t in (T1, T2))
                            half = RD // 2
                            dve.tensor_tensor(t1, rot, bcast(RO[:, 0, j, :], 1, 4), ALU.mult).then_inc(s_ro, 1)
                            dve.tensor_tensor(t2[:, :, 0:half], rot[:, :, half:RD], bcast(RO[:, 1, j, 0:half], 1, 4), ALU.mult).then_inc(s_ro, 1)
                            dve.tensor_tensor(t2[:, :, half:RD], rot[:, :, 0:half], bcast(RO[:, 1, j, half:RD], 1, 4), ALU.mult).then_inc(s_ro, 1)
                            if j:
                                lows(j - 1)
                        lows(TB - 1)

                        def finish(i):
                            dve.wait_ge(s_bt, TB * it + i + 1)
                            dve.reciprocal(RD_[:, 2 * i:2 * i + 2], DN[:, 2 * i:2 * i + 2]).then_inc(s_dn, 1)
                            dve.wait_ge(s_dn, TB * it + i + 1)
                            dve.tensor_tensor(LA[:, i, bass.ds(r * P, P)].rearrange("p (h d) -> p h d", h=2),
                                              bank(7)[:, 0:P].rearrange("p (h d) -> p h d", h=2), bcast(RD_[:, 2 * i:2 * i + 2], 2, DKVL), ALU.mult).then_inc(s_la, 1)

                        def out_copy(i):
                            dve.wait_ge(s_ot, TB * it + i + 1)
                            if i:
                                dve.wait_ge(s_bt, TB * it + i)
                            dve.tensor_copy(OT[:, :], bank(6)[:, 0:P]).then_inc(s_otc, 1)

                        for n in range(NU):
                            dve.wait_ge(s_sc, NU * it + n + 1)
                            dve.tensor_reduce(MX[:, n:n + 1], banks(2 * (n % 2), 2)[:, :], AX_X, ALU.max).then_inc(s_mx, 1)
                            dve.wait_ge(s_mx, NU * it + n + 1)
                            dve.tensor_scalar(NB[:, n:n + 1], MX[:, n:n + 1], -MLA_SCALE, None, ALU.mult).then_inc(s_nb, 1)
                            if n >= 3 and n % 2 == 1:
                                out_copy(n // 2 - 1)
                            if n >= 4 and n % 2 == 0:
                                finish(n // 2 - 2)
                        finish(TB - 2)
                        out_copy(TB - 1)
                        finish(TB - 1)
                    for i in range(TB):
                        dve.wait_ge(s_o, TB * b + i + 1)
                        xt = g.X[:, b * TB + i, :]
                        dve.tensor_tensor(xt, bank(6 + i % 2)[:, 0:D], xt, ALU.add).then_inc(s_x, 1)


def store_stage(nc, g, out):
    s_out = g.sem("stored")
    with nc.Block() as block:
        @block.sync
        def _(sp):
            sp.dma_start(out.rearrange("b (t p) d -> p (b t) d", p=P), g.X[:, :, :]).then_inc(s_out.handle, 16)
            sp.wait_ge(s_out.handle, 16)


def macaron_program(nc, dram, out, stages="mamlLl"):
    with ExitStack() as ctx:
        g = Core(nc, ctx)
        g.X = g.sb(ctx, "X", [P, NT, D])
        g.C = g.sb(ctx, "C", [P, C_END])
        g.ST = g.sb(ctx, "ST", [P, NT, 6])
        g.MV = g.sb(ctx, "MV", [P, NT, 2])
        g.SD = g.sb(ctx, "SD", [P, NT])
        g.RS = g.sb(ctx, "RS", [P, NT])
        g.XG = nc.dram_tensor("slots_in", [(NTILE + 2) * P, D], F32, kind="Internal").ap()
        g.YG = nc.dram_tensor("slots_out", [NTILE * P, D], F32, kind="Internal").ap()
        PS = ctx.enter_context(nc.psum_tensor("PS", [P, 8, 512], F32))
        g.bank = lambda n: PS[:, n, :]
        g.banks = lambda n, m: PS[:, n:n + m, :].rearrange("p b c -> p (b c)")
        g.s_w1 = g.sem("loaded_W1")
        g.s_second = [g.sem(f"second_added{r}") for r in range(2)]
        with ExitStack() as moe:
            g.XN = g.sb(moe, "XN", [P, NT, D])
            g.W1 = g.sb(moe, "W1", [P, NE, KD, FF])
            load_stage(nc, g, dram)
            moe_stage(nc, g, dram, 0)
            if "a" in stages:
                attention_stage(nc, g, dram)
            if stages.count("m") > 1:
                moe_stage(nc, g, dram, 1)
        if "l" in stages:
            lora_stage(nc, g, dram, 0)
        if "L" in stages:
            mla_stage(nc, g, dram)
        if stages.count("l") > 1:
            lora_stage(nc, g, dram, 1)
        store_stage(nc, g, out)


def shape_constants():
    c = np.zeros((P, C_END), np.float32)
    c[:, C_ID:C_ID + P] = np.eye(P)
    c[:, C_ONE:C_ONE + P] = 1.0
    c[:, C_TRI:C_TRI + P] = np.triu(np.ones((P, P)), 1)
    c[:, C_LOW:C_LOW + P] = np.tril(np.ones((P, P)))
    c[:, C_IOTA:C_IOTA + NE] = np.arange(NE)
    c[:, C_TILE:C_TILE + NTILE] = np.arange(NTILE)
    c[:, C_EPS] = LN_EPS
    c[:, C_EPS + 1] = RMS_EPS
    freqs = (np.float32(1.0) / np.float32(10000.0) ** (np.arange(0, RD, 2, dtype=np.float32) / np.float32(RD))).astype(np.float32)
    ang = np.outer(np.arange(SEQ, dtype=np.float32), freqs).astype(np.float32)
    cos, sin = np.cos(ang).astype(np.float32), np.sin(ang).astype(np.float32)
    rope = np.stack([np.concatenate([cos, cos], 1), np.concatenate([-sin, sin], 1)])
    rope = rope.reshape(2, TB, P, RD).transpose(2, 0, 1, 3)
    return c, np.ascontiguousarray(rope)


def lay_out(a):
    f = np.ascontiguousarray
    chunks = lambda w: w.reshape(w.shape[0] // P, P, -1).transpose(1, 0, 2)
    const, rope = shape_constants()
    r = {"const": const, "rope": rope, "x": f(a["L0_attn_x"].reshape(BATCH * SEQ, D))}
    r["router_w"] = f(chunks(a["L0_ffn_router_w"]))
    r["W1"] = f(a["L0_ffn_W1"].reshape(NE, KD, P, FF).transpose(2, 0, 1, 3))
    r["W2"] = f(a["L0_ffn_W2"].reshape(NE, KF, P, D).transpose(2, 0, 1, 3))
    heads = lambda w: w.reshape(D, NG0, HG * DH0)
    r["Wqkv"] = f(chunks(np.concatenate([heads(a["L0_attn_Wq"]), heads(a["L0_attn_Wk"]), heads(a["L0_attn_Wv"])], 2).reshape(D, -1)))
    r["Wo"] = f(chunks(a["L0_attn_Wo"]))
    pairs = lambda w: w.reshape(D, NP1, 2, RD // 2, 2).transpose(0, 1, 2, 4, 3).reshape(D, NP1, 1, 2 * RD)
    r["Wrope"] = f(chunks(np.concatenate([pairs(a["L1_attn_Wq_rope"]), pairs(a["L1_attn_Wk_rope"])], 2).reshape(D, -1)))
    r["Wdown"] = f(chunks(np.concatenate([a["L1_attn_Wq_down"], a["L1_attn_Wkv_down"]], 1)))
    r["norms"] = f(np.concatenate([a["L1_attn_q_norm_w"], a["L1_attn_kv_norm_w"]]).reshape(1, -1))
    up = lambda w: f(w.reshape(-1, H1, HD1).transpose(2, 1, 0))
    r["WqT"], r["WkT"], r["WvT"] = up(a["L1_attn_Wq_up"]), up(a["L1_attn_Wk_up"]), up(a["L1_attn_Wv_up"])
    r["Wout"] = f(a["L1_attn_Wout"].reshape(H1, HD1, D).transpose(1, 0, 2))
    r["Wbase"] = f(chunks(np.ascontiguousarray(a["L1_ffn_base_w"].T)))
    lora = a["L1_ffn_lora_A"].transpose(1, 0, 2).reshape(D, LE * LR)
    r["Wlora"] = f(chunks(np.concatenate([lora, a["L1_ffn_router_w"].T], 1)))
    r["Blora"] = f(a["L1_ffn_lora_B"].reshape(LE * LR, D))
    r["biases"] = f(np.concatenate([a["L1_ffn_base_b"], a["L1_ffn_router_b"]]).reshape(1, -1))
    return r


def kernel(**inputs):
    import concourse.bacc as _bacc
    from concourse.bass_utils import run_bass_kernel_spmd as _run

    nc = _bacc.Bacc("TRN2", target_bir_lowering=False, num_devices=1)
    arrays, dram = {}, {}
    for name, a in lay_out({k: np.asarray(v) for k, v in inputs.items()}).items():
        arrays[f"in_{name}_dram"] = a
        dram[name] = nc.dram_tensor(f"in_{name}_dram", a.shape, F32, kind="ExternalInput").ap()
    out = nc.dram_tensor("out_0_dram", (BATCH, SEQ, D), F32, kind="ExternalOutput").ap()
    macaron_program(nc, dram, out)
    r = _run(nc, [arrays], core_ids=[0])
    return r.results[0]["out_0_dram"]
```

```python
from contextlib import ExitStack

import numpy as np

import concourse.bass as bass
from concourse import mybir

F32 = mybir.dt.float32
F32R = mybir.dt.float32r
I32 = mybir.dt.int32
U32 = mybir.dt.uint32
ALU = mybir.AluOpType
ACT = mybir.ActivationFunctionType
AX_X = mybir.AxisListType.X
AX_XY = mybir.AxisListType.XY

P = 128
BATCH, SEQ, D = 2, 1024, 256
NT = BATCH * SEQ // P
TB = SEQ // P
KD = D // P
LN_EPS = 1e-5

NE, FF, TOP = 16, 512, 2
KF = FF // P
NTILE = 48
assert NTILE >= NT * TOP + NE - 1 and NTILE % 2 == 0

H0, DH0 = 16, 16
HG = 4
NG0 = H0 // HG
VW = 32

H1, RD, HD1, DQL, DKVL = 16, 64, 128, 48, 64
NP1 = H1 // 2
MLA_SCALE = float(HD1 + RD) ** -0.5
RMS_EPS = 1e-6

LE, LR = 8, 16
LORA_SCALE = 2.0

MOE_STEPS = 54
LORA_STEPS = 14

C_ID, C_ONE, C_TRI, C_LOW, C_IOTA, C_TILE = 0, 128, 256, 384, 512, 528
C_EPS = C_TILE + NTILE
C_END = C_EPS + 2


class Sem:

    def __init__(self, handle, each, rep, pool_dma):
        self.handle, self.base = handle, each * rep + (0 if pool_dma else 1)

    def at(self, n):
        return self.base + n


def bcast(ap, axis, n):
    ap = ap.unsqueeze(axis)
    shape = list(ap.shape)
    shape[axis] = n
    return ap.to_broadcast(shape)


class Core:

    def __init__(self, nc, ctx):
        self.nc, self.ctx = nc, ctx
        self.handles = {}
        self.fresh = []

    def sb(self, ctx, name, shape, dt=F32):
        return ctx.enter_context(self.nc.sbuf_tensor(name, shape, dt))

    def sem(self, name, each=0, rep=0, pool_dma=False):
        if name not in self.handles:
            self.handles[name] = self.ctx.enter_context(self.nc.semaphore(name))
            if not pool_dma:
                self.fresh.append(self.handles[name])
        return Sem(self.handles[name], each, rep, pool_dma)

    def credit(self, sp):
        for handle in self.fresh:
            sp.sem_inc(handle, 1)
        self.fresh = []


def norm_stats_dve(dve, g, s_stat, s_mv):
    with dve.Fori(0, NT) as t:
        dve.bn_stats(g.ST[:, t, :], g.X[:, t, :]).then_inc(s_stat.handle, 1)
    dve.wait_ge(s_stat.handle, s_stat.at(NT))
    for t in range(NT):
        dve.bn_aggr(g.MV[:, t, :], g.ST[:, t, :]).then_inc(s_mv.handle, 1)


def norm_sd_act(act, g, s_mv, s_sd):
    act.wait_ge(s_mv.handle, s_mv.at(NT))
    act.activation(g.SD[:, :], g.MV[:, :, 1], ACT.Sqrt, bias=g.C[:, C_EPS:C_EPS + 1]).then_inc(s_sd.handle, 1)


def norm_rs_dve(dve, g, s_sd, s_rs):
    dve.wait_ge(s_sd.handle, s_sd.at(1))
    dve.reciprocal(g.RS[:, :], g.SD[:, :]).then_inc(s_rs.handle, 1)
    dve.wait_ge(s_rs.handle, s_rs.at(1))


def normalize(dve, g, out, t):
    return dve.tensor_scalar(out, g.X[:, t, :], g.MV[:, t, 0:1], g.RS[:, bass.ds(t, 1)], ALU.subtract, ALU.mult)


def load_stage(nc, g, dram):
    s_in = g.sem("loaded_x")
    s_c = g.sem("loaded_constants")
    s_z = g.sem("zeros_made")
    s_zd = g.sem("slots_zeroed", pool_dma=True)
    with nc.Block() as block:
        @block.sync
        def _(sp):
            g.credit(sp)
            sp.dma_start(g.X[:, :, :], dram["x"].rearrange("(t p) d -> p t d", p=P)).then_inc(s_in.handle, 16)
            sp.dma_start(g.C[:, :], dram["const"]).then_inc(s_c.handle, 16)
            for e in range(0, NE, 4):
                sp.dma_start(g.W1[:, e:e + 4], dram["W1"][:, e:e + 4]).then_inc(g.s_w1.handle, 16)
            sp.wait_ge(s_in.handle, s_in.at(16))
            sp.wait_ge(s_c.handle, s_c.at(16))

        @block.vector
        def _(dve):
            dve.memset(g.XN[:, 0, :], 0.0).then_inc(s_z.handle, 1)

        @block.gpsimd
        def _(pool):
            pool.wait_ge(s_z.handle, s_z.at(1))
            pool.dma_start(g.XG.rearrange("(n p) d -> p n d", p=P), bcast(g.XN[:, 0, :], 1, NTILE + 2)).then_inc(s_zd.handle, 16)
            pool.wait_ge(s_zd.handle, s_zd.at(16))


def moe_stage(nc, g, dram, rep):
    S = lambda name, each, **kind: g.sem("moe_" + name, each, rep, **kind)
    s_w2 = S("loaded_W2", 64)
    s_rw = S("loaded_router", 16)
    s_stat, s_mv, s_sd, s_rs = S("partial_stats", NT), S("stats", NT), S("deviations", 1), S("reciprocals", 1)
    s_xn, s_save, s_xtp, s_xtc = S("xn_tile", NT), S("xn_saved", NT), S("xnT_in_psum", NT), S("xnT_copied", NT)
    s_lgp, s_lgc = S("logits_in_psum", NT), S("logits_copied", NT)
    s_max, s_idx = S("top_values", NT), S("top_experts", NT)
    s_dve = S("routing_step", MOE_STEPS)
    s_gap, s_exp = S("gap", 1), S("gap_exp", 1)
    s_msk, s_cnt = S("mask", 1), S("counts_in_psum", 1)
    s_pos, s_ei = S("slots", 1), S("tile_experts", 1)
    s_sc = S("rows_scattered", 32 * NT, pool_dma=True)
    s_xs = [S(f"slots_loaded{u}", 16 * (NTILE // 2 + 1)) for u in range(2)]
    s_tap, s_tac = S("slotsT_in_psum", NTILE + 2), S("slotsT_copied", NTILE + 2)
    s_h, s_hs = S("hidden_in_psum", NTILE), S("hidden", NTILE)
    s_thp, s_thc = S("hiddenT_in_psum", NTILE), S("hiddenT_copied", NTILE)
    s_y, s_yc = S("expert_out_in_psum", NTILE), S("expert_out_copied", NTILE)
    s_yd = S("expert_out_stored", 16 * NTILE)
    NQ = 4
    s_ga = [S(f"rows_gathered{q}", 32 * NT // NQ, pool_dma=True) for q in range(NQ)]
    s_add = S("first_added", NT)

    with ExitStack() as ctx:
        sb = lambda name, shape, dt=F32: g.sb(ctx, f"moe{rep}_{name}", shape, dt)
        W2 = sb("W2", [P, NE, KF, D])
        RW = sb("RW", [P, KD, NE])
        XNS = sb("XNS", [P, 2, D])
        XT = sb("XT", [P, 2, KD, P])
        LG = sb("LG", [P, NT, NE])
        M8 = sb("M8", [P, NT, 8])
        I8 = sb("I8", [P, NT, 8], U32)
        IF = sb("IF", [P, NT, 8])
        OH = sb("OH", [P, 2, NT, NE])
        MK = sb("MK", [P, NT, NE])
        EXC = sb("EXC", [P, NT + 1, NE])
        NI = sb("NI", [P, NE], I32)
        NI2 = sb("NI2", [P, NE], I32)
        TE = sb("TE", [P, NE])
        TI = sb("TI", [P, NE + 1])
        BS = sb("BS", [P, NE])
        PB = sb("PB", [P, NT, NE])
        PT = sb("PT", [P, 2, NT, NE])
        PF = sb("PF", [P, 2, NT])
        PI = sb("PI", [P, 2, NT], I32)
        CM = sb("CM", [1, NTILE, NE])
        EF = sb("EF", [1, NTILE])
        EC = sb("EC", [1, NTILE])
        EI = sb("EI", [1, NTILE], I32)
        GP = sb("GP", [P, NT])
        GE = sb("GE", [P, NT])
        GS = sb("GS", [P, NT])
        GH = sb("GH", [P, 2, NT])
        GR = sb("GR", [P, NT])
        XS = sb("XS", [P, 2, D])
        ST = sb("ST", [P, 2, KD, P])
        HS = sb("HS", [P, 2, FF])
        HT = sb("HT", [P, 2, KF, P])
        YS = sb("YS", [P, 2, D])
        Y2 = sb("Y2", [P, 8, D])
        bank = g.bank

        with nc.Block() as block:
            @block.sync
            def _(sp):
                g.credit(sp)
                sp.dma_start(RW[:, :, :], dram["router_w"]).then_inc(s_rw.handle, 16)
                for e in range(0, NE, 4):
                    sp.dma_start(W2[:, e:e + 4], dram["W2"][:, e:e + 4]).then_inc(s_w2.handle, 16)
                sp.wait_ge(s_sc.handle, s_sc.at(32 * NT))
                for u in range(2):
                    sp.dma_start(XS[:, u, :], g.XG[u * P:(u + 1) * P, :]).then_inc(s_xs[u].handle, 16)
                with sp.Fori(0, NTILE // 2) as i:
                    for u in range(2):
                        sp.wait_ge(s_tap.handle, s_tap.at(2 * i + u + 1))
                        sp.dma_start(XS[:, u, :], g.XG[bass.ds((2 * i + u + 2) * P, P), :]).then_inc(s_xs[u].handle, 16)

            @block.vector
            def _(dve):
                norm_stats_dve(dve, g, s_stat, s_mv)
                norm_rs_dve(dve, g, s_sd, s_rs)
                with dve.Fori(0, NT // 2) as i:
                    for u in range(2):
                        dve.wait_ge(s_xtp.handle, s_xtp.at(2 * i))
                        dve.wait_ge(s_save.handle, s_save.at(2 * i))
                        normalize(dve, g, XNS[:, u, :], 2 * i + u).then_inc(s_xn.handle, 1)

                for t in range(NT):
                    dve.wait_ge(s_lgc.handle, s_lgc.at(t + 1))
                    dve.max(M8[:, t, :], LG[:, t, :]).then_inc(s_max.handle, 1)
                for t in range(NT):
                    dve.wait_ge(s_max.handle, s_max.at(t + 1))
                    dve.max_index(I8[:, t, :], M8[:, t, :], LG[:, t, :]).then_inc(s_idx.handle, 1)
                dve.tensor_tensor(GP[:, :], M8[:, :, 1], M8[:, :, 0], ALU.subtract).then_inc(s_gap.handle, 1)
                dve.wait_ge(s_idx.handle, s_idx.at(NT))
                n = [0]

                def then_wait(ins):
                    n[0] += 1
                    ins.then_inc(s_dve.handle, 1)
                    dve.wait_ge(s_dve.handle, s_dve.at(n[0]))

                then_wait(dve.tensor_copy(IF[:, :, :], I8[:, :, :]))
                iota = bcast(g.C[:, C_IOTA:C_IOTA + NE], 1, NT)
                for k in range(2):
                    ins = dve.tensor_tensor(OH[:, k], iota, bcast(IF[:, :, k], 2, NE), ALU.is_equal)
                    then_wait(ins)
                dve.tensor_tensor(MK[:, :, :], OH[:, 0], OH[:, 1], ALU.add).then_inc(s_msk.handle, 1)
                then_wait(dve.memset(EXC[:, 0, :], 0.0))
                dve.wait_ge(s_cnt.handle, s_cnt.at(1))
                with dve.Fori(0, NT) as t:
                    dve.wait_ge(s_dve.handle, s_dve.at(n[0] + t))
                    dve.tensor_tensor(EXC[:, t + 1, :], bank(5)[:, bass.ds(t * NE, NE)], EXC[:, t, :],
                                      ALU.add).then_inc(s_dve.handle, 1)
                n[0] += NT
                dve.wait_ge(s_dve.handle, s_dve.at(n[0]))
                then_wait(dve.tensor_scalar(NI[:, :], EXC[:, NT, :], float(P - 1), None, ALU.add))
                then_wait(dve.tensor_scalar(NI2[:, :], NI[:, :], 7, None, ALU.arith_shift_right))
                then_wait(dve.tensor_copy(TE[:, :], NI2[:, :]))
                then_wait(dve.memset(TI[:, 0:1], 0.0))
                with dve.Fori(0, NE) as e:
                    dve.wait_ge(s_dve.handle, s_dve.at(n[0] + e))
                    dve.tensor_tensor(TI[:, bass.ds(e + 1, 1)], TI[:, bass.ds(e, 1)], TE[:, bass.ds(e, 1)],
                                      ALU.add).then_inc(s_dve.handle, 1)
                n[0] += NE
                dve.wait_ge(s_dve.handle, s_dve.at(n[0]))
                then_wait(dve.tensor_scalar(BS[:, :], TI[:, 0:NE], float(P), None, ALU.mult))
                then_wait(dve.tensor_tensor(PB[:, :, :], EXC[:, 0:NT, :], bcast(BS[:, :], 1, NT), ALU.add))
                then_wait(dve.tensor_tensor(MK[:, :, :], bank(4)[:, 0:NT * NE].rearrange("p (t e) -> p t e", e=NE),
                                            PB[:, :, :], ALU.add))
                for k in range(2):
                    then_wait(dve.tensor_tensor(PT[:, k], OH[:, k], MK[:, :, :], ALU.mult))
                    then_wait(dve.tensor_reduce(PF[:, k, :], PT[:, k], AX_X, ALU.add))
                dve.tensor_copy(PI[:, :, :], PF[:, :, :]).then_inc(s_pos.handle, 1)
                then_wait(dve.tensor_tensor(CM[:, :, :], bcast(TI[0:1, 1:NE + 1], 1, NTILE),
                                            bcast(g.C[0:1, C_TILE:C_TILE + NTILE], 2, NE), ALU.is_le))
                then_wait(dve.tensor_reduce(EF[:, :], CM[:, :, :], AX_X, ALU.add))
                then_wait(dve.tensor_scalar(EC[:, :], EF[:, :], float(NE - 1), None, ALU.min))
                dve.tensor_copy(EI[:, :], EC[:, :]).then_inc(s_ei.handle, 1)
                dve.wait_ge(s_exp.handle, s_exp.at(1))
                then_wait(dve.tensor_scalar(GS[:, :], GE[:, :], 1.0, None, ALU.add))
                then_wait(dve.reciprocal(GR[:, :], GS[:, :]))
                then_wait(dve.tensor_scalar(GH[:, 0, :], GR[:, :], 0.5, None, ALU.mult))
                then_wait(dve.tensor_tensor(GH[:, 1, :], GH[:, 0, :], GE[:, :], ALU.mult))
                assert n[0] == MOE_STEPS

                for u in range(2):
                    dve.wait_ge(s_tap.handle, s_tap.at(u + 1))
                    dve.tensor_copy(ST[:, u], bank(u)[:, 0:KD * P].rearrange("p (k s) -> p k s", s=P)).then_inc(s_tac.handle, 1)
                with dve.Fori(0, NTILE // 2) as i:
                    for u in range(2):
                        dve.wait_ge(s_thp.handle, s_thp.at(2 * i + u + 1))
                        dve.wait_ge(s_y.handle, s_y.at(2 * i))
                        dve.tensor_copy(HT[:, u], bank(4 + u)[:, :].rearrange("p (k s) -> p k s", s=P)).then_inc(s_thc.handle, 1)
                    for u in range(2):
                        dve.wait_ge(s_tap.handle, s_tap.at(2 * i + u + 3))
                        dve.wait_ge(s_h.handle, s_h.at(2 * i + u + 1))
                        dve.tensor_copy(ST[:, u], bank(u)[:, 0:KD * P].rearrange("p (k s) -> p k s", s=P)).then_inc(s_tac.handle, 1)
                per = NT // NQ
                for q in range(NQ):
                    dve.wait_ge(s_ga[q].handle, s_ga[q].at(32 * per))
                    with dve.Fori(q * per, (q + 1) * per) as t:
                        dve.scalar_tensor_tensor(g.X[:, t, :], g.XN[:, t, :], GH[:, 0, bass.ds(t, 1)], g.X[:, t, :],
                                                 ALU.mult, ALU.add).then_inc(s_add.handle, 1)
                    with dve.Fori(q * per, (q + 1) * per) as t:
                        dve.wait_ge(s_add.handle, s_add.at(t + 1))
                        ins = dve.scalar_tensor_tensor(g.X[:, t, :], Y2[:, t - (q // 2) * 2 * per, :], GH[:, 1, bass.ds(t, 1)],
                                                       g.X[:, t, :], ALU.mult, ALU.add)
                        ins.then_inc(g.s_second[rep].handle, 1)

            @block.scalar
            def _(act):
                norm_sd_act(act, g, s_mv, s_sd)
                with act.Fori(0, NT // 2) as i:
                    for u in range(2):
                        act.wait_ge(s_xn.handle, s_xn.at(2 * i + u + 1))
                        act.copy(g.XN[:, 2 * i + u, :], XNS[:, u, :]).then_inc(s_save.handle, 1)
                        act.wait_ge(s_xtp.handle, s_xtp.at(2 * i + u + 1))
                        act.wait_ge(s_lgp.handle, s_lgp.at(2 * i))
                        act.copy(XT[:, u], bank(u)[:, 0:KD * P].rearrange("p (k s) -> p k s", s=P)).then_inc(s_xtc.handle, 1)
                    for u in range(2):
                        act.wait_ge(s_lgp.handle, s_lgp.at(2 * i + u + 1))
                        act.copy(LG[:, 2 * i + u, :], bank(2 + u)[:, 0:NE]).then_inc(s_lgc.handle, 1)
                nc.scalar.preload_act_table(ACT.Exp)
                act.wait_ge(s_gap.handle, s_gap.at(1))
                act.activation(GE[:, :], GP[:, :], ACT.Exp).then_inc(s_exp.handle, 1)
                nc.scalar.preload_act_table(ACT.Silu)
                with act.Fori(0, NTILE // 2) as i:
                    for u in range(2):
                        act.wait_ge(s_h.handle, s_h.at(2 * i + u + 1))
                        act.wait_ge(s_thp.handle, s_thp.at(2 * i))
                        act.activation(HS[:, u, :], bank(2 + u)[:, :], ACT.Silu).then_inc(s_hs.handle, 1)
                    for u in range(2):
                        act.wait_ge(s_y.handle, s_y.at(2 * i + u + 1))
                        act.wait_ge(s_yd.handle, s_yd.at(32 * i))
                        act.copy(YS[:, u, :], bank(6 + u)[:, 0:D]).then_inc(s_yc.handle, 1)
                        act.wait_ge(s_yc.handle, s_yc.at(2 * i + u + 1))
                        act.dma_start(g.YG[bass.ds((2 * i + u) * P, P), :], YS[:, u, :]).then_inc(s_yd.handle, 16)

            @block.tensor
            def _(pe):
                ident = g.C[:, C_ID:C_ID + P]
                pe.wait_ge(s_rw.handle, s_rw.at(16))
                with pe.Fori(0, NT // 2) as i:
                    for u in range(2):
                        pe.wait_ge(s_xn.handle, s_xn.at(2 * i + u + 1))
                        pe.wait_ge(s_xtc.handle, s_xtc.at(2 * i))
                        for k in range(KD):
                            ins = pe.transpose(bank(u)[:, k * P:(k + 1) * P], XNS[:, u, k * P:(k + 1) * P], ident)
                        ins.then_inc(s_xtp.handle, 1)
                    for u in range(2):
                        pe.wait_ge(s_xtc.handle, s_xtc.at(2 * i + u + 1))
                        pe.wait_ge(s_lgc.handle, s_lgc.at(2 * i))
                        for k in range(KD):
                            ins = pe.matmul(bank(2 + u)[:, 0:NE], XT[:, u, k, :], RW[:, k, :], start=(k == 0), stop=(k == KD - 1))
                        ins.then_inc(s_lgp.handle, 1)
                pe.wait_ge(s_msk.handle, s_msk.at(1))
                mask = MK[:, :, :].rearrange("p t e -> p (t e)")
                pe.matmul(bank(4)[:, 0:NT * NE], g.C[:, C_TRI:C_TRI + P], mask, start=True, stop=True)
                pe.matmul(bank(5)[:, 0:NT * NE], g.C[:, C_ONE:C_ONE + P], mask, start=True, stop=True).then_inc(s_cnt.handle, 1)

                pe.wait_ge(g.s_w1.handle, g.s_w1.at(64))
                pe.wait_ge(s_w2.handle, s_w2.at(64))
                pe.wait_ge(s_ei.handle, s_ei.at(1))

                def slots_t(u, j, loads):
                    pe.wait_ge(s_xs[u].handle, s_xs[u].at(16 * loads))
                    for k in range(KD):
                        ins = pe.transpose(bank(u)[:, k * P:(k + 1) * P], XS[:, u, k * P:(k + 1) * P], ident)
                    ins.then_inc(s_tap.handle, 1)

                slots_t(0, 0, 1)
                slots_t(1, 1, 1)
                with pe.Fori(0, NTILE // 2) as i:
                    experts = [pe.value_load(EI[0:1, bass.ds(2 * i + u, 1)], min_val=0, max_val=NE - 1) for u in range(2)]
                    for u in range(2):
                        pe.wait_ge(s_tac.handle, s_tac.at(2 * i + u + 1))
                        pe.wait_ge(s_hs.handle, s_hs.at(2 * i))
                        for k in range(KD):
                            ins = pe.matmul(bank(2 + u)[:, :], ST[:, u, k, :], g.W1[:, experts[u], k, :], start=(k == 0), stop=(k == KD - 1))
                        ins.then_inc(s_h.handle, 1)
                    for u in range(2):
                        pe.wait_ge(s_hs.handle, s_hs.at(2 * i + u + 1))
                        pe.wait_ge(s_thc.handle, s_thc.at(2 * i))
                        for k in range(KF):
                            ins = pe.transpose(bank(4 + u)[:, k * P:(k + 1) * P], HS[:, u, k * P:(k + 1) * P], ident)
                        ins.then_inc(s_thp.handle, 1)
                    for u in range(2):
                        slots_t(u, 2 * i + u + 2, i + 2)
                    for u in range(2):
                        pe.wait_ge(s_thc.handle, s_thc.at(2 * i + u + 1))
                        pe.wait_ge(s_yc.handle, s_yc.at(2 * i))
                        for k in range(KF):
                            ins = pe.matmul(bank(6 + u)[:, 0:D], HT[:, u, k, :], W2[:, experts[u], k, :], start=(k == 0), stop=(k == KF - 1))
                        ins.then_inc(s_y.handle, 1)

            @block.gpsimd
            def _(pool):
                pool.wait_ge(s_pos.handle, s_pos.at(1))
                pool.wait_ge(s_save.handle, s_save.at(NT))
                for t in range(NT):
                    for k in range(2):
                        pool.indirect_dma_start(g.XG, bass.IndirectOffsetOnAxis(PI[:, k, t:t + 1], 0),
                                                g.XN[:, t, :], None).then_inc(s_sc.handle, 16)
                pool.wait_ge(s_yd.handle, s_yd.at(16 * NTILE))
                per = NT // NQ
                for t in range(NT):
                    if t >= NT // 2:
                        pool.wait_ge(g.s_second[rep].handle, g.s_second[rep].at(t - NT // 2 + 1))
                    q = t // per
                    pool.indirect_dma_start(g.XN[:, t, :], None, g.YG, bass.IndirectOffsetOnAxis(PI[:, 0, t:t + 1], 0)).then_inc(s_ga[q].handle, 16)
                    pool.indirect_dma_start(Y2[:, t % 8, :], None, g.YG, bass.IndirectOffsetOnAxis(PI[:, 1, t:t + 1], 0)).then_inc(s_ga[q].handle, 16)


def attention_stage(nc, g, dram):
    S = lambda name: g.sem("att_" + name)
    s_w, s_fill = S("weights"), S("filled")
    s_stat, s_mv, s_sd, s_rs = (g.sem("att_" + n) for n in ("partial_stats", "stats", "deviations", "reciprocals"))
    s_xn, s_xtp, s_xtc = S("xn_tile"), S("xnT_in_psum"), S("xnT_copied")
    s_pr, s_hi, s_rows = S("qkv_in_psum"), S("high_parts"), S("low_parts")
    s_qkp, s_qc, s_kc = S("qkT_in_psum"), S("qT_copied"), S("kT_copied")
    s_cs, s_suf = S("tile_sums_in_psum"), S("later_sums")
    s_sc, s_mask, s_mx, s_nb = S("scores"), S("masked"), S("row_max"), S("negative_max")
    s_p, s_e0 = S("probs"), S("later_weight")
    s_ptp, s_ptc = S("probsT_in_psum"), S("probsT_copied")
    s_ot, s_otc, s_bt = S("outT_in_psum"), S("outT_copied"), S("out_in_psum")
    s_f = [S(n) for n in ("later_part", "out_sum", "out_denominator", "out_rows")]
    s_aop, s_aoc, s_wo, s_x = S("outrowsT_in_psum"), S("outrowsT_copied"), S("projected"), S("x_updated")

    NU = TB * HG
    chunks = []
    for n in range(NU):
        nk = n // HG + 1
        chunks += [(n, c, min(4, nk - c)) for c in range(0, nk, 4)]
    NC = len(chunks)
    first_chunk = [next(c for c, ch in enumerate(chunks) if ch[0] == n) for n in range(NU)] + [NC]

    with ExitStack() as ctx:
        sb = lambda name, shape, dt=F32: g.sb(ctx, "att_" + name, shape, dt)
        WQ = sb("Wqkv", [P, KD, NG0 * 3 * HG * DH0])
        WO = sb("Wo", [P, KD, D])
        XNS = sb("XNS", [P, 2, D])
        XT = sb("XT", [P, KD, SEQ])
        QS = sb("QS", [P, 2, HG * 64])
        KS = sb("KS", [P, 2, HG * 64])
        QT = sb("QT", [P, 2, 2, SEQ], F32R)
        KT = sb("KT", [P, 2, SEQ], F32R)
        VV = sb("VV", [P, TB, HG * VW])
        SF = sb("SF", [P, TB, HG * VW])
        PR = sb("PR", [P, 2, SEQ])
        PT = sb("PT", [P, 2, HG, TB, P])
        MX = sb("MX", [P, NU])
        NB = sb("NB", [P, NU])
        E0 = sb("E0", [P, 2, HG])
        OT = sb("OT", [P, P])
        F1 = sb("F1", [P, HG * VW])
        F2 = sb("F2", [P, HG * VW])
        F3 = sb("F3", [P, HG])
        AO = sb("AO", [P, TB, D])
        AT = sb("AT", [P, 2, KD, P])
        bank, banks = g.bank, g.banks
        ident = g.C[:, C_ID:C_ID + P]
        sc_bank = lambda n: 2 * (n % 2)
        scores = lambda n, w: banks(sc_bank(n), 2)[:, 0:w]
        slots = lambda rows, j: rows[:, j % 2, :].rearrange("p (h s d) -> p h s d", h=HG, s=4)
        part = lambda j, m: bank(j % 2)[:, m * 64:(m + 1) * 64].rearrange("p (h d) -> p h d", h=HG)
        v4 = lambda ap: ap.rearrange("p (h d) -> p h d", h=HG)

        with nc.Block() as block:
            @block.sync
            def _(sp):
                g.credit(sp)
                sp.dma_start(WQ[:, :, :], dram["Wqkv"]).then_inc(s_w.handle, 16)
                sp.dma_start(WO[:, :, :], dram["Wo"]).then_inc(s_w.handle, 16)
                sp.wait_ge(s_w.handle, s_w.at(32))

            @block.gpsimd
            def _(pool):
                pool.memset(QT[:, :, :, :].bitcast(F32), 0.0).then_inc(s_fill.handle, 1)
                pool.memset(VV[:, :, :], 0.0).then_inc(s_fill.handle, 1)
                pool.wait_ge(s_fill.handle, s_fill.at(2))
                pool.memset(VV[:, :, :].rearrange("p j (h d) -> p (j h) d", d=VW)[:, :, DH0:DH0 + 1], 1.0).then_inc(s_fill.handle, 1)

            @block.tensor
            def _(pe):
                pe.wait_ge(s_w.handle, s_w.at(32))
                pe.wait_ge(s_fill.handle, s_fill.at(3))
                with pe.Fori(0, BATCH) as b:
                    for j in range(TB):
                        pe.wait_ge(s_xn.handle, s_xn.at(TB * b + j + 1))
                        if j >= 2:
                            pe.wait_ge(s_xtc.handle, s_xtc.at(TB * b + j - 1))
                        for k in range(KD):
                            ins = pe.transpose(bank(j % 2)[:, k * P:(k + 1) * P], XNS[:, j % 2, k * P:(k + 1) * P], ident)
                        ins.then_inc(s_xtp.handle, 1)
                    with pe.Fori(0, NG0) as gg:
                        it = b * NG0 + gg
                        pe.wait_ge(s_xtc.handle, s_xtc.at(TB * b + TB))

                        def qk_transposes(j):
                            pe.wait_ge(s_rows.handle, s_rows.at(2 * (TB * it + j + 1)))
                            if j >= 2:
                                pe.wait_ge(s_qc.handle, s_qc.at(2 * (TB * it + j - 1)))
                                pe.wait_ge(s_kc.handle, s_kc.at(TB * it + j - 1))
                            for r in range(2):
                                pe.transpose(bank(2 + j % 2)[:, r * P:(r + 1) * P], QS[:, j % 2, r * P:(r + 1) * P], ident)
                            for r in range(2):
                                ins = pe.transpose(bank(4 + j % 2)[:, r * P:(r + 1) * P], KS[:, j % 2, r * P:(r + 1) * P], ident)
                            ins.then_inc(s_qkp.handle, 1)

                        for j in range(TB):
                            if j >= 2:
                                pe.wait_ge(s_rows.handle, s_rows.at(2 * (TB * it + j - 1)))
                            for k in range(KD):
                                ins = pe.matmul(bank(j % 2)[:, 0:3 * HG * DH0], XT[:, k, j * P:(j + 1) * P],
                                                WQ[:, k, bass.ds(gg * (3 * HG * DH0), 3 * HG * DH0)], start=(k == 0), stop=(k == KD - 1))
                            ins.then_inc(s_pr.handle, 1)
                            if j:
                                qk_transposes(j - 1)
                        qk_transposes(TB - 1)
                        for m in range(2):
                            ins = pe.matmul(bank(6 + m)[:, :], g.C[:, C_ONE:C_ONE + P],
                                            VV[:, 4 * m:4 * m + 4, :].rearrange("p j c -> p (j c)"), start=True, stop=True)
                        ins.then_inc(s_cs.handle, 1)
                        pe.wait_ge(s_qc.handle, s_qc.at(2 * TB * (it + 1)))
                        pe.wait_ge(s_kc.handle, s_kc.at(TB * (it + 1)))

                        def scores_of(n):
                            i, h = n // HG, n % HG
                            if n >= 2:
                                pe.wait_ge(s_p.handle, s_p.at(NU * it + n - 1))
                            width = (i // 2 + 1) * 2 * P
                            for c in range(0, width, 512):
                                w = min(512, width - c)
                                ins = pe.matmul(bank(sc_bank(n) + c // 512)[:, 0:w], QT[:, h // 2, h % 2, i * P:(i + 1) * P],
                                                KT[:, h // 2, c:c + w], start=True, stop=True)
                            ins.then_inc(s_sc.handle, 1)

                        def transposes_of(n):
                            pe.wait_ge(s_p.handle, s_p.at(NU * it + n + 1))
                            for c in range(first_chunk[n], first_chunk[n + 1]):
                                _, k0, nk = chunks[c]
                                if c >= 2:
                                    pe.wait_ge(s_ptc.handle, s_ptc.at(NC * it + c - 1))
                                for k in range(nk):
                                    ins = pe.transpose(bank(4 + c % 2)[:, k * P:(k + 1) * P], PR[:, n % 2, (k0 + k) * P:(k0 + k + 1) * P], ident)
                                ins.then_inc(s_ptp.handle, 1)

                        def values_of(i):
                            pe.wait_ge(s_ptc.handle, s_ptc.at(NC * it + first_chunk[HG * (i + 1)]))
                            if i:
                                pe.wait_ge(s_otc.handle, s_otc.at(TB * it + i))
                            else:
                                pe.wait_ge(s_suf.handle, s_suf.at(TB * (it + 1)))
                            for k in range(i + 1):
                                for h in range(HG):
                                    ins = pe.matmul(bank(6)[h * VW:(h + 1) * VW, 0:P], VV[:, k, h * VW:(h + 1) * VW],
                                                    PT[:, i % 2, h, k, :], start=(k == 0), stop=(k == i))
                            ins.then_inc(s_ot.handle, 1)

                        def out_rows_of(i):
                            pe.wait_ge(s_otc.handle, s_otc.at(TB * it + i + 1))
                            if i:
                                pe.wait_ge(s_f[1].handle, s_f[1].at(TB * it + i))
                            pe.transpose(bank(7)[:, 0:P], OT[:, :], ident).then_inc(s_bt.handle, 1)

                        scores_of(0)
                        for n in range(NU):
                            if n + 1 < NU:
                                scores_of(n + 1)
                            transposes_of(n)
                            if n >= HG and n % HG == 0:
                                values_of(n // HG - 1)
                            if n >= HG and n % HG == 3:
                                out_rows_of(n // HG - 1)
                        values_of(TB - 1)
                        out_rows_of(TB - 1)
                    for i in range(TB):
                        pe.wait_ge(s_f[3].handle, s_f[3].at(TB * NG0 * (b + 1)))
                        if i >= 2:
                            pe.wait_ge(s_aoc.handle, s_aoc.at(TB * b + i - 1))
                        for k in range(KD):
                            ins = pe.transpose(bank(4 + i % 2)[:, k * P:(k + 1) * P], AO[:, i, k * P:(k + 1) * P], ident)
                        ins.then_inc(s_aop.handle, 1)
                        pe.wait_ge(s_aoc.handle, s_aoc.at(TB * b + i + 1))
                        if i >= 2:
                            pe.wait_ge(s_x.handle, s_x.at(TB * b + i - 1))
                        for k in range(KD):
                            ins = pe.matmul(bank(i % 2)[:, 0:D], AT[:, i % 2, k, :], WO[:, k, :], start=(k == 0), stop=(k == KD - 1))
                        ins.then_inc(s_wo.handle, 1)
                    pe.wait_ge(s_x.handle, s_x.at(TB * (b + 1)))

            @block.scalar
            def _(act):
                norm_sd_act(act, g, s_mv, s_sd)
                act.wait_ge(s_fill.handle, s_fill.at(3))
                with act.Fori(0, BATCH) as b:
                    for j in range(TB):
                        act.wait_ge(s_xtp.handle, s_xtp.at(TB * b + j + 1))
                        act.copy(XT[:, :, j * P:(j + 1) * P], bank(j % 2)[:, 0:KD * P].rearrange("p (k s) -> p k s", s=P)).then_inc(s_xtc.handle, 1)
                    with act.Fori(0, NG0) as gg:
                        it = b * NG0 + gg

                        def q_copies(j):
                            act.wait_ge(s_qkp.handle, s_qkp.at(TB * it + j + 1))
                            for m in range(2):
                                act.copy(QT[m * 64:(m + 1) * 64, :, m, j * P:(j + 1) * P],
                                         bank(2 + j % 2)[m * 64:(m + 1) * 64, 0:2 * P].rearrange("p (r s) -> p r s", r=2)).then_inc(s_qc.handle, 1)

                        for j in range(TB):
                            act.wait_ge(s_pr.handle, s_pr.at(TB * it + j + 1))
                            if j >= 2:
                                act.wait_ge(s_qkp.handle, s_qkp.at(TB * it + j - 1))
                            act.copy(slots(QS, j)[:, :, 0:4:2, :].bitcast(F32R), bcast(part(j, 0), 2, 2)).then_inc(s_hi.handle, 1)
                            act.copy(slots(KS, j)[:, :, 0:2, :].bitcast(F32R), bcast(part(j, 1), 2, 2)).then_inc(s_hi.handle, 1)
                            if j == 0:
                                act.wait_ge(s_bt.handle, s_bt.at(TB * it))
                            act.copy(v4(VV[:, j, :])[:, :, 0:DH0], part(j, 2)).then_inc(s_hi.handle, 1)
                            if j:
                                q_copies(j - 1)
                        q_copies(TB - 1)

                        def copies_of(n):
                            for c in range(first_chunk[n], first_chunk[n + 1]):
                                _, k0, nk = chunks[c]
                                i, h = n // HG, n % HG
                                act.wait_ge(s_ptp.handle, s_ptp.at(NC * it + c + 1))
                                if i >= 2 and n % HG == 0 and k0 == 0:
                                    act.wait_ge(s_ot.handle, s_ot.at(TB * it + i - 1))
                                act.copy(PT[:, i % 2, h, k0:k0 + nk, :], bank(4 + c % 2)[:, 0:nk * P].rearrange("p (k s) -> p k s", s=P)).then_inc(s_ptc.handle, 1)

                        for n in range(NU):
                            i, w = n // HG, (n // HG + 1) * P
                            act.wait_ge(s_nb.handle, s_nb.at(NU * it + n + 1))
                            if n >= 2:
                                act.wait_ge(s_ptp.handle, s_ptp.at(NC * it + first_chunk[n - 1]))
                            act.activation(PR[:, n % 2, 0:w], scores(n, w), ACT.Exp, bias=NB[:, n:n + 1], scale=SEQ ** -0.5).then_inc(s_p.handle, 1)
                            if n % HG == 3:
                                if i >= 2:
                                    act.wait_ge(s_f[0].handle, s_f[0].at((TB - 1) * it + i - 1))
                                act.activation(E0[:, i % 2, :], NB[:, HG * i:HG * i + HG], ACT.Exp).then_inc(s_e0.handle, 1)
                            if n:
                                copies_of(n - 1)
                        copies_of(NU - 1)
                    for i in range(TB):
                        act.wait_ge(s_aop.handle, s_aop.at(TB * b + i + 1))
                        if i >= 2:
                            act.wait_ge(s_wo.handle, s_wo.at(TB * b + i - 1))
                        act.copy(AT[:, i % 2], bank(4 + i % 2)[:, 0:KD * P].rearrange("p (k s) -> p k s", s=P)).then_inc(s_aoc.handle, 1)

            @block.vector
            def _(dve):
                norm_stats_dve(dve, g, s_stat, s_mv)
                norm_rs_dve(dve, g, s_sd, s_rs)
                with dve.Fori(0, BATCH) as b:
                    for j in range(TB):
                        if j >= 2:
                            dve.wait_ge(s_xtp.handle, s_xtp.at(TB * b + j - 1))
                        normalize(dve, g, XNS[:, j % 2, :], b * TB + j).then_inc(s_xn.handle, 1)
                    with dve.Fori(0, NG0) as gg:
                        it = b * NG0 + gg

                        def k_copy(j):
                            dve.wait_ge(s_qkp.handle, s_qkp.at(TB * it + j + 1))
                            dve.tensor_copy(KT[:, :, j * P:(j + 1) * P], bank(4 + j % 2)[:, 0:2 * P].rearrange("p (r s) -> p r s", r=2)).then_inc(s_kc.handle, 1)

                        for j in range(TB):
                            dve.wait_ge(s_hi.handle, s_hi.at(3 * (TB * it + j + 1)))
                            qs, ks = slots(QS, j), slots(KS, j)
                            dve.tensor_tensor(qs[:, :, 1:4:2, :], bcast(part(j, 0), 2, 2), qs[:, :, 0:4:2, :], ALU.subtract).then_inc(s_rows.handle, 1)
                            dve.tensor_tensor(ks[:, :, 2:4, :], bcast(part(j, 1), 2, 2), ks[:, :, 0:2, :], ALU.subtract).then_inc(s_rows.handle, 1)
                            if j:
                                k_copy(j - 1)
                        k_copy(TB - 1)
                        dve.wait_ge(s_cs.handle, s_cs.at(it + 1))
                        dve.wait_ge(s_f[0].handle, s_f[0].at((TB - 1) * it))
                        dve.memset(SF[:, TB - 1, :], 0.0).then_inc(s_suf.handle, 1)
                        for i in range(TB - 2, -1, -1):
                            dve.wait_ge(s_suf.handle, s_suf.at(TB * it + TB - 1 - i))
                            dve.tensor_tensor(SF[:, i, :], bank(6 + (i + 1) // 4)[:, (i + 1) % 4 * P:((i + 1) % 4 + 1) * P], SF[:, i + 1, :],
                                              ALU.add).then_inc(s_suf.handle, 1)
                        dve.wait_ge(s_suf.handle, s_suf.at(TB * (it + 1)))

                        def finish(i):
                            dve.wait_ge(s_bt.handle, s_bt.at(TB * it + i + 1))
                            if i < TB - 1:
                                dve.wait_ge(s_e0.handle, s_e0.at(TB * it + i + 1))
                                dve.tensor_tensor(v4(F1[:, :]), v4(SF[:, i, :]), bcast(E0[:, i % 2, :], 2, VW), ALU.mult).then_inc(s_f[0].handle, 1)
                                dve.wait_ge(s_f[0].handle, s_f[0].at((TB - 1) * it + i + 1))
                                dve.tensor_tensor(F2[:, :], bank(7)[:, 0:P], F1[:, :], ALU.add).then_inc(s_f[1].handle, 1)
                            else:
                                dve.tensor_copy(F2[:, :], bank(7)[:, 0:P]).then_inc(s_f[1].handle, 1)
                            dve.wait_ge(s_f[1].handle, s_f[1].at(TB * it + i + 1))
                            dve.reciprocal(F3[:, :], v4(F2[:, :])[:, :, DH0]).then_inc(s_f[2].handle, 1)
                            dve.wait_ge(s_f[2].handle, s_f[2].at(TB * it + i + 1))
                            out = AO[:, i, bass.ds(gg * (HG * DH0), HG * DH0)]
                            dve.tensor_tensor(v4(out), v4(F2[:, :])[:, :, 0:DH0], bcast(F3[:, :], 2, DH0), ALU.mult).then_inc(s_f[3].handle, 1)

                        def out_copy(i):
                            dve.wait_ge(s_ot.handle, s_ot.at(TB * it + i + 1))
                            if i:
                                dve.wait_ge(s_bt.handle, s_bt.at(TB * it + i))
                            dve.tensor_copy(OT[:, :], bank(6)[:, 0:P]).then_inc(s_otc.handle, 1)

                        for n in range(NU):
                            i, h = n // HG, n % HG
                            w = (i + 1) * P
                            dve.wait_ge(s_sc.handle, s_sc.at(NU * it + n + 1))
                            diag = scores(n, w)[:, i * P:w]
                            dve.tensor_tensor(diag, diag, g.C[:, C_LOW:C_LOW + P], ALU.mult).then_inc(s_mask.handle, 1)
                            dve.wait_ge(s_mask.handle, s_mask.at(NU * it + n + 1))
                            dve.tensor_reduce(MX[:, n:n + 1], scores(n, w), AX_X, ALU.max).then_inc(s_mx.handle, 1)
                            dve.wait_ge(s_mx.handle, s_mx.at(NU * it + n + 1))
                            if i < TB - 1:
                                ins = dve.tensor_scalar(NB[:, n:n + 1], MX[:, n:n + 1], 0.0, -(SEQ ** -0.5), ALU.max, ALU.mult)
                            else:
                                ins = dve.tensor_scalar(NB[:, n:n + 1], MX[:, n:n + 1], -(SEQ ** -0.5), None, ALU.mult)
                            ins.then_inc(s_nb.handle, 1)
                            if n >= HG and n % HG == 2:
                                out_copy(n // HG - 1)
                            if n >= 2 * HG and n % HG == 0:
                                finish(n // HG - 2)
                        finish(TB - 2)
                        out_copy(TB - 1)
                        finish(TB - 1)
                    for i in range(TB):
                        dve.wait_ge(s_wo.handle, s_wo.at(TB * b + i + 1))
                        xt = g.X[:, b * TB + i, :]
                        dve.tensor_tensor(xt, bank(i % 2)[:, 0:D], xt, ALU.add).then_inc(s_x.handle, 1)


def lora_stage(nc, g, dram, rep):
    S = lambda name, each: g.sem("lora_" + name, each, rep)
    s_w = S("weights", 64)
    s_stat, s_mv, s_sd, s_rs = S("partial_stats", NT), S("stats", NT), S("deviations", 1), S("reciprocals", 1)
    s_xn, s_xtp, s_xtc = S("xn_tile", NT), S("xnT_in_psum", NT), S("xnT_copied", NT)
    s_pr, s_mid, s_lg, s_b1, s_b2 = S("projected", NT), S("mids_copied", NT), S("logits", NT), S("biased", NT), S("base_added", NT)
    s_step, s_max, s_idx, s_e = S("routing_step", LORA_STEPS), S("top_probs", NT), S("top_experts", NT), S("exps", 1)
    s_gm, s_mtp, s_mtc, s_lo, s_x = S("gated", NT), S("midsT_in_psum", NT), S("midsT_copied", NT), S("lora_out", NT), S("lora_added", NT)
    NL = LE * LR + LE
    with ExitStack() as ctx:
        sb = lambda name, shape, dt=F32: g.sb(ctx, f"lora{rep}_{name}", shape, dt)
        WB, WL, BL, BI = sb("Wbase", [P, KD, D]), sb("Wlora", [P, KD, NL]), sb("B", [P, D]), sb("biases", [P, D + LE])
        XNS, XT = sb("XNS", [P, 2, D]), sb("XT", [P, 2, KD, P])
        MID, LG, BB = sb("MID", [P, NT, LE * LR]), sb("LG", [P, NT, LE]), sb("BB", [P, 2, D])
        MX, SH, EX, SM, RC, PB = sb("MX", [P, NT]), sb("SH", [P, NT, LE]), sb("EX", [P, NT, LE]), sb("SM", [P, NT]), sb("RC", [P, NT]), sb("PB", [P, NT, LE])
        M8, I8, IF = sb("M8", [P, NT, 8]), sb("I8", [P, NT, 8], U32), sb("IF", [P, NT, 8])
        OH, G1, G2, TS, TR, GT = sb("OH", [P, 2, NT, LE]), sb("G1", [P, NT, LE]), sb("G2", [P, NT, LE]), sb("TS", [P, NT]), sb("TR", [P, NT]), sb("GT", [P, NT, LE])
        GM, MT = sb("GM", [P, 2, LE * LR]), sb("MT", [P, 2, P])
        bank = g.bank
        ident = g.C[:, C_ID:C_ID + P]
        with nc.Block() as block:
            @block.sync
            def _(sp):
                g.credit(sp)
                sp.dma_start(WB[:, :, :], dram["Wbase"]).then_inc(s_w.handle, 16)
                sp.dma_start(WL[:, :, :], dram["Wlora"]).then_inc(s_w.handle, 16)
                sp.dma_start(BL[:, :], dram["Blora"]).then_inc(s_w.handle, 16)
                sp.dma_start(BI[:, :], dram["biases"].to_broadcast([P, D + LE])).then_inc(s_w.handle, 16)
                sp.wait_ge(s_w.handle, s_w.at(64))

            @block.tensor
            def _(pe):
                pe.wait_ge(s_w.handle, s_w.at(64))
                with pe.Fori(0, NT // 2) as i:
                    for u in range(2):
                        pe.wait_ge(s_xn.handle, s_xn.at(2 * i + u + 1))
                        pe.wait_ge(s_xtc.handle, s_xtc.at(2 * i))
                        for k in range(KD):
                            ins = pe.transpose(bank(u)[:, k * P:(k + 1) * P], XNS[:, u, k * P:(k + 1) * P], ident)
                        ins.then_inc(s_xtp.handle, 1)
                    for u in range(2):
                        pe.wait_ge(s_xtc.handle, s_xtc.at(2 * i + u + 1))
                        pe.wait_ge(s_b1.handle, s_b1.at(2 * i))
                        pe.wait_ge(s_lg.handle, s_lg.at(2 * i))
                        for k in range(KD):
                            pe.matmul(bank(2 + u)[:, 0:D], XT[:, u, k, :], WB[:, k, :], start=(k == 0), stop=(k == KD - 1))
                        for k in range(KD):
                            ins = pe.matmul(bank(4 + u)[:, 0:NL], XT[:, u, k, :], WL[:, k, :], start=(k == 0), stop=(k == KD - 1))
                        ins.then_inc(s_pr.handle, 1)
                with pe.Fori(0, NT // 2) as i:
                    for u in range(2):
                        pe.wait_ge(s_gm.handle, s_gm.at(2 * i + u + 1))
                        pe.wait_ge(s_mtc.handle, s_mtc.at(2 * i))
                        pe.transpose(bank(u)[:, 0:P], GM[:, u, :], ident).then_inc(s_mtp.handle, 1)
                    for u in range(2):
                        pe.wait_ge(s_mtc.handle, s_mtc.at(2 * i + u + 1))
                        pe.wait_ge(s_x.handle, s_x.at(2 * i))
                        pe.matmul(bank(2 + u)[:, 0:D], MT[:, u, :], BL[:, :], start=True, stop=True).then_inc(s_lo.handle, 1)

            @block.scalar
            def _(act):
                norm_sd_act(act, g, s_mv, s_sd)
                act.wait_ge(s_w.handle, s_w.at(64))
                with act.Fori(0, NT // 2) as i:
                    for u in range(2):
                        act.wait_ge(s_xtp.handle, s_xtp.at(2 * i + u + 1))
                        act.wait_ge(s_pr.handle, s_pr.at(2 * i))
                        act.copy(XT[:, u], bank(u)[:, 0:KD * P].rearrange("p (k s) -> p k s", s=P)).then_inc(s_xtc.handle, 1)
                    for u in range(2):
                        act.wait_ge(s_pr.handle, s_pr.at(2 * i + u + 1))
                        act.copy(MID[:, 2 * i + u, :], bank(4 + u)[:, 0:LE * LR]).then_inc(s_mid.handle, 1)
                act.wait_ge(s_step.handle, s_step.at(2))
                act.activation(EX[:, :, :], SH[:, :, :], ACT.Exp).then_inc(s_e.handle, 1)
                with act.Fori(0, NT // 2) as i:
                    for u in range(2):
                        act.wait_ge(s_mtp.handle, s_mtp.at(2 * i + u + 1))
                        act.wait_ge(s_lo.handle, s_lo.at(2 * i))
                        act.copy(MT[:, u, :], bank(u)[:, 0:P]).then_inc(s_mtc.handle, 1)

            @block.vector
            def _(dve):
                norm_stats_dve(dve, g, s_stat, s_mv)
                norm_rs_dve(dve, g, s_sd, s_rs)
                dve.wait_ge(s_w.handle, s_w.at(64))
                for u in range(2):
                    normalize(dve, g, XNS[:, u, :], u).then_inc(s_xn.handle, 1)
                def base_outputs(i, more):
                    for u in range(2):
                        dve.wait_ge(s_pr.handle, s_pr.at(2 * i + u + 1))
                        dve.wait_ge(s_mid.handle, s_mid.at(2 * i + u + 1))
                        dve.tensor_tensor(LG[:, 2 * i + u, :], bank(4 + u)[:, LE * LR:NL], BI[:, D:D + LE], ALU.add).then_inc(s_lg.handle, 1)
                        dve.wait_ge(s_b2.handle, s_b2.at(2 * i))
                        dve.tensor_tensor(BB[:, u, :], bank(2 + u)[:, 0:D], BI[:, 0:D], ALU.add).then_inc(s_b1.handle, 1)
                        dve.wait_ge(s_b1.handle, s_b1.at(2 * i + u + 1))
                        dve.scalar_tensor_tensor(g.X[:, 2 * i + u, :], BB[:, u, :], 0.5, g.X[:, 2 * i + u, :],
                                                 ALU.mult, ALU.add).then_inc(s_b2.handle, 1)
                    for u in range(2 if more else 0):
                        normalize(dve, g, XNS[:, u, :], 2 * i + 2 + u).then_inc(s_xn.handle, 1)

                with dve.Fori(0, NT // 2 - 1) as i:
                    base_outputs(i, True)
                base_outputs(NT // 2 - 1, False)
                dve.wait_ge(s_lg.handle, s_lg.at(NT))
                n = [0]

                def then_wait(ins):
                    n[0] += 1
                    ins.then_inc(s_step.handle, 1)
                    dve.wait_ge(s_step.handle, s_step.at(n[0]))

                then_wait(dve.tensor_reduce(MX[:, :], LG[:, :, :], AX_X, ALU.max))
                then_wait(dve.tensor_tensor(SH[:, :, :], LG[:, :, :], bcast(MX[:, :], 2, LE), ALU.subtract))
                dve.wait_ge(s_e.handle, s_e.at(1))
                then_wait(dve.tensor_reduce(SM[:, :], EX[:, :, :], AX_X, ALU.add))
                then_wait(dve.reciprocal(RC[:, :], SM[:, :]))
                then_wait(dve.tensor_tensor(PB[:, :, :], EX[:, :, :], bcast(RC[:, :], 2, LE), ALU.mult))
                for t in range(NT):
                    dve.max(M8[:, t, :], PB[:, t, :]).then_inc(s_max.handle, 1)
                for t in range(NT):
                    dve.wait_ge(s_max.handle, s_max.at(t + 1))
                    dve.max_index(I8[:, t, :], M8[:, t, :], PB[:, t, :]).then_inc(s_idx.handle, 1)
                dve.wait_ge(s_idx.handle, s_idx.at(NT))
                then_wait(dve.tensor_copy(IF[:, :, :], I8[:, :, :]))
                iota = bcast(g.C[:, C_IOTA:C_IOTA + LE], 1, NT)
                for k in range(2):
                    then_wait(dve.tensor_tensor(OH[:, k], iota, bcast(IF[:, :, k], 2, LE), ALU.is_equal))
                then_wait(dve.tensor_tensor(G1[:, :, :], OH[:, 0], bcast(M8[:, :, 0], 2, LE), ALU.mult))
                then_wait(dve.tensor_tensor(G2[:, :, :], OH[:, 1], bcast(M8[:, :, 1], 2, LE), ALU.mult))
                then_wait(dve.tensor_tensor(SH[:, :, :], G1[:, :, :], G2[:, :, :], ALU.add))
                then_wait(dve.tensor_tensor(TS[:, :], M8[:, :, 0], M8[:, :, 1], ALU.add))
                then_wait(dve.reciprocal(TR[:, :], TS[:, :]))
                then_wait(dve.tensor_tensor(GT[:, :, :], SH[:, :, :], bcast(TR[:, :], 2, LE), ALU.mult))
                assert n[0] == LORA_STEPS
                dve.wait_ge(s_mid.handle, s_mid.at(NT))
                dve.wait_ge(s_b2.handle, s_b2.at(NT))

                def gated(u, t):
                    mid = MID[:, t, :].rearrange("p (e r) -> p e r", r=LR)
                    dve.tensor_tensor(GM[:, u, :].rearrange("p (e r) -> p e r", r=LR), mid, bcast(GT[:, t, :], 2, LR), ALU.mult).then_inc(s_gm.handle, 1)

                gated(0, 0)
                gated(1, 1)

                def lora_outputs(i, more):
                    for u in range(2 if more else 0):
                        dve.wait_ge(s_mtp.handle, s_mtp.at(2 * i + u + 1))
                        gated(u, 2 * i + 2 + u)
                    for u in range(2):
                        dve.wait_ge(s_lo.handle, s_lo.at(2 * i + u + 1))
                        dve.scalar_tensor_tensor(g.X[:, 2 * i + u, :], bank(2 + u)[:, 0:D], 0.5 * LORA_SCALE, g.X[:, 2 * i + u, :],
                                                 ALU.mult, ALU.add).then_inc(s_x.handle, 1)

                with dve.Fori(0, NT // 2 - 1) as i:
                    lora_outputs(i, True)
                lora_outputs(NT // 2 - 1, False)


def mla_stage(nc, g, dram):
    S = lambda name: g.sem("mla_" + name)
    s_w, s_w2 = S("weights"), S("up_weights")
    s_stat, s_mv, s_sd, s_rs = (g.sem("mla_" + n) for n in ("partial_stats", "stats", "deviations", "reciprocals"))
    s_gp, s_gc, s_up, s_uc = S("absorbed_q_in_psum"), S("absorbed_q"), S("absorbed_v_in_psum"), S("absorbed_v")
    s_xn, s_xtp, s_xtc, s_cp, s_cc, s_sq = S("xn_tile"), S("xnT_in_psum"), S("xnT_copied"), S("latents_in_psum"), S("latents_copied"), S("squares")
    s_rd, s_rr, s_re, s_xb, s_xs = S("latent_deviations"), S("latent_scales"), S("latent_mean_squares"), S("sequence_xnT"), S("xnT_saved")
    s_cn, s_cn2, s_ctp, s_cq, s_ckh, s_ckl = S("latents"), S("latent_twice"), S("latentsT_in_psum"), S("cqT_copied"), S("latent_keys_high"), S("latent_keys_low")
    s_pr, s_ab, s_ro, s_rows = S("projected"), S("latent_queries"), S("rotary_products"), S("rotary_rows")
    s_qkp, s_hi, s_lo = S("qkT_in_psum"), S("high_parts"), S("low_parts")
    s_sc, s_mx, s_nb, s_p = S("scores"), S("row_max"), S("negative_max"), S("probs")
    s_ptp, s_ptc, s_ot, s_otc, s_bt = S("probsT_in_psum"), S("probsT_copied"), S("outT_in_psum"), S("outT_copied"), S("out_in_psum")
    s_dn, s_la = S("denominators"), S("latent_rows")
    s_lp, s_lc, s_o, s_x = S("latent_rowsT_in_psum"), S("latent_rowsT_copied"), S("outputs"), S("x_updated")
    NL = DQL + DKVL
    NU = 2 * TB
    with ExitStack() as ctx:
        sb = lambda name, shape, dt=F32: g.sb(ctx, "mla_" + name, shape, dt)
        WR = sb("Wrope", [P, KD, NP1 * 4 * RD])
        WD, WN = sb("Wdown", [P, KD, NL]), sb("norms", [P, NL])
        RO = sb("rope", [P, 2, TB, RD])
        GQ, UV = sb("GQ", [DQL, H1 * DKVL]), sb("UV", [P, NP1, D])
        bank, banks = g.bank, g.banks
        ident = g.C[:, C_ID:C_ID + P]
        kv = slice(DQL, NL)

        with ExitStack() as up:
            WQT, WKT, WVT = (g.sb(up, "mla_" + n, [P, H1, m]) for n, m in (("WqT", DQL), ("WkT", DKVL), ("WvT", DKVL)))
            WOU = g.sb(up, "mla_Wout", [P, H1, D])
            with nc.Block() as block:
                @block.sync
                def _(sp):
                    g.credit(sp)
                    for dst, name in ((WQT, "WqT"), (WKT, "WkT"), (WVT, "WvT"), (WOU, "Wout")):
                        sp.dma_start(dst[:, :, :], dram[name]).then_inc(s_w2.handle, 16)
                    sp.dma_start(WD[:, :, :], dram["Wdown"]).then_inc(s_w.handle, 16)
                    sp.dma_start(WN[:, :], dram["norms"].to_broadcast([P, NL])).then_inc(s_w.handle, 16)
                    sp.dma_start(RO[:, :, :, :], dram["rope"].rearrange("p c t d -> p c t d")).then_inc(s_w.handle, 16)
                    sp.dma_start(WR[:, :, :], dram["Wrope"]).then_inc(s_w.handle, 16)
                    sp.wait_ge(s_w.handle, s_w.at(64))
                    sp.wait_ge(s_w2.handle, s_w2.at(64))

                @block.tensor
                def _(pe):
                    pe.wait_ge(s_w2.handle, s_w2.at(64))
                    for h in range(H1):
                        ins = pe.matmul(bank(h // 8)[0:DQL, h % 8 * DKVL:(h % 8 + 1) * DKVL], WQT[:, h, :], WKT[:, h, :], start=True, stop=True)
                    ins.then_inc(s_gp.handle, 1)
                    for h in range(H1):
                        ins = pe.matmul(bank(2 + h // 4)[h % 2 * DKVL:(h % 2 + 1) * DKVL, h // 2 % 2 * D:(h // 2 % 2 + 1) * D],
                                        WVT[:, h, :], WOU[:, h, :], start=True, stop=True)
                    ins.then_inc(s_up.handle, 1)

                @block.scalar
                def _(act):
                    act.wait_ge(s_gp.handle, s_gp.at(1))
                    act.copy(GQ[:, :], banks(0, 2)[0:DQL, :]).then_inc(s_gc.handle, 1)
                    act.wait_ge(s_up.handle, s_up.at(1))
                    for m in range(4):
                        act.copy(UV[:, 2 * m:2 * m + 2, :].rearrange("p a d -> p (a d)"), bank(2 + m)[:, :]).then_inc(s_uc.handle, 1)

        XNS, XT = sb("XNS", [P, 2, D]), sb("XT", [P, KD, SEQ])
        CR, SQ, SS = sb("CR", [P, TB, NL]), sb("SQ", [P, 2, NL]), sb("SS", [P, 2, TB])
        SE, SD2, RS2 = sb("SE", [P, 2, TB]), sb("SD2", [P, 2, TB]), sb("RS2", [P, 2, TB])
        CN = sb("CN", [P, TB, DQL + 2 * DKVL])
        CQ = sb("CQ", [DQL, SEQ])
        QH, QL, KH, KL = (sb(n, [P, 2, 2, SEQ], F32R) for n in ("QH", "QL", "KH", "KL"))
        T1, T2 = sb("T1", [P, 2, 4 * RD]), sb("T2", [P, 2, 4 * RD])
        QR, KR = sb("QR", [P, 2, 6 * RD]), sb("KR", [P, 2, 2 * RD])
        PR, PT = sb("PR", [P, 2, SEQ]), sb("PT", [P, 2, 2, TB, P])
        MX, NB, DN, RD_ = sb("MX", [P, NU]), sb("NB", [P, NU]), sb("DN", [P, NU]), sb("RD", [P, 2])
        OT, LA = sb("OT", [P, P]), sb("LA", [P, TB, NP1 * P])
        LT = PR[:, :, :].rearrange("p u (k s) -> p u k s", s=P)

        steps = {}
        for j in range(TB):
            steps[7 * j // 2] = ("projections", j)
            steps[7 * j // 2 + 2] = ("transposes", j)
        assert len(steps) == 2 * TB and max(steps) < 2 * NU - 4

        def pairs_of_a_sequence(engine, b, pair):
            pair(b * NP1, 0, 0, True, False)
            with engine.Fori(0, NP1 // 2 - 1) as rr:
                pair(b * NP1 + 2 * rr + 1, 2 * rr + 1, 1, False, False)
                pair(b * NP1 + 2 * rr + 2, 2 * rr + 2, 0, False, False)
            pair(b * NP1 + NP1 - 1, NP1 - 1, 1, False, True)

        pr_bank = lambda j, alone: bank(j % 2) if alone else bank(7)
        tr_bank = lambda j, alone: bank(2 + j % 2) if alone else bank(7)

        with nc.Block() as block:
            @block.tensor
            def _(pe):
                with pe.Fori(0, BATCH) as b:
                    for j in range(TB):
                        pe.wait_ge(s_xn.handle, s_xn.at(TB * b + j + 1))
                        if j >= 2:
                            pe.wait_ge(s_xtc.handle, s_xtc.at(TB * b + j - 1))
                        for k in range(KD):
                            ins = pe.transpose(bank(j % 2)[:, k * P:(k + 1) * P], XNS[:, j % 2, k * P:(k + 1) * P], ident)
                        ins.then_inc(s_xtp.handle, 1)
                        pe.wait_ge(s_xtc.handle, s_xtc.at(TB * b + j + 1))
                        if j >= 2:
                            pe.wait_ge(s_cc.handle, s_cc.at(TB * b + j - 1))
                        for k in range(KD):
                            ins = pe.matmul(bank(2 + j % 2)[:, 0:NL], XT[:, k, j * P:(j + 1) * P], WD[:, k, :], start=(k == 0), stop=(k == KD - 1))
                        ins.then_inc(s_cp.handle, 1)
                    for j in range(TB):
                        pe.wait_ge(s_cn2.handle, s_cn2.at(TB * b + j + 1))
                        if j >= 2:
                            pe.wait_ge(s_ckl.handle, s_ckl.at(2 * (TB * b + j - 1)))
                        pe.transpose(bank(4 + j % 2)[:, 0:P], CN[:, j, 0:P], ident)
                        pe.transpose(bank(4 + j % 2)[:, P:2 * P], CN[:, j, DQL:DQL + 2 * DKVL], ident).then_inc(s_ctp.handle, 1)
                    pe.wait_ge(s_cq.handle, s_cq.at(TB * (b + 1)))
                    pe.wait_ge(s_ckl.handle, s_ckl.at(2 * TB * (b + 1)))

                    def projections(it, r, j, alone):
                        if not alone:
                            pe.wait_ge(s_lo.handle, s_lo.at(3 * (TB * it + j)))
                        elif j >= 2:
                            pe.wait_ge(s_ro.handle, s_ro.at(3 * (TB * it + j - 1)))
                        out = pr_bank(j, alone)
                        for k in range(KD):
                            pe.matmul(out[:, 0:4 * RD], XT[:, k, j * P:(j + 1) * P], WR[:, k, bass.ds(r * (4 * RD), 4 * RD)],
                                      start=(k == 0), stop=(k == KD - 1))
                        pe.matmul(out[:, 4 * RD:6 * RD], CQ[:, j * P:(j + 1) * P], GQ[:, bass.ds(r * (2 * RD), 2 * RD)],
                                  start=True, stop=True).then_inc(s_pr.handle, 1)

                    def transposes(it, j, alone):
                        pe.wait_ge(s_rows.handle, s_rows.at(2 * (TB * it + j + 1)))
                        if alone and j >= 2:
                            pe.wait_ge(s_lo.handle, s_lo.at(3 * (TB * it + j - 1)))
                        out = tr_bank(j, alone)
                        for m in range(2):
                            pe.transpose(out[:, m * P:(m + 1) * P], QR[:, j % 2, m * P:(m + 1) * P], ident)
                        pe.transpose(out[:, 2 * P:3 * P], KR[:, j % 2, :], ident).then_inc(s_qkp.handle, 1)

                    for j in range(TB):
                        projections(b * NP1, 0, j, True)
                        if j:
                            transposes(b * NP1, j - 1, True)
                    transposes(b * NP1, TB - 1, True)

                    def scores_of(it, n, buf, free, between=None):
                        if n == 0:
                            pe.wait_ge(s_lo.handle, s_lo.at(3 * TB * (it + 1)))
                        if not free:
                            pe.wait_ge(s_p.handle, s_p.at(NU * it + n - 1))
                        qs = slice(n // 2 * P, (n // 2 + 1) * P)
                        for c in range(2):
                            if c and between:
                                between()
                            ks = slice(c * 512, (c + 1) * 512)
                            for m, (q, k) in enumerate(((QH, KH), (QL, KH), (QH, KL))):
                                ins = pe.matmul(bank(2 * (n % 2) + c)[:, :], q[:, buf, n % 2, qs], k[:, buf, n % 2, ks], start=(m == 0), stop=(m == 2))
                        ins.then_inc(s_sc.handle, 1)

                    def probs_transposes(it, n, free):
                        pe.wait_ge(s_p.handle, s_p.at(NU * it + n + 1))
                        for c in range(2):
                            if not free:
                                pe.wait_ge(s_ptc.handle, s_ptc.at(2 * (NU * it + n) + c - 1))
                            for k in range(4):
                                ins = pe.transpose(bank(4 + c)[:, k * P:(k + 1) * P], PR[:, n % 2, (4 * c + k) * P:(4 * c + k + 1) * P], ident)
                            ins.then_inc(s_ptp.handle, 1)

                    def values_of(tile, i, half, free):
                        if half == 0:
                            pe.wait_ge(s_ptc.handle, s_ptc.at(4 * (tile + 1)))
                            if not free:
                                pe.wait_ge(s_la.handle, s_la.at(tile))
                        for k in range(4 * half, 4 * half + 4):
                            for h in range(2):
                                ins = pe.matmul(bank(6)[h * DKVL:(h + 1) * DKVL, 0:P], CN[:, k, DQL:DQL + DKVL], PT[:, i % 2, h, k, :],
                                                start=(k == 0), stop=(k == TB - 1))
                        if half == 1:
                            ins.then_inc(s_ot.handle, 1)

                    def out_rows_of(tile):
                        pe.wait_ge(s_otc.handle, s_otc.at(tile + 1))
                        pe.transpose(bank(6)[:, P:2 * P], OT[:, :], ident).then_inc(s_bt.handle, 1)

                    def pair(it, r, buf, first, last):
                        def step(s):
                            if s in steps and not last:
                                what, j = steps[s]
                                if what == "projections":
                                    projections(it + 1, r + 1, j, False)
                                else:
                                    transposes(it + 1, j, False)

                        if first:
                            scores_of(it, 0, buf, True)
                        for n in range(NU):
                            rows = None
                            if n % 2 == 0 and (n >= 4 or not first):
                                rows = lambda: out_rows_of(TB * it + n // 2 - 2)
                            if n + 1 < NU:
                                scores_of(it, n + 1, buf, first and n == 0, rows)
                            elif not last:
                                scores_of(it + 1, 0, 1 - buf, False)
                            step(2 * n)
                            probs_transposes(it, n, first and n == 0)
                            if n >= 2 or not first:
                                values_of(TB * it + n // 2 - 1, (n // 2 - 1) % TB, n % 2, first and n < 4)
                            step(2 * n + 1)
                        if last:
                            out_rows_of(TB * it + TB - 2)
                            for half in range(2):
                                values_of(TB * it + TB - 1, TB - 1, half, False)
                            out_rows_of(TB * it + TB - 1)

                    pairs_of_a_sequence(pe, b, pair)

                    for i in range(TB):
                        pe.wait_ge(s_la.handle, s_la.at(TB * NP1 * (b + 1)))
                        for c in range(2):
                            if i:
                                pe.wait_ge(s_lc.handle, s_lc.at(2 * (TB * b + i) + c - 1))
                            for k in range(4):
                                ins = pe.transpose(bank(4 + c)[:, k * P:(k + 1) * P], LA[:, i, (4 * c + k) * P:(4 * c + k + 1) * P], ident)
                            ins.then_inc(s_lp.handle, 1)
                        pe.wait_ge(s_lc.handle, s_lc.at(2 * (TB * b + i + 1)))
                        if i >= 2:
                            pe.wait_ge(s_x.handle, s_x.at(TB * b + i - 1))
                        for k in range(NP1):
                            ins = pe.matmul(bank(6 + i % 2)[:, 0:D], LT[:, i % 2, k, :], UV[:, k, :], start=(k == 0), stop=(k == NP1 - 1))
                        ins.then_inc(s_o.handle, 1)
                    pe.wait_ge(s_x.handle, s_x.at(TB * (b + 1)))

            @block.scalar
            def _(act):
                norm_sd_act(act, g, s_mv, s_sd)
                with act.Fori(0, BATCH) as b:
                    def latents(j):
                        act.wait_ge(s_cp.handle, s_cp.at(TB * b + j + 1))
                        for m, cols in enumerate((slice(0, DQL), kv)):
                            if j >= 2:
                                act.wait_ge(s_sq.handle, s_sq.at(2 * (TB * b + j - 2) + m + 1))
                            act.activation(SQ[:, j % 2, cols], bank(2 + j % 2)[:, cols], ACT.Square, accum_out=SS[:, m, j:j + 1]).then_inc(s_sq.handle, 1)
                        act.copy(CR[:, j, :], bank(2 + j % 2)[:, 0:NL]).then_inc(s_cc.handle, 1)

                    for j in range(TB):
                        act.wait_ge(s_xtp.handle, s_xtp.at(TB * b + j + 1))
                        act.copy(XT[:, :, j * P:(j + 1) * P], bank(j % 2)[:, 0:KD * P].rearrange("p (k s) -> p k s", s=P)).then_inc(s_xtc.handle, 1)
                        if j:
                            latents(j - 1)
                    latents(TB - 1)
                    act.wait_ge(s_re.handle, s_re.at(b + 1))
                    act.activation(SD2[:, :, :], SE[:, :, :], ACT.Sqrt, bias=g.C[:, C_EPS + 1:C_EPS + 2]).then_inc(s_rd.handle, 1)
                    nc.scalar.preload_act_table(ACT.Exp)
                    for j in range(TB):
                        tok = slice(j * P, (j + 1) * P)
                        act.wait_ge(s_ctp.handle, s_ctp.at(TB * b + j + 1))
                        act.copy(CQ[:, tok], bank(4 + j % 2)[0:DQL, 0:P]).then_inc(s_cq.handle, 1)
                        act.copy(KH[DKVL:P, :, 0, tok], bcast(bank(4 + j % 2)[DKVL:P, P:2 * P], 1, 2)).then_inc(s_ckh.handle, 1)
                        act.copy(KH[0:DKVL, :, 1, tok], bcast(bank(4 + j % 2)[0:DKVL, P:2 * P], 1, 2)).then_inc(s_ckh.handle, 1)

                    def latent_queries(it, j, alone):
                        act.wait_ge(s_pr.handle, s_pr.at(TB * it + j + 1))
                        if j >= 2:
                            act.wait_ge(s_qkp.handle, s_qkp.at(TB * it + j - 1))
                        act.copy(QR[:, j % 2, RD:3 * RD], pr_bank(j, alone)[:, 4 * RD:6 * RD]).then_inc(s_ab.handle, 1)

                    def highs(it, buf, j, alone):
                        tok = slice(j * P, (j + 1) * P)
                        rows_t = tr_bank(j, alone)
                        act.wait_ge(s_qkp.handle, s_qkp.at(TB * it + j + 1))
                        act.copy(QH[:, buf, :, tok], rows_t[:, 0:2 * P].rearrange("p (m s) -> p m s", m=2)).then_inc(s_hi.handle, 1)
                        act.copy(KH[0:RD, buf, 0, tok], rows_t[0:RD, 2 * P:3 * P]).then_inc(s_hi.handle, 1)
                        act.copy(KH[RD:P, buf, 1, tok], rows_t[RD:P, 2 * P:3 * P]).then_inc(s_hi.handle, 1)

                    for j in range(TB):
                        latent_queries(b * NP1, j, True)
                        if j:
                            highs(b * NP1, 0, j - 1, True)
                    highs(b * NP1, 0, TB - 1, True)

                    def exp_of(it, n, free):
                        act.wait_ge(s_nb.handle, s_nb.at(NU * it + n + 1))
                        if not free:
                            act.wait_ge(s_ptp.handle, s_ptp.at(2 * (NU * it + n - 1)))
                        act.activation(PR[:, n % 2, :], banks(2 * (n % 2), 2)[:, :], ACT.Exp, bias=NB[:, n:n + 1], scale=MLA_SCALE,
                                       accum_out=DN[:, n:n + 1]).then_inc(s_p.handle, 1)

                    def pair(it, r, buf, first, last):
                        def step(s):
                            if s in steps and not last:
                                what, j = steps[s]
                                if what == "projections":
                                    latent_queries(it + 1, j, False)
                                else:
                                    highs(it + 1, 1 - buf, j, False)

                        if first:
                            exp_of(it, 0, True)
                        for n in range(NU):
                            i, h = n // 2, n % 2
                            step(2 * n - 1)
                            step(2 * n)
                            for c in range(2):
                                act.wait_ge(s_ptp.handle, s_ptp.at(2 * (NU * it + n) + c + 1))
                                if h == 0 and c == 0 and (i >= 2 or not first):
                                    act.wait_ge(s_ot.handle, s_ot.at(TB * it + i - 1))
                                act.copy(PT[:, i % 2, h, 4 * c:4 * c + 4, :], bank(4 + c)[:, :].rearrange("p (k s) -> p k s", s=P)).then_inc(s_ptc.handle, 1)
                            if n + 1 < NU:
                                exp_of(it, n + 1, first and n == 0)
                            elif not last:
                                exp_of(it + 1, 0, False)

                    pairs_of_a_sequence(act, b, pair)

                    for i in range(TB):
                        for c in range(2):
                            act.wait_ge(s_lp.handle, s_lp.at(2 * (TB * b + i) + c + 1))
                            if i >= 2 and c == 0:
                                act.wait_ge(s_o.handle, s_o.at(TB * b + i - 1))
                            act.copy(LT[:, i % 2, 4 * c:4 * c + 4, :], bank(4 + c)[:, :].rearrange("p (k s) -> p k s", s=P)).then_inc(s_lc.handle, 1)

            @block.gpsimd
            def _(pool):
                with pool.Fori(0, BATCH * NP1) as it:
                    for j in range(TB):
                        u = j % 2
                        pool.wait_ge(s_ro.handle, s_ro.at(3 * (TB * it + j + 1)))
                        if j >= 2:
                            pool.wait_ge(s_qkp.handle, s_qkp.at(TB * it + j - 1))
                        heads = lambda ap: ap.rearrange("p (m d) -> p m d", m=2)
                        qr = QR[:, u, :].rearrange("p (m d) -> p m d", m=2)[:, :, 0:RD]
                        pool.tensor_tensor(qr, heads(T1[:, u, 0:2 * RD]), heads(T2[:, u, 0:2 * RD]), ALU.add).then_inc(s_rows.handle, 1)
                        pool.tensor_tensor(KR[:, u, :], T1[:, u, 2 * RD:4 * RD], T2[:, u, 2 * RD:4 * RD], ALU.add).then_inc(s_rows.handle, 1)

            @block.vector
            def _(dve):
                norm_stats_dve(dve, g, s_stat, s_mv)
                norm_rs_dve(dve, g, s_sd, s_rs)
                with dve.Fori(0, BATCH) as b:
                    for j in range(TB):
                        if j >= 2:
                            dve.wait_ge(s_xtp.handle, s_xtp.at(TB * b + j - 1))
                        normalize(dve, g, XNS[:, j % 2, :], b * TB + j).then_inc(s_xn.handle, 1)
                    dve.wait_ge(s_cc.handle, s_cc.at(TB * (b + 1)))
                    for m, n in enumerate((DQL, DKVL)):
                        ins = dve.tensor_scalar(SE[:, m, :], SS[:, m, :], 1.0 / n, None, ALU.mult)
                    ins.then_inc(s_re.handle, 1)
                    dve.wait_ge(s_rd.handle, s_rd.at(b + 1))
                    dve.reciprocal(RS2[:, :, :], SD2[:, :, :]).then_inc(s_rr.handle, 1)
                    dve.wait_ge(s_rr.handle, s_rr.at(b + 1))
                    for j in range(TB):
                        dve.scalar_tensor_tensor(CN[:, j, 0:DQL], CR[:, j, 0:DQL], RS2[:, 0, j:j + 1], WN[:, 0:DQL], ALU.mult, ALU.mult)
                        for m in range(2):
                            ins = dve.scalar_tensor_tensor(CN[:, j, DQL + m * DKVL:DQL + (m + 1) * DKVL], CR[:, j, kv], RS2[:, 1, j:j + 1],
                                                           WN[:, kv], ALU.mult, ALU.mult)
                        ins.then_inc(s_cn2.handle, 1)
                    for j in range(TB):
                        tok = slice(j * P, (j + 1) * P)
                        dve.wait_ge(s_ckh.handle, s_ckh.at(2 * (TB * b + j + 1)))
                        for h, rows in ((0, slice(DKVL, P)), (1, slice(0, DKVL))):
                            dve.tensor_tensor(KL[rows, :, h, tok], bcast(bank(4 + j % 2)[rows, P:2 * P], 1, 2), KH[rows, :, h, tok].bitcast(F32),
                                              ALU.subtract).then_inc(s_ckl.handle, 1)

                    def rotary(it, j, alone):
                        u = j % 2
                        dve.wait_ge(s_ab.handle, s_ab.at(TB * it + j + 1))
                        if j >= 2:
                            dve.wait_ge(s_rows.handle, s_rows.at(2 * (TB * it + j - 1)))
                        rot = pr_bank(j, alone)[:, 0:4 * RD].rearrange("p (m d) -> p m d", d=RD)
                        t1, t2 = (t[:, u, :].rearrange("p (m d) -> p m d", d=RD) for t in (T1, T2))
                        half = RD // 2
                        dve.tensor_tensor(t1, rot, bcast(RO[:, 0, j, :], 1, 4), ALU.mult).then_inc(s_ro.handle, 1)
                        dve.tensor_tensor(t2[:, :, 0:half], rot[:, :, half:RD], bcast(RO[:, 1, j, 0:half], 1, 4), ALU.mult).then_inc(s_ro.handle, 1)
                        dve.tensor_tensor(t2[:, :, half:RD], rot[:, :, 0:half], bcast(RO[:, 1, j, half:RD], 1, 4), ALU.mult).then_inc(s_ro.handle, 1)

                    def lows(it, buf, j, alone):
                        tok = slice(j * P, (j + 1) * P)
                        rows_t = tr_bank(j, alone)
                        dve.wait_ge(s_hi.handle, s_hi.at(3 * (TB * it + j + 1)))
                        dve.tensor_tensor(QL[:, buf, :, tok], rows_t[:, 0:2 * P].rearrange("p (m s) -> p m s", m=2),
                                          QH[:, buf, :, tok].bitcast(F32), ALU.subtract).then_inc(s_lo.handle, 1)
                        for h, rows in ((0, slice(0, RD)), (1, slice(RD, P))):
                            dve.tensor_tensor(KL[rows, buf, h, tok], rows_t[rows, 2 * P:3 * P], KH[rows, buf, h, tok].bitcast(F32), ALU.subtract).then_inc(s_lo.handle, 1)

                    for j in range(TB):
                        rotary(b * NP1, j, True)
                        if j:
                            lows(b * NP1, 0, j - 1, True)
                    lows(b * NP1, 0, TB - 1, True)

                    def max_of(it, n):
                        dve.wait_ge(s_sc.handle, s_sc.at(NU * it + n + 1))
                        dve.tensor_reduce(MX[:, n:n + 1], banks(2 * (n % 2), 2)[:, :], AX_X, ALU.max).then_inc(s_mx.handle, 1)
                        dve.wait_ge(s_mx.handle, s_mx.at(NU * it + n + 1))
                        dve.tensor_scalar(NB[:, n:n + 1], MX[:, n:n + 1], -MLA_SCALE, None, ALU.mult).then_inc(s_nb.handle, 1)

                    def out_copy(tile):
                        dve.wait_ge(s_ot.handle, s_ot.at(tile + 1))
                        dve.tensor_copy(OT[:, :], bank(6)[:, 0:P]).then_inc(s_otc.handle, 1)

                    def finish(tile, i, r):
                        dve.reciprocal(RD_[:, :], DN[:, 2 * i:2 * i + 2]).then_inc(s_dn.handle, 1)
                        dve.wait_ge(s_dn.handle, s_dn.at(tile + 1))
                        dve.wait_ge(s_bt.handle, s_bt.at(tile + 1))
                        dve.tensor_tensor(LA[:, i, bass.ds(r * P, P)].rearrange("p (h d) -> p h d", h=2),
                                          bank(6)[:, P:2 * P].rearrange("p (h d) -> p h d", h=2), bcast(RD_[:, :], 2, DKVL), ALU.mult).then_inc(s_la.handle, 1)

                    def pair(it, r, buf, first, last):
                        def step(s):
                            if s in steps and not last:
                                what, j = steps[s]
                                if what == "projections":
                                    rotary(it + 1, j, False)
                                else:
                                    lows(it + 1, 1 - buf, j, False)

                        if first:
                            max_of(it, 0)
                        for n in range(NU):
                            ends = n % 2 == 0 and (n >= 4 or not first)
                            tile, i = TB * it + n // 2 - 2, (n // 2 - 2) % TB
                            if ends:
                                out_copy(tile)
                            step(2 * n - 1)
                            if ends:
                                finish(tile, i, r if n >= 4 else r - 1)
                            if n + 1 < NU:
                                max_of(it, n + 1)
                            elif not last:
                                max_of(it + 1, 0)
                            step(2 * n)
                        if last:
                            for i in (TB - 2, TB - 1):
                                out_copy(TB * it + i)
                                finish(TB * it + i, i, r)

                    pairs_of_a_sequence(dve, b, pair)

                    for i in range(TB):
                        dve.wait_ge(s_o.handle, s_o.at(TB * b + i + 1))
                        xt = g.X[:, b * TB + i, :]
                        dve.tensor_tensor(xt, bank(6 + i % 2)[:, 0:D], xt, ALU.add).then_inc(s_x.handle, 1)


def store_stage(nc, g, out):
    s_out = g.sem("stored")
    with nc.Block() as block:
        @block.sync
        def _(sp):
            g.credit(sp)
            sp.dma_start(out.rearrange("b (t p) d -> p (b t) d", p=P), g.X[:, :, :]).then_inc(s_out.handle, 16)
            sp.wait_ge(s_out.handle, s_out.at(16))


def macaron_program(nc, dram, out, stages="mamlLl"):
    with ExitStack() as ctx:
        g = Core(nc, ctx)
        g.X = g.sb(ctx, "X", [P, NT, D])
        g.C = g.sb(ctx, "C", [P, C_END])
        g.ST = g.sb(ctx, "ST", [P, NT, 6])
        g.MV = g.sb(ctx, "MV", [P, NT, 2])
        g.SD = g.sb(ctx, "SD", [P, NT])
        g.RS = g.sb(ctx, "RS", [P, NT])
        g.XG = nc.dram_tensor("slots_in", [(NTILE + 2) * P, D], F32, kind="Internal").ap()
        g.YG = nc.dram_tensor("slots_out", [NTILE * P, D], F32, kind="Internal").ap()
        PS = ctx.enter_context(nc.psum_tensor("PS", [P, 8, 512], F32))
        g.bank = lambda n: PS[:, n, :]
        g.banks = lambda n, m: PS[:, n:n + m, :].rearrange("p b c -> p (b c)")
        g.s_w1 = g.sem("loaded_W1")
        g.s_second = [g.sem(f"second_added{r}") for r in range(2)]
        with ExitStack() as moe:
            g.XN = g.sb(moe, "XN", [P, NT, D])
            g.W1 = g.sb(moe, "W1", [P, NE, KD, FF])
            load_stage(nc, g, dram)
            moe_stage(nc, g, dram, 0)
            if "a" in stages:
                attention_stage(nc, g, dram)
            if stages.count("m") > 1:
                moe_stage(nc, g, dram, 1)
        if "l" in stages:
            lora_stage(nc, g, dram, 0)
        if "L" in stages:
            mla_stage(nc, g, dram)
        if stages.count("l") > 1:
            lora_stage(nc, g, dram, 1)
        store_stage(nc, g, out)


def shape_constants():
    c = np.zeros((P, C_END), np.float32)
    c[:, C_ID:C_ID + P] = np.eye(P)
    c[:, C_ONE:C_ONE + P] = 1.0
    c[:, C_TRI:C_TRI + P] = np.triu(np.ones((P, P)), 1)
    c[:, C_LOW:C_LOW + P] = np.tril(np.ones((P, P)))
    c[:, C_IOTA:C_IOTA + NE] = np.arange(NE)
    c[:, C_TILE:C_TILE + NTILE] = np.arange(NTILE)
    c[:, C_EPS] = LN_EPS
    c[:, C_EPS + 1] = RMS_EPS
    freqs = (np.float32(1.0) / np.float32(10000.0) ** (np.arange(0, RD, 2, dtype=np.float32) / np.float32(RD))).astype(np.float32)
    ang = np.outer(np.arange(SEQ, dtype=np.float32), freqs).astype(np.float32)
    cos, sin = np.cos(ang).astype(np.float32), np.sin(ang).astype(np.float32)
    rope = np.stack([np.concatenate([cos, cos], 1), np.concatenate([-sin, sin], 1)])
    rope = rope.reshape(2, TB, P, RD).transpose(2, 0, 1, 3)
    return c, np.ascontiguousarray(rope)


def lay_out(a):
    f = np.ascontiguousarray
    chunks = lambda w: w.reshape(w.shape[0] // P, P, -1).transpose(1, 0, 2)
    const, rope = shape_constants()
    r = {"const": const, "rope": rope, "x": f(a["L0_attn_x"].reshape(BATCH * SEQ, D))}
    r["router_w"] = f(chunks(a["L0_ffn_router_w"]))
    r["W1"] = f(a["L0_ffn_W1"].reshape(NE, KD, P, FF).transpose(2, 0, 1, 3))
    r["W2"] = f(a["L0_ffn_W2"].reshape(NE, KF, P, D).transpose(2, 0, 1, 3))
    heads = lambda w: w.reshape(D, NG0, HG * DH0)
    r["Wqkv"] = f(chunks(np.concatenate([heads(a["L0_attn_Wq"]), heads(a["L0_attn_Wk"]), heads(a["L0_attn_Wv"])], 2).reshape(D, -1)))
    r["Wo"] = f(chunks(a["L0_attn_Wo"]))
    pairs = lambda w: w.reshape(D, NP1, 2, RD // 2, 2).transpose(0, 1, 2, 4, 3).reshape(D, NP1, 1, 2 * RD)
    r["Wrope"] = f(chunks(np.concatenate([pairs(a["L1_attn_Wq_rope"]), pairs(a["L1_attn_Wk_rope"])], 2).reshape(D, -1)))
    r["Wdown"] = f(chunks(np.concatenate([a["L1_attn_Wq_down"], a["L1_attn_Wkv_down"]], 1)))
    r["norms"] = f(np.concatenate([a["L1_attn_q_norm_w"], a["L1_attn_kv_norm_w"]]).reshape(1, -1))
    up = lambda w: f(w.reshape(-1, H1, HD1).transpose(2, 1, 0))
    r["WqT"], r["WkT"], r["WvT"] = up(a["L1_attn_Wq_up"]), up(a["L1_attn_Wk_up"]), up(a["L1_attn_Wv_up"])
    r["Wout"] = f(a["L1_attn_Wout"].reshape(H1, HD1, D).transpose(1, 0, 2))
    r["Wbase"] = f(chunks(np.ascontiguousarray(a["L1_ffn_base_w"].T)))
    lora = a["L1_ffn_lora_A"].transpose(1, 0, 2).reshape(D, LE * LR)
    r["Wlora"] = f(chunks(np.concatenate([lora, a["L1_ffn_router_w"].T], 1)))
    r["Blora"] = f(a["L1_ffn_lora_B"].reshape(LE * LR, D))
    r["biases"] = f(np.concatenate([a["L1_ffn_base_b"], a["L1_ffn_router_b"]]).reshape(1, -1))
    return r


def kernel(**inputs):
    import concourse.bacc as _bacc
    from concourse.bass_utils import run_bass_kernel_spmd as _run

    nc = _bacc.Bacc("TRN2", target_bir_lowering=False, num_devices=1)
    arrays, dram = {}, {}
    for name, a in lay_out({k: np.asarray(v) for k, v in inputs.items()}).items():
        arrays[f"in_{name}_dram"] = a
        dram[name] = nc.dram_tensor(f"in_{name}_dram", a.shape, F32, kind="ExternalInput").ap()
    out = nc.dram_tensor("out_0_dram", (BATCH, SEQ, D), F32, kind="ExternalOutput").ap()
    macaron_program(nc, dram, out)
    r = _run(nc, [arrays], core_ids=[0])
    return r.results[0]["out_0_dram"]
```

```python
from contextlib import ExitStack

import numpy as np

import concourse.bass as bass
from concourse import mybir

F32 = mybir.dt.float32
F32R = mybir.dt.float32r
I32 = mybir.dt.int32
U32 = mybir.dt.uint32
ALU = mybir.AluOpType
ACT = mybir.ActivationFunctionType
AX_X = mybir.AxisListType.X
AX_XY = mybir.AxisListType.XY

P = 128
BATCH, SEQ, D = 2, 1024, 256
NT = BATCH * SEQ // P
TB = SEQ // P
KD = D // P
LN_EPS = 1e-5

NE, FF, TOP = 16, 512, 2
KF = FF // P
NTILE = 48
assert NTILE >= NT * TOP + NE - 1 and NTILE % 2 == 0
ROWS = NT * P + P
NB4 = 4

H0, DH0 = 16, 16
HG = 4
NG0 = H0 // HG
VW = 32

H1, RD, HD1, DQL, DKVL = 16, 64, 128, 48, 64
NP1 = H1 // 2
LEAST = -3.0e38
MLA_SCALE = float(HD1 + RD) ** -0.5
RMS_EPS = 1e-6

LE, LR = 8, 16
LORA_SCALE = 2.0

MOE_STEPS = 55
LORA_STEPS = 32

C_ID, C_ONE, C_TRI, C_LOW, C_IOTA, C_TILE = 0, 128, 256, 384, 512, 528
C_EPS = C_TILE + NTILE + 2
C_END = C_EPS + 2


class Sem:

    def __init__(self, handle, each, rep, pool_dma):
        self.handle, self.base = handle, each * rep + (0 if pool_dma else 1)

    def at(self, n):
        return self.base + n


def bcast(ap, axis, n):
    ap = ap.unsqueeze(axis)
    shape = list(ap.shape)
    shape[axis] = n
    return ap.to_broadcast(shape)


class Core:

    def __init__(self, nc, ctx):
        self.nc, self.ctx = nc, ctx
        self.handles = {}
        self.fresh = []

    def sb(self, ctx, name, shape, dt=F32):
        return ctx.enter_context(self.nc.sbuf_tensor(name, shape, dt))

    def sem(self, name, each=0, rep=0, pool_dma=False):
        if name not in self.handles:
            self.handles[name] = self.ctx.enter_context(self.nc.semaphore(name))
            if not pool_dma:
                self.fresh.append(self.handles[name])
        return Sem(self.handles[name], each, rep, pool_dma)

    def credit(self, sp):
        for handle in self.fresh:
            sp.sem_inc(handle, 1)
        self.fresh = []


def norm_stats_dve(dve, g, s_mv):
    for t in range(NT):
        dve.bn_aggr(g.MV[:, t, :], g.ST[:, t, :]).then_inc(s_mv.handle, 1)


def norm_sd_act(act, g, s_mv, s_sd):
    act.wait_ge(s_mv.handle, s_mv.at(NT))
    act.activation(g.SD[:, :], g.MV[:, :, 1], ACT.Sqrt, bias=g.C[:, C_EPS:C_EPS + 1]).then_inc(s_sd.handle, 1)


def norm_rs_dve(dve, g, s_sd, s_rs):
    dve.wait_ge(s_sd.handle, s_sd.at(1))
    dve.reciprocal(g.RS[:, :], g.SD[:, :]).then_inc(s_rs.handle, 1)
    dve.wait_ge(s_rs.handle, s_rs.at(1))


def normalize(dve, g, out, t):
    return dve.tensor_scalar(out, g.X[:, t, :], g.MV[:, t, 0:1], g.RS[:, bass.ds(t, 1)], ALU.subtract, ALU.mult)


def load_stage(nc, g, dram):
    s_in = g.sem("loaded_x")
    s_c = g.sem("loaded_constants")
    s_z = g.sem("zeros_made")
    s_zd = g.sem("zero_tile_stored")
    with nc.Block() as block:
        @block.sync
        def _(sp):
            g.credit(sp)
            sp.dma_start(g.X[:, :, :], dram["x"].rearrange("(t p) d -> p t d", p=P)).then_inc(s_in.handle, 16)
            sp.dma_start(g.C[:, :], dram["const"]).then_inc(s_c.handle, 16)
            sp.wait_ge(s_z.handle, s_z.at(1))
            sp.dma_start(g.XG[NE * ROWS:NE * ROWS + P, :], g.Z[:, :]).then_inc(s_zd.handle, 16)
            sp.wait_ge(s_zd.handle, s_zd.at(16))
            sp.wait_ge(s_c.handle, s_c.at(16))

        @block.vector
        def _(dve):
            dve.memset(g.Z[:, :], 0.0).then_inc(s_z.handle, 1)
            dve.wait_ge(s_in.handle, s_in.at(16))
            with dve.Fori(0, NT) as t:
                dve.bn_stats(g.ST[:, t, :], g.X[:, t, :])


def moe_stage(nc, g, dram, rep):
    S = lambda name, each, **kind: g.sem("moe_" + name, each, rep, **kind)
    s_w2 = S("loaded_W2", 64)
    s_rw = S("loaded_router", 16)
    s_mv, s_sd, s_rs = S("stats", NT), S("deviations", 1), S("reciprocals", 1)
    s_xn, s_xtp, s_xtc = S("xn_tile", NT), S("xnT_in_psum", NT), S("xnT_copied", NT)
    s_lgp, s_lgc = S("logits_in_psum", NT), S("logits_copied", NB4)
    s_max, s_idx = S("top_values", NT), S("top_experts", NT)
    s_dve = S("routing_step", MOE_STEPS)
    s_gap, s_exp = S("gap", 1), S("gap_exp", 1)
    s_msk, s_sum, s_cnt, s_tot = S("mask", NB4), S("pairs_so_far", NB4), S("ranks_in_psum", NB4), S("totals_in_psum", 1)
    s_pos, s_ei, s_ri, s_po = S("slots", NB4), S("tile_experts", 1), S("tile_rows", 1), S("out_rows", 1)
    s_tz, s_zt = S("tail_rows", 1), S("tails_zeroed", 16 * NE)
    s_sc = S("rows_scattered", 32 * NT, pool_dma=True)
    s_xs = [S(f"slots_loaded{u}", 16 * (NTILE // 2 + 1)) for u in range(2)]
    s_tap, s_tac = S("slotsT_in_psum", NTILE + 2), S("slotsT_copied", NTILE + 2)
    s_h, s_hs = S("hidden_in_psum", NTILE), S("hidden", NTILE)
    s_thp, s_thc = S("hiddenT_in_psum", NTILE), S("hiddenT_copied", NTILE)
    s_y, s_yc = S("expert_out_in_psum", NTILE), S("expert_out_copied", NTILE)
    s_yd = S("expert_out_stored", 16 * NTILE)
    NQ = 8
    s_ga = [S(f"rows_gathered{q}", 32 * NT // NQ, pool_dma=True) for q in range(NQ)]
    s_add = S("first_added", NT)
    BT = NT // NB4
    AHEAD = 2

    with ExitStack() as ctx:
        sb = lambda name, shape, dt=F32: g.sb(ctx, f"moe{rep}_{name}", shape, dt)
        W2 = sb("W2", [P, NE, KF, D])
        RW = sb("RW", [P, KD, NE])
        XT = sb("XT", [P, BT, KD, P])
        LG = sb("LG", [P, NT, NE])
        M8 = sb("M8", [P, NT, 8])
        I8 = sb("I8", [P, NT, 8], U32)
        IF = sb("IF", [P, NT, 8])
        OH = sb("OH", [P, 2, NT, NE])
        MK = sb("MK", [P, NT, NE])
        MB = sb("MB", [P, NE])
        MS = sb("MS", [P, NB4 + 1, NE])
        BASE = sb("BASE", [P, NE])
        SL = sb("SL", [P, NT, NE])
        PT = sb("PT", [P, 2, NT, NE])
        PF = sb("PF", [P, 2, NT])
        PI, PO = sb("PI", [P, 2, NT], I32), sb("PO", [P, 2, NT], I32)
        NI = sb("NI", [P, NE], I32)
        NI2 = sb("NI2", [P, NE], I32)
        TE = sb("TE", [P, NE])
        TP = sb("TP", [P, 2, NE // 2 + NE])
        TZF, TZ = sb("TZF", [1, NE]), sb("TZ", [1, NE], I32)
        CM = sb("CM", [1, NTILE + 2, NE])
        EF, EC, ES, R1, R2, R3 = (sb(n, [1, NTILE + 2]) for n in ("EF", "EC", "ES", "R1", "R2", "R3"))
        EI, RI = (sb(n, [1, NTILE + 2], I32) for n in ("EI", "RI"))
        GP = sb("GP", [P, NT])
        GE = sb("GE", [P, NT])
        GS = sb("GS", [P, NT])
        GH = sb("GH", [P, 2, NT])
        GR = sb("GR", [P, NT])
        XS = sb("XS", [P, 2, D])
        ST = sb("ST", [P, 2, KD, P])
        HS = sb("HS", [P, 2, FF])
        HT = sb("HT", [P, 2, KF, P])
        YS = sb("YS", [P, 2, D])
        Y2 = sb("Y2", [P, 8, D])
        bank = g.bank

        def zero_tails(engine, first, end):
            engine.wait_ge(s_tz.handle, s_tz.at(1))
            with engine.Fori(first, end) as e:
                row = engine.value_load(TZ[0:1, bass.ds(e, 1)], min_val=0, max_val=NE * ROWS - P)
                engine.dma_start(g.XG[bass.ds(row, P), :], g.Z[:, :]).then_inc(s_zt.handle, 16)

        with nc.Block() as block:
            @block.sync
            def _(sp):
                g.credit(sp)
                sp.dma_start(RW[:, :, :], dram["router_w"]).then_inc(s_rw.handle, 16)
                for e in range(0, NE, 4):
                    if rep == 0:
                        sp.dma_start(g.W1[:, e:e + 4], dram["W1"][:, e:e + 4]).then_inc(g.s_w1.handle, 16)
                for e in range(0, NE, 4):
                    sp.dma_start(W2[:, e:e + 4], dram["W2"][:, e:e + 4]).then_inc(s_w2.handle, 16)
                zero_tails(sp, 0, NE // 2)
                sp.wait_ge(s_ri.handle, s_ri.at(1))
                sp.wait_ge(s_zt.handle, s_zt.at(16 * NE))
                sp.wait_ge(s_sc.handle, s_sc.at(32 * NT))

                def load_slots(u, j):
                    row = sp.value_load(RI[0:1, bass.ds(j, 1)], min_val=0, max_val=NE * ROWS)
                    sp.dma_start(XS[:, u, :], g.XG[bass.ds(row, P), :]).then_inc(s_xs[u].handle, 16)

                for u in range(2):
                    load_slots(u, u)
                with sp.Fori(0, NTILE // 2) as i:
                    for u in range(2):
                        sp.wait_ge(s_tap.handle, s_tap.at(2 * i + u + 1))
                        load_slots(u, 2 * i + u + 2)

            @block.vector
            def _(dve):
                n = [0]

                def then_wait(ins):
                    n[0] += 1
                    ins.then_inc(s_dve.handle, 1)
                    dve.wait_ge(s_dve.handle, s_dve.at(n[0]))

                norm_stats_dve(dve, g, s_mv)
                norm_rs_dve(dve, g, s_sd, s_rs)
                iota = g.C[:, C_IOTA:C_IOTA + NE]

                def normalized(b):
                    for t in range(BT * b, BT * (b + 1)):
                        normalize(dve, g, g.XN[:, t, :], t).then_inc(s_xn.handle, 1)

                def routed(b):
                    ts = slice(BT * b, BT * (b + 1))
                    dve.wait_ge(s_lgc.handle, s_lgc.at(b + 1))
                    for t in range(BT * b, BT * (b + 1)):
                        dve.max(M8[:, t, :], LG[:, t, :]).then_inc(s_max.handle, 1)
                    for t in range(BT * b, BT * (b + 1)):
                        dve.wait_ge(s_max.handle, s_max.at(t + 1))
                        dve.max_index(I8[:, t, :], M8[:, t, :], LG[:, t, :]).then_inc(s_idx.handle, 1)
                    dve.wait_ge(s_idx.handle, s_idx.at(BT * (b + 1)))
                    then_wait(dve.tensor_copy(IF[:, ts, :], I8[:, ts, :]))
                    for k in range(2):
                        then_wait(dve.tensor_tensor(OH[:, k, ts], bcast(iota, 1, BT), bcast(IF[:, ts, k], 2, NE), ALU.is_equal))
                    dve.tensor_tensor(MK[:, ts, :], OH[:, 0, ts], OH[:, 1, ts], ALU.add).then_inc(s_msk.handle, 1)
                    dve.wait_ge(s_msk.handle, s_msk.at(b + 1))
                    by_expert = MK[:, ts, :].rearrange("p t e -> p e t")
                    if b == 0:
                        dve.tensor_reduce(MS[:, 1, :], by_expert, AX_X, ALU.add).then_inc(s_sum.handle, 1)
                    else:
                        then_wait(dve.tensor_reduce(MB[:, :], by_expert, AX_X, ALU.add))
                        dve.wait_ge(s_sum.handle, s_sum.at(b))
                        dve.tensor_tensor(MS[:, b + 1, :], MS[:, b, :], MB[:, :], ALU.add).then_inc(s_sum.handle, 1)
                    dve.wait_ge(s_cnt.handle, s_cnt.at(b + 1))
                    then_wait(dve.tensor_tensor(SL[:, ts, :], bank(4 + b % 2)[:, 0:BT * NE].rearrange("p (t e) -> p t e", e=NE),
                                                bcast(BASE[:, :], 1, BT), ALU.add))
                    then_wait(dve.tensor_tensor(PT[:, :, ts], OH[:, :, ts], bcast(SL[:, ts, :], 1, 2), ALU.mult))
                    then_wait(dve.tensor_reduce(PF[:, :, ts], PT[:, :, ts], AX_X, ALU.add))
                    dve.tensor_copy(PI[:, :, ts], PF[:, :, ts]).then_inc(s_pos.handle, 1)

                then_wait(dve.tensor_scalar(BASE[:, :], iota, float(ROWS), None, ALU.mult))
                then_wait(dve.memset(TP[:, :, :], 0.0))
                for b in range(AHEAD):
                    normalized(b)
                for b in range(NB4):
                    routed(b)
                    if b + AHEAD < NB4:
                        normalized(b + AHEAD)

                dve.wait_ge(s_tot.handle, s_tot.at(1))
                totals = bank(6)[:, 0:NE]
                then_wait(dve.tensor_tensor(TZF[:, :], totals[0:1, :], BASE[0:1, :], ALU.add))
                dve.tensor_copy(TZ[:, :], TZF[:, :]).then_inc(s_tz.handle, 1)
                then_wait(dve.tensor_scalar(NI[:, :], totals, float(P - 1), None, ALU.add))
                then_wait(dve.tensor_scalar(NI2[:, :], NI[:, :], 7, None, ALU.arith_shift_right))
                then_wait(dve.tensor_copy(TE[:, :], NI2[:, :]))
                pad = NE // 2
                then_wait(dve.tensor_copy(TP[:, 0, pad:], TE[:, :]))
                src, dist = 0, 1
                while dist < NE:
                    then_wait(dve.tensor_tensor(TP[:, 1 - src, pad:], TP[:, src, pad:], TP[:, src, pad - dist:pad - dist + NE], ALU.add))
                    src, dist = 1 - src, 2 * dist
                then_wait(dve.tensor_tensor(CM[:, :, :], bcast(TP[0:1, src, pad:], 1, NTILE + 2),
                                            bcast(g.C[0:1, C_TILE:C_TILE + NTILE + 2], 2, NE), ALU.is_le))
                then_wait(dve.tensor_reduce(EF[:, :], CM[:, :, :], AX_X, ALU.add))
                then_wait(dve.tensor_scalar(EC[:, :], EF[:, :], float(NE - 1), None, ALU.min))
                dve.tensor_copy(EI[:, :], EC[:, :]).then_inc(s_ei.handle, 1)
                then_wait(dve.tensor_tensor(CM[:, :, :], CM[:, :, :], bcast(TE[0:1, :], 1, NTILE + 2), ALU.mult))
                then_wait(dve.tensor_reduce(ES[:, :], CM[:, :, :], AX_X, ALU.add))
                then_wait(dve.tensor_tensor(R1[:, :], g.C[0:1, C_TILE:C_TILE + NTILE + 2], ES[:, :], ALU.subtract))
                then_wait(dve.tensor_scalar(R2[:, :], R1[:, :], float(P), None, ALU.mult))
                then_wait(dve.scalar_tensor_tensor(R3[:, :], EF[:, :], float(ROWS), R2[:, :], ALU.mult, ALU.add))
                then_wait(dve.tensor_scalar(R1[:, :], R3[:, :], float(NE * ROWS), None, ALU.min))
                dve.tensor_copy(RI[:, :], R1[:, :]).then_inc(s_ri.handle, 1)
                then_wait(dve.scalar_tensor_tensor(MB[:, :], TP[:, src, pad - 1:pad - 1 + NE], float(P), BASE[:, :], ALU.mult, ALU.subtract))
                then_wait(dve.tensor_tensor(SL[:, :, :], SL[:, :, :], bcast(MB[:, :], 1, NT), ALU.add))
                then_wait(dve.tensor_tensor(PT[:, :, :, :], OH[:, :, :, :], bcast(SL[:, :, :], 1, 2), ALU.mult))
                then_wait(dve.tensor_reduce(PF[:, :, :], PT[:, :, :, :], AX_X, ALU.add))
                dve.tensor_copy(PO[:, :, :], PF[:, :, :]).then_inc(s_po.handle, 1)
                dve.tensor_tensor(GP[:, :], M8[:, :, 1], M8[:, :, 0], ALU.subtract).then_inc(s_gap.handle, 1)
                dve.wait_ge(s_exp.handle, s_exp.at(1))
                then_wait(dve.tensor_scalar(GS[:, :], GE[:, :], 1.0, None, ALU.add))
                then_wait(dve.reciprocal(GR[:, :], GS[:, :]))
                then_wait(dve.tensor_scalar(GH[:, 0, :], GR[:, :], 0.5, None, ALU.mult))
                then_wait(dve.tensor_tensor(GH[:, 1, :], GH[:, 0, :], GE[:, :], ALU.mult))
                assert n[0] == MOE_STEPS, n[0]

                for u in range(2):
                    dve.wait_ge(s_tap.handle, s_tap.at(u + 1))
                    dve.tensor_copy(ST[:, u], bank(u)[:, 0:KD * P].rearrange("p (k s) -> p k s", s=P)).then_inc(s_tac.handle, 1)
                with dve.Fori(0, NTILE // 2) as i:
                    for u in range(2):
                        dve.wait_ge(s_thp.handle, s_thp.at(2 * i + u + 1))
                        dve.wait_ge(s_y.handle, s_y.at(2 * i))
                        dve.tensor_copy(HT[:, u], bank(4 + u)[:, :].rearrange("p (k s) -> p k s", s=P)).then_inc(s_thc.handle, 1)
                    for u in range(2):
                        dve.wait_ge(s_tap.handle, s_tap.at(2 * i + u + 3))
                        dve.wait_ge(s_h.handle, s_h.at(2 * i + u + 1))
                        dve.tensor_copy(ST[:, u], bank(u)[:, 0:KD * P].rearrange("p (k s) -> p k s", s=P)).then_inc(s_tac.handle, 1)
                per = NT // NQ
                for q in range(NQ):
                    dve.wait_ge(s_ga[q].handle, s_ga[q].at(32 * per))
                    with dve.Fori(q * per, (q + 1) * per) as t:
                        dve.scalar_tensor_tensor(g.X[:, t, :], g.XN[:, t, :], GH[:, 0, bass.ds(t, 1)], g.X[:, t, :],
                                                 ALU.mult, ALU.add).then_inc(s_add.handle, 1)
                    with dve.Fori(q * per, (q + 1) * per) as t:
                        dve.wait_ge(s_add.handle, s_add.at(t + 1))
                        ins = dve.scalar_tensor_tensor(g.X[:, t, :], Y2[:, t - q * per // 8 * 8, :], GH[:, 1, bass.ds(t, 1)],
                                                       g.X[:, t, :], ALU.mult, ALU.add)
                        ins.then_inc(g.s_second[rep].handle, 1)
                    with dve.Fori(q * per, (q + 1) * per) as t:
                        dve.wait_ge(g.s_second[rep].handle, g.s_second[rep].at(t + 1))
                        dve.bn_stats(g.ST[:, t, :], g.X[:, t, :])

            @block.scalar
            def _(act):
                norm_sd_act(act, g, s_mv, s_sd)
                for t in range(NT):
                    act.wait_ge(s_xtp.handle, s_xtp.at(t + 1))
                    if t >= BT:
                        act.wait_ge(s_lgp.handle, s_lgp.at(t - BT + 1))
                    act.copy(XT[:, t % BT], bank(t % 2)[:, 0:KD * P].rearrange("p (k s) -> p k s", s=P)).then_inc(s_xtc.handle, 1)
                    if t % BT == BT - 1:
                        b = t // BT
                        act.wait_ge(s_lgp.handle, s_lgp.at(t + 1))
                        act.copy(LG[:, t - BT + 1:t + 1, :].rearrange("p t e -> p (t e)"), bank(2 + b % 2)[:, 0:BT * NE]).then_inc(s_lgc.handle, 1)
                nc.scalar.preload_act_table(ACT.Exp)
                zero_tails(act, NE // 2, NE)
                act.wait_ge(s_gap.handle, s_gap.at(1))
                act.activation(GE[:, :], GP[:, :], ACT.Exp).then_inc(s_exp.handle, 1)
                nc.scalar.preload_act_table(ACT.Silu)
                with act.Fori(0, NTILE // 2) as i:
                    for u in range(2):
                        act.wait_ge(s_h.handle, s_h.at(2 * i + u + 1))
                        act.wait_ge(s_thp.handle, s_thp.at(2 * i))
                        act.activation(HS[:, u, :], bank(2 + u)[:, :], ACT.Silu).then_inc(s_hs.handle, 1)
                    for u in range(2):
                        act.wait_ge(s_y.handle, s_y.at(2 * i + u + 1))
                        act.wait_ge(s_yd.handle, s_yd.at(32 * i))
                        act.copy(YS[:, u, :], bank(6 + u)[:, 0:D]).then_inc(s_yc.handle, 1)
                        act.wait_ge(s_yc.handle, s_yc.at(2 * i + u + 1))
                        act.dma_start(g.YG[bass.ds((2 * i + u) * P, P), :], YS[:, u, :]).then_inc(s_yd.handle, 16)

            @block.tensor
            def _(pe):
                ident = g.C[:, C_ID:C_ID + P]
                tri, one = g.C[:, C_TRI:C_TRI + P], g.C[:, C_ONE:C_ONE + P]
                pe.wait_ge(s_rw.handle, s_rw.at(16))

                def logits_of(t):
                    b = t // BT
                    pe.wait_ge(s_xtc.handle, s_xtc.at(t + 1))
                    if t % BT == 0 and b >= 2:
                        pe.wait_ge(s_lgc.handle, s_lgc.at(b - 1))
                    for k in range(KD):
                        ins = pe.matmul(bank(2 + b % 2)[:, t % BT * NE:(t % BT + 1) * NE], XT[:, t % BT, k, :], RW[:, k, :], start=(k == 0), stop=(k == KD - 1))
                    ins.then_inc(s_lgp.handle, 1)

                def batch(b):
                    for t in range(BT * b, BT * (b + 1)):
                        pe.wait_ge(s_xn.handle, s_xn.at(t + 1))
                        if t >= 2:
                            pe.wait_ge(s_xtc.handle, s_xtc.at(t - 1))
                        for k in range(KD):
                            ins = pe.transpose(bank(t % 2)[:, k * P:(k + 1) * P], g.XN[:, t, k * P:(k + 1) * P], ident)
                        ins.then_inc(s_xtp.handle, 1)
                        if t % BT:
                            logits_of(t - 1)
                    logits_of(BT * b + BT - 1)

                def ranks(b):
                    pe.wait_ge(s_msk.handle, s_msk.at(b + 1))
                    if b:
                        pe.wait_ge(s_sum.handle, s_sum.at(b))
                    if b >= 2:
                        pe.wait_ge(s_pos.handle, s_pos.at(b - 1))
                    out = bank(4 + b % 2)[:, 0:BT * NE].rearrange("p (t e) -> p t e", e=NE)
                    pe.matmul(out, tri, MK[:, BT * b:BT * (b + 1), :], start=True, stop=False)
                    if b:
                        pe.matmul(out, one, bcast(MS[:, b, :], 1, BT), start=False, stop=False)
                    for a in range(BT - 1):
                        ins = pe.matmul(out[:, a + 1:BT, :], one, bcast(MK[:, BT * b + a, :], 1, BT - 1 - a), start=False, stop=(a == BT - 2))
                    ins.then_inc(s_cnt.handle, 1)

                for b in range(AHEAD):
                    batch(b)
                for b in range(NB4):
                    ranks(b)
                    if b + AHEAD < NB4:
                        batch(b + AHEAD)
                pe.wait_ge(s_sum.handle, s_sum.at(NB4))
                pe.matmul(bank(6)[:, 0:NE], one, MS[:, NB4, :], start=True, stop=True).then_inc(s_tot.handle, 1)

                pe.wait_ge(g.s_w1.handle, g.s_w1.at(64))
                pe.wait_ge(s_w2.handle, s_w2.at(64))
                pe.wait_ge(s_ei.handle, s_ei.at(1))

                def slots_t(u, j, loads):
                    pe.wait_ge(s_xs[u].handle, s_xs[u].at(16 * loads))
                    for k in range(KD):
                        ins = pe.transpose(bank(u)[:, k * P:(k + 1) * P], XS[:, u, k * P:(k + 1) * P], ident)
                    ins.then_inc(s_tap.handle, 1)

                slots_t(0, 0, 1)
                slots_t(1, 1, 1)
                with pe.Fori(0, NTILE // 2) as i:
                    experts = [pe.value_load(EI[0:1, bass.ds(2 * i + u, 1)], min_val=0, max_val=NE - 1) for u in range(2)]
                    for u in range(2):
                        pe.wait_ge(s_tac.handle, s_tac.at(2 * i + u + 1))
                        pe.wait_ge(s_hs.handle, s_hs.at(2 * i))
                        for k in range(KD):
                            ins = pe.matmul(bank(2 + u)[:, :], ST[:, u, k, :], g.W1[:, experts[u], k, :], start=(k == 0), stop=(k == KD - 1))
                        ins.then_inc(s_h.handle, 1)
                    for u in range(2):
                        pe.wait_ge(s_hs.handle, s_hs.at(2 * i + u + 1))
                        pe.wait_ge(s_thc.handle, s_thc.at(2 * i))
                        for k in range(KF):
                            ins = pe.transpose(bank(4 + u)[:, k * P:(k + 1) * P], HS[:, u, k * P:(k + 1) * P], ident)
                        ins.then_inc(s_thp.handle, 1)
                    for u in range(2):
                        slots_t(u, 2 * i + u + 2, i + 2)
                    for u in range(2):
                        pe.wait_ge(s_thc.handle, s_thc.at(2 * i + u + 1))
                        pe.wait_ge(s_yc.handle, s_yc.at(2 * i))
                        for k in range(KF):
                            ins = pe.matmul(bank(6 + u)[:, 0:D], HT[:, u, k, :], W2[:, experts[u], k, :], start=(k == 0), stop=(k == KF - 1))
                        ins.then_inc(s_y.handle, 1)

            @block.gpsimd
            def _(pool):
                for t in range(NT):
                    if t % BT == 0:
                        pool.wait_ge(s_pos.handle, s_pos.at(t // BT + 1))
                        pool.wait_ge(s_xn.handle, s_xn.at(t + BT))
                    for k in range(2):
                        pool.indirect_dma_start(g.XG, bass.IndirectOffsetOnAxis(PI[:, k, t:t + 1], 0),
                                                g.XN[:, t, :], None).then_inc(s_sc.handle, 16)
                pool.wait_ge(s_po.handle, s_po.at(1))
                pool.wait_ge(s_yd.handle, s_yd.at(16 * NTILE))
                per = NT // NQ
                for t in range(NT):
                    if t >= NT // 2:
                        pool.wait_ge(g.s_second[rep].handle, g.s_second[rep].at(t - NT // 2 + 1))
                    q = t // per
                    pool.indirect_dma_start(g.XN[:, t, :], None, g.YG, bass.IndirectOffsetOnAxis(PO[:, 0, t:t + 1], 0)).then_inc(s_ga[q].handle, 16)
                    pool.indirect_dma_start(Y2[:, t % 8, :], None, g.YG, bass.IndirectOffsetOnAxis(PO[:, 1, t:t + 1], 0)).then_inc(s_ga[q].handle, 16)


def attention_stage(nc, g, dram):
    S = lambda name, **kind: g.sem("att_" + name, **kind)
    s_w, s_fill, s_fill2 = S("weights"), S("filled"), S("ones_filled")
    s_mv, s_sd, s_rs = (g.sem("att_" + n) for n in ("stats", "deviations", "reciprocals"))
    s_xn, s_xtp, s_xtc = S("xn_tile"), S("xnT_in_psum"), S("xnT_copied")
    s_pr, s_hi, s_rows = S("qkv_in_psum"), S("high_parts"), S("low_parts")
    s_qkp, s_qc, s_kc = S("qkT_in_psum"), S("qT_copied"), S("kT_copied")
    s_suf = S("later_values")
    s_sc, s_mask, s_mx, s_nb = S("scores"), S("masked"), S("row_max"), S("negative_max")
    s_p, s_e0 = S("probs"), S("later_weight")
    s_ptp, s_ptc = S("probsT_in_psum"), S("probsT_copied")
    s_ot, s_otc, s_bt = S("outT_in_psum"), S("outT_copied"), S("out_in_psum")
    s_part, s_sum, s_den, s_out = S("later_part"), S("out_sum"), S("out_denominator"), S("out_rows")
    s_aop, s_aoc, s_wo, s_x = S("outrowsT_in_psum"), S("outrowsT_copied"), S("projected"), S("x_updated")

    NU = TB * HG
    chunks = []
    for n in range(NU):
        nk = n // HG + 1
        chunks += [(n, c, min(4, nk - c)) for c in range(0, nk, 4)]
    NC = len(chunks)
    first_chunk = [next(c for c, ch in enumerate(chunks) if ch[0] == n) for n in range(NU)] + [NC]
    NS = TB - 2

    steps = {}
    for j in range(TB):
        unit = max(HG + 3 * j, HG * j)
        steps[unit] = ("projections", j)
        steps[unit + 1] = ("transposes", j)
        assert unit + 1 >= HG * j + 1
    assert len(steps) == 2 * TB and max(steps) < NU - 2

    NARROW = HG * 4
    ahead = {n: [n + 3] for n in range(1, NARROW - 3)} | {n: [n + 2] for n in range(NARROW - 2, NU - 2)}
    ahead[NU - 2], ahead[NU - 1] = [NU, NU + 1], [NU + 2, NU + 3]

    def scores_read_before(n):
        if n < HG:
            return n // 2 - 1
        if n < NARROW + 2:
            return n - 3 if n < NARROW else 2 * n - NARROW - 2
        return n - 1

    with ExitStack() as ctx:
        sb = lambda name, shape, dt=F32: g.sb(ctx, "att_" + name, shape, dt)
        WQ = sb("Wqkv", [P, KD, NG0 * 3 * HG * DH0])
        WO = sb("Wo", [P, KD, D])
        XNS = sb("XNS", [P, 2, D])
        QS = sb("QS", [P, 2, HG * 64])
        KS = sb("KS", [P, 2, HG * 64])
        QT = sb("QT", [P, 2, 2, SEQ], F32R)
        KT = sb("KT", [P, 2, 2, SEQ], F32R)
        VV = sb("VV", [P, 2, TB, HG * VW])
        VS = sb("VS", [P, 2, NS, HG * VW])
        PR = sb("PR", [P, 2, SEQ])
        PT = sb("PT", [P, 2, HG, TB, P])
        MX, MY = sb("MX", [P, NU]), sb("MY", [P, NU])
        NB = sb("NB", [P, NU])
        E0 = sb("E0", [P, 2, HG])
        OT = sb("OT", [P, P])
        F1 = sb("F1", [P, HG * VW])
        F2 = sb("F2", [P, HG * VW])
        F3 = sb("F3", [P, HG])
        AT = sb("AT", [P, 2, KD, P])
        AO = g.XN[:, 0:TB, :]
        XT = g.XN[:, TB:2 * TB, :].rearrange("p (k a) d -> p k (a d)", k=KD)
        bank, banks = g.bank, g.banks
        ident = g.C[:, C_ID:C_ID + P]
        sc_bank = lambda n: n % 4 if n < NARROW else 2 * (n % 2)
        scores = lambda n, w: banks(sc_bank(n), (w + 511) // 512)[:, 0:w]
        slots = lambda rows, j: rows[:, j % 2, :].rearrange("p (h s d) -> p h s d", h=HG, s=4)
        v4 = lambda ap: ap.rearrange("p (h d) -> p h d", h=HG)
        pr_bank = lambda j, alone: bank(j % 2) if alone else bank(7)
        tr_bank = lambda j, alone: bank(2 + j % 2) if alone else bank(7)
        part = lambda j, alone, m: pr_bank(j, alone)[:, m * 64:(m + 1) * 64].rearrange("p (h d) -> p h d", h=HG)

        def groups_of_a_sequence(engine, b, group):
            group(b * NG0, 0, 0, True, False)
            with engine.Fori(0, NG0 // 2 - 1) as rr:
                group(b * NG0 + 2 * rr + 1, 2 * rr + 1, 1, False, False)
                group(b * NG0 + 2 * rr + 2, 2 * rr + 2, 0, False, False)
            group(b * NG0 + NG0 - 1, NG0 - 1, 1, False, True)

        with nc.Block() as block:
            @block.sync
            def _(sp):
                g.credit(sp)
                sp.dma_start(WQ[:, :, :], dram["Wqkv"]).then_inc(s_w.handle, 16)
                sp.dma_start(WO[:, :, :], dram["Wo"]).then_inc(s_w.handle, 16)
                sp.wait_ge(s_w.handle, s_w.at(32))

            @block.gpsimd
            def _(pool):
                for buf in range(2):
                    pool.memset(VV[:, buf], 0.0).then_inc(s_fill.handle, 1)
                pool.memset(QT[:, :, :, :].bitcast(F32), 0.0).then_inc(s_fill.handle, 1)
                pool.wait_ge(s_fill.handle, s_fill.at(3))
                pool.memset(VV[:, :, :, :].rearrange("p u j (h d) -> p (u j h) d", d=VW)[:, :, DH0:DH0 + 1], 1.0).then_inc(s_fill2.handle, 1)
                pool.wait_ge(s_fill2.handle, s_fill2.at(1))

                def later_values(it, buf):
                    pool.wait_ge(s_hi.handle, s_hi.at(3 * TB * (it + 1)))
                    pool.wait_ge(s_bt.handle, s_bt.at(TB * it))
                    for i in range(NS - 1, -1, -1):
                        later = VV[:, buf, TB - 1, :] if i == NS - 1 else VS[:, buf, i + 1, :]
                        if i < NS - 1:
                            pool.wait_ge(s_suf.handle, s_suf.at(NS * it + NS - 1 - i))
                        pool.tensor_tensor(VS[:, buf, i, :], later, VV[:, buf, i + 1, :], ALU.add).then_inc(s_suf.handle, 1)

                with pool.Fori(0, BATCH * NG0 // 2) as r:
                    for buf in range(2):
                        later_values(2 * r + buf, buf)

            @block.tensor
            def _(pe):
                pe.wait_ge(s_w.handle, s_w.at(32))
                with pe.Fori(0, BATCH) as b:
                    def xn_transposes(j):
                        pe.wait_ge(s_xn.handle, s_xn.at(TB * b + j + 1))
                        if j >= 2:
                            pe.wait_ge(s_xtc.handle, s_xtc.at(TB * b + j - 1))
                        for k in range(KD):
                            ins = pe.transpose(bank(4 + j % 2)[:, k * P:(k + 1) * P], XNS[:, j % 2, k * P:(k + 1) * P], ident)
                        ins.then_inc(s_xtp.handle, 1)

                    def projections(it, gg, j, alone):
                        if not alone:
                            pe.wait_ge(s_kc.handle, s_kc.at(TB * it + j))
                        elif j >= 2:
                            pe.wait_ge(s_rows.handle, s_rows.at(2 * (TB * it + j - 1)))
                        if alone:
                            pe.wait_ge(s_xtc.handle, s_xtc.at(TB * b + j + 1))
                        for k in range(KD):
                            ins = pe.matmul(pr_bank(j, alone)[:, 0:3 * HG * DH0], XT[:, k, j * P:(j + 1) * P],
                                            WQ[:, k, bass.ds(gg * (3 * HG * DH0), 3 * HG * DH0)], start=(k == 0), stop=(k == KD - 1))
                        ins.then_inc(s_pr.handle, 1)

                    def transposes(it, j, alone):
                        pe.wait_ge(s_rows.handle, s_rows.at(2 * (TB * it + j + 1)))
                        if alone and j >= 2:
                            pe.wait_ge(s_kc.handle, s_kc.at(TB * it + j - 1))
                        for m, rows in enumerate((QS, KS)):
                            for r in range(2):
                                ins = pe.transpose(tr_bank(j, alone)[:, (2 * m + r) * P:(2 * m + r + 1) * P], rows[:, j % 2, r * P:(r + 1) * P], ident)
                        ins.then_inc(s_qkp.handle, 1)

                    for j in range(TB + 2):
                        if j < TB:
                            xn_transposes(j)
                        if 1 <= j <= TB:
                            projections(b * NG0, 0, j - 1, True)
                        if j >= 2:
                            transposes(b * NG0, j - 2, True)

                    def scores_of(it, n, buf, free):
                        if n == 0:
                            pe.wait_ge(s_kc.handle, s_kc.at(TB * (it + 1)))
                        if not free:
                            pe.wait_ge(s_p.handle, s_p.at(NU * it + scores_read_before(n)))
                        i, h = n // HG, n % HG
                        width = (i // 2 + 1) * 2 * P
                        for c in range(0, width, 512):
                            w = min(512, width - c)
                            ins = pe.matmul(bank(sc_bank(n) + c // 512)[:, 0:w], QT[:, h // 2, h % 2, i * P:(i + 1) * P],
                                            KT[:, buf, h // 2, c:c + w], start=True, stop=True)
                        ins.then_inc(s_sc.handle, 1)

                    def probs_transposes(it, n, first):
                        pe.wait_ge(s_p.handle, s_p.at(NU * it + n + 1))
                        for c in range(first_chunk[n], first_chunk[n + 1]):
                            _, k0, nk = chunks[c]
                            if c >= 2 or not first:
                                pe.wait_ge(s_ptc.handle, s_ptc.at(NC * it + c - 1))
                            for k in range(nk):
                                ins = pe.transpose(bank(4 + c % 2)[:, k * P:(k + 1) * P], PR[:, n % 2, (k0 + k) * P:(k0 + k + 1) * P], ident)
                            ins.then_inc(s_ptp.handle, 1)

                    def values_of(it, i, buf, keys, free):
                        for k in keys:
                            if k == 0:
                                pe.wait_ge(s_ptc.handle, s_ptc.at(NC * it + first_chunk[HG * (i + 1)]))
                                if not free:
                                    pe.wait_ge(s_sum.handle, s_sum.at(TB * it + i))
                            for h in range(HG):
                                ins = pe.matmul(bank(6)[h * VW:(h + 1) * VW, 0:P], VV[:, buf, k, h * VW:(h + 1) * VW],
                                                PT[:, i % 2, h, k, :], start=(k == 0), stop=(k == i))
                            if k == i:
                                ins.then_inc(s_ot.handle, 1)

                    def out_rows_of(it, i, buf):
                        pe.wait_ge(s_otc.handle, s_otc.at(TB * it + i + 1))
                        if i < TB - 1:
                            pe.wait_ge(s_suf.handle, s_suf.at(NS * (it + 1)))
                            later = VS[:, buf, i, :] if i < NS else VV[:, buf, TB - 1, :]
                            pe.matmul(bank(6)[:, 2 * P:3 * P], g.C[:, C_ONE:C_ONE + P], later, start=True, stop=True)
                        pe.transpose(bank(6)[:, P:2 * P], OT[:, :], ident).then_inc(s_bt.handle, 1)

                    def group(it, gg, buf, first, last):
                        if first:
                            for m in range(HG):
                                scores_of(it, m, buf, True)
                        for n in range(NU):
                            if n == NU - 2:
                                probs_transposes(it, n, first)
                            for m in ahead.get(n, []):
                                if m < NU:
                                    scores_of(it, m, buf, False)
                                elif not last:
                                    scores_of(it + 1, m - NU, 1 - buf, False)
                            if n != NU - 2:
                                probs_transposes(it, n, first)
                            if n in steps and not last:
                                what, j = steps[n]
                                if what == "projections":
                                    projections(it + 1, gg + 1, j, False)
                                else:
                                    transposes(it + 1, j, False)
                            i, h = n // HG, n % HG
                            if h:
                                if i:
                                    values_of(it, i - 1, buf, [k for k in range(i) if k * (HG - 1) // i == h - 1], first and i == 1)
                                elif not first:
                                    values_of(it - 1, TB - 1, 1 - buf, [k for k in range(TB) if k * (HG - 1) // TB == h - 1], False)
                            elif i >= 2:
                                out_rows_of(it, i - 2, buf)
                            elif not first:
                                out_rows_of(it - 1, TB - 2 + i, 1 - buf)
                        if last:
                            out_rows_of(it, TB - 2, buf)
                            values_of(it, TB - 1, buf, range(TB), False)
                            out_rows_of(it, TB - 1, buf)

                    groups_of_a_sequence(pe, b, group)

                    def rows_t(i):
                        if i >= 2:
                            pe.wait_ge(s_aoc.handle, s_aoc.at(TB * b + i - 1))
                        for k in range(KD):
                            ins = pe.transpose(bank(4 + i % 2)[:, k * P:(k + 1) * P], AO[:, i, k * P:(k + 1) * P], ident)
                        ins.then_inc(s_aop.handle, 1)

                    pe.wait_ge(s_out.handle, s_out.at(TB * NG0 * (b + 1)))
                    rows_t(0)
                    for i in range(TB):
                        if i + 1 < TB:
                            rows_t(i + 1)
                        pe.wait_ge(s_aoc.handle, s_aoc.at(TB * b + i + 1))
                        if i >= 2:
                            pe.wait_ge(s_x.handle, s_x.at(TB * b + i - 1))
                        for k in range(KD):
                            ins = pe.matmul(bank(i % 2)[:, 0:D], AT[:, i % 2, k, :], WO[:, k, :], start=(k == 0), stop=(k == KD - 1))
                        ins.then_inc(s_wo.handle, 1)
                    pe.wait_ge(s_x.handle, s_x.at(TB * (b + 1)))

            @block.scalar
            def _(act):
                norm_sd_act(act, g, s_mv, s_sd)
                nc.scalar.preload_act_table(ACT.Exp)
                with act.Fori(0, BATCH) as b:
                    def xt_copy(j):
                        act.wait_ge(s_xtp.handle, s_xtp.at(TB * b + j + 1))
                        act.copy(XT[:, :, j * P:(j + 1) * P], bank(4 + j % 2)[:, 0:KD * P].rearrange("p (k s) -> p k s", s=P)).then_inc(s_xtc.handle, 1)

                    def highs(it, buf, j, alone):
                        act.wait_ge(s_pr.handle, s_pr.at(TB * it + j + 1))
                        if j >= 2:
                            act.wait_ge(s_qkp.handle, s_qkp.at(TB * it + j - 1))
                        act.copy(slots(QS, j)[:, :, 0:4:2, :].bitcast(F32R), bcast(part(j, alone, 0), 2, 2)).then_inc(s_hi.handle, 1)
                        act.copy(slots(KS, j)[:, :, 0:2, :].bitcast(F32R), bcast(part(j, alone, 1), 2, 2)).then_inc(s_hi.handle, 1)
                        act.copy(v4(VV[:, buf, j, :])[:, :, 0:DH0], part(j, alone, 2)).then_inc(s_hi.handle, 1)

                    def q_copies(it, j, alone):
                        act.wait_ge(s_qkp.handle, s_qkp.at(TB * it + j + 1))
                        for m in range(2):
                            act.copy(QT[m * 64:(m + 1) * 64, :, m, j * P:(j + 1) * P],
                                     tr_bank(j, alone)[m * 64:(m + 1) * 64, 0:2 * P].rearrange("p (r s) -> p r s", r=2)).then_inc(s_qc.handle, 1)

                    for j in range(TB + 2):
                        if j < TB:
                            xt_copy(j)
                        if j == 1:
                            act.wait_ge(s_fill.handle, s_fill.at(3))
                            act.wait_ge(s_fill2.handle, s_fill2.at(1))
                        if 1 <= j <= TB:
                            highs(b * NG0, 0, j - 1, True)
                        if j >= 2:
                            q_copies(b * NG0, j - 2, True)

                    def exp_of(it, n, free):
                        i, w = n // HG, (n // HG + 1) * P
                        act.wait_ge(s_nb.handle, s_nb.at(NU * it + n + 1))
                        if not free:
                            act.wait_ge(s_ptp.handle, s_ptp.at(NC * it + (first_chunk[n - 1] if n else 0)))
                        act.activation(PR[:, n % 2, 0:w], scores(n, w), ACT.Exp, bias=NB[:, n:n + 1], scale=SEQ ** -0.5).then_inc(s_p.handle, 1)
                        if n % HG == HG - 1 and i < TB - 1:
                            act.wait_ge(s_part.handle, s_part.at((TB - 1) * it + max(i - 1, 0)))
                            act.activation(E0[:, i % 2, :], NB[:, HG * i:HG * i + HG], ACT.Exp).then_inc(s_e0.handle, 1)

                    def group(it, gg, buf, first, last):
                        if first:
                            exp_of(it, 0, True)
                        for n in range(NU):
                            if n + 1 < NU:
                                exp_of(it, n + 1, first and n == 0)
                            elif not last:
                                exp_of(it + 1, 0, False)
                            i, h = n // HG, n % HG
                            for c in range(first_chunk[n], first_chunk[n + 1]):
                                _, k0, nk = chunks[c]
                                act.wait_ge(s_ptp.handle, s_ptp.at(NC * it + c + 1))
                                if h == 0 and k0 == 0 and (i >= 2 or not first):
                                    act.wait_ge(s_ot.handle, s_ot.at(TB * it + i - 1))
                                act.copy(PT[:, i % 2, h, k0:k0 + nk, :], bank(4 + c % 2)[:, 0:nk * P].rearrange("p (k s) -> p k s", s=P)).then_inc(s_ptc.handle, 1)
                            if n in steps and not last:
                                what, j = steps[n]
                                if what == "projections":
                                    highs(it + 1, 1 - buf, j, False)
                                else:
                                    q_copies(it + 1, j, False)

                    groups_of_a_sequence(act, b, group)

                    for i in range(TB):
                        act.wait_ge(s_aop.handle, s_aop.at(TB * b + i + 1))
                        if i >= 2:
                            act.wait_ge(s_wo.handle, s_wo.at(TB * b + i - 1))
                        act.copy(AT[:, i % 2], bank(4 + i % 2)[:, 0:KD * P].rearrange("p (k s) -> p k s", s=P)).then_inc(s_aoc.handle, 1)

            @block.vector
            def _(dve):
                norm_stats_dve(dve, g, s_mv)
                norm_rs_dve(dve, g, s_sd, s_rs)
                with dve.Fori(0, BATCH) as b:
                    def normalized(j):
                        if j >= 2:
                            dve.wait_ge(s_xtp.handle, s_xtp.at(TB * b + j - 1))
                        normalize(dve, g, XNS[:, j % 2, :], b * TB + j).then_inc(s_xn.handle, 1)

                    def lows(it, j, alone):
                        dve.wait_ge(s_hi.handle, s_hi.at(3 * (TB * it + j + 1)))
                        qs, ks = slots(QS, j), slots(KS, j)
                        dve.tensor_tensor(qs[:, :, 1:4:2, :], bcast(part(j, alone, 0), 2, 2), qs[:, :, 0:4:2, :], ALU.subtract).then_inc(s_rows.handle, 1)
                        dve.tensor_tensor(ks[:, :, 2:4, :], bcast(part(j, alone, 1), 2, 2), ks[:, :, 0:2, :], ALU.subtract).then_inc(s_rows.handle, 1)

                    def k_copy(it, buf, j, alone):
                        dve.wait_ge(s_qc.handle, s_qc.at(2 * (TB * it + j + 1)))
                        dve.tensor_copy(KT[:, buf, :, j * P:(j + 1) * P], tr_bank(j, alone)[:, 2 * P:4 * P].rearrange("p (r s) -> p r s", r=2)).then_inc(s_kc.handle, 1)

                    normalized(0)
                    for j in range(TB + 2):
                        if j + 1 < TB:
                            normalized(j + 1)
                        if 1 <= j <= TB:
                            lows(b * NG0, j - 1, True)
                        if j >= 2:
                            k_copy(b * NG0, 0, j - 2, True)

                    def max_of(it, n):
                        i, w = n // HG, (n // HG + 1) * P
                        dve.wait_ge(s_sc.handle, s_sc.at(NU * it + n + 1))
                        diag = scores(n, w)[:, i * P:w]
                        low, floor = g.C[:, C_LOW:C_LOW + P], 0.0 if i < TB - 1 else LEAST
                        if i:
                            dve.tensor_reduce(MY[:, n:n + 1], scores(n, w)[:, 0:i * P], AX_X, ALU.max).then_inc(s_mx.handle, 1)
                            dve.tensor_tensor_reduce(diag, diag, low, 1.0, floor, ALU.mult, ALU.max, MX[:, n:n + 1]).then_inc(s_mask.handle, 1)
                        else:
                            dve.tensor_tensor(diag, diag, low, ALU.mult).then_inc(s_mask.handle, 1)
                            dve.wait_ge(s_mask.handle, s_mask.at(NU * it + n + 1))
                            dve.tensor_reduce(MX[:, n:n + 1], diag, AX_X, ALU.max).then_inc(s_mx.handle, 1)

                    def negative_max(it, n):
                        i = n // HG
                        dve.wait_ge(s_mx.handle, s_mx.at(NU * it + n + 1))
                        dve.wait_ge(s_mask.handle, s_mask.at(NU * it + n + 1))
                        other = MY[:, n:n + 1] if i else 0.0
                        dve.tensor_scalar(NB[:, n:n + 1], MX[:, n:n + 1], other, -(SEQ ** -0.5), ALU.max, ALU.mult).then_inc(s_nb.handle, 1)

                    def maxima(it, first_n, ms, finish_last):
                        pending = first_n
                        for m in ms:
                            g_it, n = (it, m) if m < NU else (it + 1, m - NU)
                            max_of(g_it, n)
                            if pending is not None:
                                negative_max(*pending)
                            pending = (g_it, n)
                        if pending is not None and finish_last:
                            negative_max(*pending)
                            pending = None
                        return pending

                    def out_copy(it, i):
                        dve.wait_ge(s_ot.handle, s_ot.at(TB * it + i + 1))
                        dve.tensor_copy(OT[:, :], bank(6)[:, 0:P]).then_inc(s_otc.handle, 1)

                    def finish(it, gg, i):
                        dve.wait_ge(s_bt.handle, s_bt.at(TB * it + i + 1))
                        if i < TB - 1:
                            dve.wait_ge(s_e0.handle, s_e0.at((TB - 1) * it + i + 1))
                            dve.tensor_tensor(v4(F1[:, :]), v4(bank(6)[:, 2 * P:3 * P]), bcast(E0[:, i % 2, :], 2, VW), ALU.mult).then_inc(s_part.handle, 1)
                            dve.wait_ge(s_part.handle, s_part.at((TB - 1) * it + i + 1))
                            dve.tensor_tensor(F2[:, :], bank(6)[:, P:2 * P], F1[:, :], ALU.add).then_inc(s_sum.handle, 1)
                        else:
                            dve.tensor_copy(F2[:, :], bank(6)[:, P:2 * P]).then_inc(s_sum.handle, 1)
                        dve.wait_ge(s_sum.handle, s_sum.at(TB * it + i + 1))
                        dve.reciprocal(F3[:, :], v4(F2[:, :])[:, :, DH0]).then_inc(s_den.handle, 1)
                        dve.wait_ge(s_den.handle, s_den.at(TB * it + i + 1))
                        out = AO[:, i, bass.ds(gg * (HG * DH0), HG * DH0)]
                        dve.tensor_tensor(v4(out), v4(F2[:, :])[:, :, 0:DH0], bcast(F3[:, :], 2, DH0), ALU.mult).then_inc(s_out.handle, 1)

                    def group(it, gg, buf, first, last):
                        if first:
                            maxima(it, None, range(HG), True)
                        pending = None
                        for n in range(NU):
                            i, h = n // HG, n % HG
                            ends = h == 0 and (i >= 2 or not first)
                            which = (it, gg, i - 2) if i >= 2 else (it - 1, gg - 1, TB - 2 + i)
                            if ends:
                                out_copy(which[0], which[2])
                            ms = [m for m in ahead.get(n, []) if m < NU or not last]
                            pending = maxima(it, pending, ms, not (n + 1 in ahead and n + 4 < NARROW))
                            if n in steps and not last:
                                what, j = steps[n]
                                if what == "projections":
                                    lows(it + 1, j, False)
                                else:
                                    k_copy(it + 1, 1 - buf, j, False)
                            if ends:
                                finish(*which)
                        if last:
                            for i in (TB - 2, TB - 1):
                                out_copy(it, i)
                                finish(it, gg, i)

                    groups_of_a_sequence(dve, b, group)

                    for i in range(TB):
                        dve.wait_ge(s_wo.handle, s_wo.at(TB * b + i + 1))
                        xt = g.X[:, b * TB + i, :]
                        dve.tensor_tensor(xt, bank(i % 2)[:, 0:D], xt, ALU.add).then_inc(s_x.handle, 1)
                        dve.wait_ge(s_x.handle, s_x.at(TB * b + i + 1))
                        dve.bn_stats(g.ST[:, b * TB + i, :], xt)


def lora_stage(nc, g, dram, rep):
    S = lambda name, each: g.sem("lora_" + name, each, rep)
    s_w = S("weights", 64)
    s_mv, s_sd, s_rs = S("stats", NT), S("deviations", 1), S("reciprocals", 1)
    s_xn, s_xtp, s_xtc = S("xn_tile", NT), S("xnT_in_psum", NT), S("xnT_copied", NT)
    s_pr, s_mid, s_hb, s_bias = S("mids_in_psum", NT), S("mids_copied", NT), S("half_bias", 1), S("bias_added", NT)
    s_step, s_max, s_idx, s_e = S("routing_step", LORA_STEPS), S("top_probs", NT), S("top_experts", NT), S("exps", 2)
    s_gm, s_mtp, s_mtc, s_lo, s_x = S("gated", NT), S("midsT_in_psum", NT), S("midsT_copied", NT), S("outputs", NT), S("x_updated", NT)
    NL = LE * LR + LE
    NR = 4
    HT = NT // 2
    with ExitStack() as ctx:
        sb = lambda name, shape, dt=F32: g.sb(ctx, f"lora{rep}_{name}", shape, dt)
        WB, WL, BL, BI = sb("Wbase", [P, KD, D]), sb("Wlora", [P, KD, NL]), sb("B", [P, D]), sb("biases", [P, D + LE])
        XN, XT, HB = sb("XN", [P, NR, D]), sb("XT", [P, NT, KD, P]), sb("HB", [P, D])
        ML, LG = sb("ML", [P, NT, NL]), sb("LG", [P, NT, LE])
        MX, SH, EX, SM, RC, PB = sb("MX", [P, NT]), sb("SH", [P, NT, LE]), sb("EX", [P, NT, LE]), sb("SM", [P, NT]), sb("RC", [P, NT]), sb("PB", [P, NT, LE])
        M8, I8, IF = sb("M8", [P, NT, 8]), sb("I8", [P, NT, 8], U32), sb("IF", [P, NT, 8])
        OH, G1, G2, TS, TR, GT = sb("OH", [P, 2, NT, LE]), sb("G1", [P, NT, LE]), sb("G2", [P, NT, LE]), sb("TS", [P, NT]), sb("TR", [P, NT]), sb("GT", [P, NT, LE])
        GM, MT = sb("GM", [P, NR, LE * LR]), sb("MT", [P, NR, P])
        bank = g.bank
        ident = g.C[:, C_ID:C_ID + P]
        with nc.Block() as block:
            @block.sync
            def _(sp):
                g.credit(sp)
                sp.dma_start(WL[:, :, :], dram["Wlora"]).then_inc(s_w.handle, 16)
                sp.dma_start(WB[:, :, :], dram["Wbase"]).then_inc(s_w.handle, 16)
                sp.dma_start(BL[:, :], dram["Blora"]).then_inc(s_w.handle, 16)
                sp.dma_start(BI[:, :], dram["biases"].to_broadcast([P, D + LE])).then_inc(s_w.handle, 16)
                sp.wait_ge(s_w.handle, s_w.at(64))

            @block.gpsimd
            def _(pool):
                pool.wait_ge(s_hb.handle, s_hb.at(1))
                for t in range(NT):
                    pool.wait_ge(s_xn.handle, s_xn.at(t + 1))
                    pool.tensor_tensor(g.X[:, t, :], g.X[:, t, :], HB[:, :], ALU.add).then_inc(s_bias.handle, 1)

            @block.tensor
            def _(pe):
                pe.wait_ge(s_w.handle, s_w.at(64))

                def mids_of(t):
                    pe.wait_ge(s_xtc.handle, s_xtc.at(t + 1))
                    if t >= 2:
                        pe.wait_ge(s_mid.handle, s_mid.at(t - 1))
                    for k in range(KD):
                        ins = pe.matmul(bank(2 + t % 2)[:, 0:NL], XT[:, t, k, :], WL[:, k, :], start=(k == 0), stop=(k == KD - 1))
                    ins.then_inc(s_pr.handle, 1)

                for t in range(NT):
                    pe.wait_ge(s_xn.handle, s_xn.at(t + 1))
                    if t >= 2:
                        pe.wait_ge(s_xtc.handle, s_xtc.at(t - 1))
                    for k in range(KD):
                        ins = pe.transpose(bank(t % 2)[:, k * P:(k + 1) * P], XN[:, t % NR, k * P:(k + 1) * P], ident)
                    ins.then_inc(s_xtp.handle, 1)
                    if t:
                        mids_of(t - 1)
                mids_of(NT - 1)

                def base(t):
                    if t >= NR:
                        pe.wait_ge(s_x.handle, s_x.at(t - NR + 1))
                    for k in range(KD):
                        pe.matmul(bank(4 + t % NR)[:, 0:D], XT[:, t, k, :], WB[:, k, :], start=(k == 0), stop=False)

                def mids_t(t):
                    pe.wait_ge(s_gm.handle, s_gm.at(t + 1))
                    if t >= 2:
                        pe.wait_ge(s_mtc.handle, s_mtc.at(t - 1))
                    pe.transpose(bank(t % 2)[:, 0:P], GM[:, t % NR, :], ident).then_inc(s_mtp.handle, 1)

                for t in range(NR):
                    base(t)
                mids_t(0)
                for t in range(NT):
                    if t + 1 < NT:
                        mids_t(t + 1)
                    pe.wait_ge(s_mtc.handle, s_mtc.at(t + 1))
                    pe.matmul(bank(4 + t % NR)[:, 0:D], MT[:, t % NR, :], BL[:, :], start=False, stop=True).then_inc(s_lo.handle, 1)
                    if t and t + NR - 1 < NT:
                        base(t + NR - 1)

            @block.scalar
            def _(act):
                norm_sd_act(act, g, s_mv, s_sd)
                nc.scalar.preload_act_table(ACT.Exp)

                def exps(h):
                    act.wait_ge(s_step.handle, s_step.at(h * LORA_STEPS // 2 + 3))
                    act.activation(EX[:, h * HT:(h + 1) * HT, :], SH[:, h * HT:(h + 1) * HT, :], ACT.Exp).then_inc(s_e.handle, 1)

                def mids_copy(t):
                    act.wait_ge(s_pr.handle, s_pr.at(t + 1))
                    act.copy(ML[:, t, :], bank(2 + t % 2)[:, 0:NL]).then_inc(s_mid.handle, 1)

                for t in range(NT):
                    act.wait_ge(s_xtp.handle, s_xtp.at(t + 1))
                    act.copy(XT[:, t], bank(t % 2)[:, 0:KD * P].rearrange("p (k s) -> p k s", s=P)).then_inc(s_xtc.handle, 1)
                    if t:
                        mids_copy(t - 1)
                    if t == HT + 2:
                        exps(0)
                mids_copy(NT - 1)
                exps(1)
                for t in range(NT):
                    act.wait_ge(s_mtp.handle, s_mtp.at(t + 1))
                    if t >= NR:
                        act.wait_ge(s_lo.handle, s_lo.at(t - NR + 1))
                    act.copy(MT[:, t % NR, :], bank(t % 2)[:, 0:P]).then_inc(s_mtc.handle, 1)

            @block.vector
            def _(dve):
                norm_stats_dve(dve, g, s_mv)
                norm_rs_dve(dve, g, s_sd, s_rs)
                for t in range(NT):
                    if t >= NR:
                        dve.wait_ge(s_xtp.handle, s_xtp.at(t - NR + 1))
                    normalize(dve, g, XN[:, t % NR, :], t).then_inc(s_xn.handle, 1)
                    if t == 0:
                        dve.wait_ge(s_w.handle, s_w.at(64))
                        dve.tensor_scalar(HB[:, :], BI[:, 0:D], 0.5, None, ALU.mult).then_inc(s_hb.handle, 1)
                n = [0]

                def then_wait(ins):
                    n[0] += 1
                    ins.then_inc(s_step.handle, 1)
                    dve.wait_ge(s_step.handle, s_step.at(n[0]))

                def routed(h):
                    ts = slice(h * HT, (h + 1) * HT)
                    dve.wait_ge(s_mid.handle, s_mid.at((h + 1) * HT))
                    then_wait(dve.tensor_tensor(LG[:, ts, :], ML[:, ts, LE * LR:NL], bcast(BI[:, D:D + LE], 1, HT), ALU.add))
                    then_wait(dve.tensor_reduce(MX[:, ts], LG[:, ts, :], AX_X, ALU.max))
                    then_wait(dve.tensor_tensor(SH[:, ts, :], LG[:, ts, :], bcast(MX[:, ts], 2, LE), ALU.subtract))
                    dve.wait_ge(s_e.handle, s_e.at(h + 1))
                    then_wait(dve.tensor_reduce(SM[:, ts], EX[:, ts, :], AX_X, ALU.add))
                    then_wait(dve.reciprocal(RC[:, ts], SM[:, ts]))
                    then_wait(dve.tensor_tensor(PB[:, ts, :], EX[:, ts, :], bcast(RC[:, ts], 2, LE), ALU.mult))
                    for t in range(h * HT, (h + 1) * HT):
                        dve.max(M8[:, t, :], PB[:, t, :]).then_inc(s_max.handle, 1)
                    for t in range(h * HT, (h + 1) * HT):
                        dve.wait_ge(s_max.handle, s_max.at(t + 1))
                        dve.max_index(I8[:, t, :], M8[:, t, :], PB[:, t, :]).then_inc(s_idx.handle, 1)
                    dve.wait_ge(s_idx.handle, s_idx.at((h + 1) * HT))
                    then_wait(dve.tensor_copy(IF[:, ts, :], I8[:, ts, :]))
                    iota = bcast(g.C[:, C_IOTA:C_IOTA + LE], 1, HT)
                    for k in range(2):
                        then_wait(dve.tensor_tensor(OH[:, k, ts], iota, bcast(IF[:, ts, k], 2, LE), ALU.is_equal))
                    then_wait(dve.tensor_tensor(G1[:, ts, :], OH[:, 0, ts], bcast(M8[:, ts, 0], 2, LE), ALU.mult))
                    then_wait(dve.tensor_tensor(G2[:, ts, :], OH[:, 1, ts], bcast(M8[:, ts, 1], 2, LE), ALU.mult))
                    then_wait(dve.tensor_tensor(SH[:, ts, :], G1[:, ts, :], G2[:, ts, :], ALU.add))
                    then_wait(dve.tensor_tensor(TS[:, ts], M8[:, ts, 0], M8[:, ts, 1], ALU.add))
                    then_wait(dve.reciprocal(TR[:, ts], TS[:, ts]))
                    then_wait(dve.tensor_scalar(TS[:, ts], TR[:, ts], LORA_SCALE, None, ALU.mult))
                    then_wait(dve.tensor_tensor(GT[:, ts, :], SH[:, ts, :], bcast(TS[:, ts], 2, LE), ALU.mult))

                def gated(t):
                    if t >= NR:
                        dve.wait_ge(s_mtp.handle, s_mtp.at(t - NR + 1))
                    mid = ML[:, t, 0:LE * LR].rearrange("p (e r) -> p e r", r=LR)
                    dve.tensor_tensor(GM[:, t % NR, :].rearrange("p (e r) -> p e r", r=LR), mid, bcast(GT[:, t, :], 2, LR), ALU.mult).then_inc(s_gm.handle, 1)

                def updated(t):
                    dve.wait_ge(s_lo.handle, s_lo.at(t + 1))
                    dve.wait_ge(s_bias.handle, s_bias.at(t + 1))
                    dve.scalar_tensor_tensor(g.X[:, t, :], bank(4 + t % NR)[:, 0:D], 0.5, g.X[:, t, :], ALU.mult, ALU.add).then_inc(s_x.handle, 1)

                def partial_stats(t):
                    if rep == 0:
                        dve.wait_ge(s_x.handle, s_x.at(t + 1))
                        dve.bn_stats(g.ST[:, t, :], g.X[:, t, :])

                routed(0)
                for t in range(NR):
                    gated(t)
                routed(1)
                assert n[0] == LORA_STEPS, n[0]
                for t in range(NT):
                    updated(t)
                    if t + NR < NT:
                        gated(t + NR)
                    if t:
                        partial_stats(t - 1)
                partial_stats(NT - 1)


def mla_stage(nc, g, dram):
    S = lambda name: g.sem("mla_" + name)
    s_w, s_w2 = S("weights"), S("up_weights")
    s_mv, s_sd, s_rs = (g.sem("mla_" + n) for n in ("stats", "deviations", "reciprocals"))
    s_gp, s_gc, s_up, s_uc = S("absorbed_q_in_psum"), S("absorbed_q"), S("absorbed_v_in_psum"), S("absorbed_v")
    s_xn, s_xtp, s_xtc, s_cp, s_cc, s_sq = S("xn_tile"), S("xnT_in_psum"), S("xnT_copied"), S("latents_in_psum"), S("latents_copied"), S("squares")
    s_rd, s_rr, s_re, s_xb, s_xs = S("latent_deviations"), S("latent_scales"), S("latent_mean_squares"), S("sequence_xnT"), S("xnT_saved")
    s_cn, s_cn2, s_ctp, s_cq, s_ckh, s_ckl = S("latents"), S("latent_twice"), S("latentsT_in_psum"), S("cqT_copied"), S("latent_keys_high"), S("latent_keys_low")
    s_pr, s_ab, s_ro, s_rows = S("projected"), S("latent_queries"), S("rotary_products"), S("rotary_rows")
    s_qkp, s_hi, s_lo = S("qkT_in_psum"), S("high_parts"), S("low_parts")
    s_sc, s_mx, s_nb, s_p = S("scores"), S("row_max"), S("negative_max"), S("probs")
    s_ptp, s_ptc, s_ot, s_otc, s_bt = S("probsT_in_psum"), S("probsT_copied"), S("outT_in_psum"), S("outT_copied"), S("out_in_psum")
    s_dn, s_la = S("denominators"), S("latent_rows")
    s_lp, s_lc, s_o, s_x = S("latent_rowsT_in_psum"), S("latent_rowsT_copied"), S("outputs"), S("x_updated")
    NL = DQL + DKVL
    NU = 2 * TB
    with ExitStack() as ctx:
        sb = lambda name, shape, dt=F32: g.sb(ctx, "mla_" + name, shape, dt)
        WR = sb("Wrope", [P, KD, NP1 * 4 * RD])
        WD, WN = sb("Wdown", [P, KD, NL]), sb("norms", [P, NL])
        RO = sb("rope", [P, 2, TB, RD])
        GQ, UV = sb("GQ", [DQL, H1 * DKVL]), sb("UV", [P, NP1, D])
        bank, banks = g.bank, g.banks
        ident = g.C[:, C_ID:C_ID + P]
        kv = slice(DQL, NL)

        with ExitStack() as up:
            WQT, WKT, WVT = (g.sb(up, "mla_" + n, [P, H1, m]) for n, m in (("WqT", DQL), ("WkT", DKVL), ("WvT", DKVL)))
            WOU = g.sb(up, "mla_Wout", [P, H1, D])
            with nc.Block() as block:
                @block.sync
                def _(sp):
                    g.credit(sp)
                    for dst, name in ((WQT, "WqT"), (WKT, "WkT"), (WVT, "WvT"), (WOU, "Wout")):
                        sp.dma_start(dst[:, :, :], dram[name]).then_inc(s_w2.handle, 16)
                    sp.dma_start(WD[:, :, :], dram["Wdown"]).then_inc(s_w.handle, 16)
                    sp.dma_start(WN[:, :], dram["norms"].to_broadcast([P, NL])).then_inc(s_w.handle, 16)
                    sp.dma_start(RO[:, :, :, :], dram["rope"].rearrange("p c t d -> p c t d")).then_inc(s_w.handle, 16)
                    sp.dma_start(WR[:, :, :], dram["Wrope"]).then_inc(s_w.handle, 16)
                    sp.wait_ge(s_w.handle, s_w.at(64))
                    sp.wait_ge(s_w2.handle, s_w2.at(64))

                @block.tensor
                def _(pe):
                    pe.wait_ge(s_w2.handle, s_w2.at(64))
                    for h in range(H1):
                        ins = pe.matmul(bank(h // 8)[0:DQL, h % 8 * DKVL:(h % 8 + 1) * DKVL], WQT[:, h, :], WKT[:, h, :], start=True, stop=True)
                    ins.then_inc(s_gp.handle, 1)
                    for h in range(H1):
                        ins = pe.matmul(bank(2 + h // 4)[h % 2 * DKVL:(h % 2 + 1) * DKVL, h // 2 % 2 * D:(h // 2 % 2 + 1) * D],
                                        WVT[:, h, :], WOU[:, h, :], start=True, stop=True)
                    ins.then_inc(s_up.handle, 1)

                @block.scalar
                def _(act):
                    act.wait_ge(s_gp.handle, s_gp.at(1))
                    act.copy(GQ[:, :], banks(0, 2)[0:DQL, :]).then_inc(s_gc.handle, 1)
                    act.wait_ge(s_up.handle, s_up.at(1))
                    for m in range(4):
                        act.copy(UV[:, 2 * m:2 * m + 2, :].rearrange("p a d -> p (a d)"), bank(2 + m)[:, :]).then_inc(s_uc.handle, 1)

        XNS, XT = sb("XNS", [P, 2, D]), sb("XT", [P, KD, SEQ])
        CR, SQ, SS = sb("CR", [P, TB, NL]), sb("SQ", [P, 2, NL]), sb("SS", [P, 2, TB])
        SE, SD2, RS2 = sb("SE", [P, 2, TB]), sb("SD2", [P, 2, TB]), sb("RS2", [P, 2, TB])
        CN = sb("CN", [P, TB, DQL + 2 * DKVL])
        CQ = sb("CQ", [DQL, SEQ])
        QH, QL, KH, KL = (sb(n, [P, 2, 2, SEQ], F32R) for n in ("QH", "QL", "KH", "KL"))
        T1, T2 = sb("T1", [P, 2, 4 * RD]), sb("T2", [P, 2, 4 * RD])
        QR, KR = sb("QR", [P, 2, 6 * RD]), sb("KR", [P, 2, 2 * RD])
        PR, PT = sb("PR", [P, 2, SEQ]), sb("PT", [P, 2, 2, TB, P])
        MX, NB, DN, RD_ = sb("MX", [P, NU]), sb("NB", [P, NU]), sb("DN", [P, NU]), sb("RD", [P, 2])
        OT, LA = sb("OT", [P, P]), sb("LA", [P, TB, NP1 * P])
        LT = PR[:, :, :].rearrange("p u (k s) -> p u k s", s=P)

        steps = {}
        for j in range(TB):
            steps[7 * j // 2] = ("projections", j)
            steps[7 * j // 2 + 2] = ("transposes", j)
        assert len(steps) == 2 * TB and max(steps) < 2 * NU - 4

        def pairs_of_a_sequence(engine, b, pair):
            pair(b * NP1, 0, 0, True, False)
            with engine.Fori(0, NP1 // 2 - 1) as rr:
                pair(b * NP1 + 2 * rr + 1, 2 * rr + 1, 1, False, False)
                pair(b * NP1 + 2 * rr + 2, 2 * rr + 2, 0, False, False)
            pair(b * NP1 + NP1 - 1, NP1 - 1, 1, False, True)

        pr_bank = lambda j, alone: bank(j % 2) if alone else bank(7)
        tr_bank = lambda j, alone: bank(2 + j % 2) if alone else bank(7)
        lt_bank = lambda i, c: bank(4 - 2 * (i % 2) + c)

        with nc.Block() as block:
            @block.tensor
            def _(pe):
                with pe.Fori(0, BATCH) as b:
                    def xn_transposes(j):
                        pe.wait_ge(s_xn.handle, s_xn.at(TB * b + j + 1))
                        if j >= 2:
                            pe.wait_ge(s_xtc.handle, s_xtc.at(TB * b + j - 1))
                        for k in range(KD):
                            ins = pe.transpose(bank(j % 2)[:, k * P:(k + 1) * P], XNS[:, j % 2, k * P:(k + 1) * P], ident)
                        ins.then_inc(s_xtp.handle, 1)

                    xn_transposes(0)
                    for j in range(TB):
                        if j + 1 < TB:
                            xn_transposes(j + 1)
                        pe.wait_ge(s_xtc.handle, s_xtc.at(TB * b + j + 1))
                        if j >= 2:
                            pe.wait_ge(s_cc.handle, s_cc.at(TB * b + j - 1))
                        for k in range(KD):
                            ins = pe.matmul(bank(2 + j % 2)[:, 0:NL], XT[:, k, j * P:(j + 1) * P], WD[:, k, :], start=(k == 0), stop=(k == KD - 1))
                        ins.then_inc(s_cp.handle, 1)

                    def latent_transposes(j):
                        pe.wait_ge(s_cn2.handle, s_cn2.at(TB * b + j + 1))
                        if j >= 2:
                            pe.wait_ge(s_ckl.handle, s_ckl.at(2 * (TB * b + j - 1)))
                        pe.transpose(bank(4 + j % 2)[:, 0:P], CN[:, j, 0:P], ident)
                        pe.transpose(bank(4 + j % 2)[:, P:2 * P], CN[:, j, DQL:DQL + 2 * DKVL], ident).then_inc(s_ctp.handle, 1)

                    def projections(it, r, j, alone):
                        if not alone:
                            pe.wait_ge(s_lo.handle, s_lo.at(3 * (TB * it + j)))
                        else:
                            pe.wait_ge(s_cq.handle, s_cq.at(TB * b + j + 1))
                            pe.wait_ge(s_cc.handle, s_cc.at(TB * (b + 1)))
                            if j >= 2:
                                pe.wait_ge(s_ro.handle, s_ro.at(3 * (TB * it + j - 1)))
                        out = pr_bank(j, alone)
                        for k in range(KD):
                            pe.matmul(out[:, 0:4 * RD], XT[:, k, j * P:(j + 1) * P], WR[:, k, bass.ds(r * (4 * RD), 4 * RD)],
                                      start=(k == 0), stop=(k == KD - 1))
                        pe.matmul(out[:, 4 * RD:6 * RD], CQ[:, j * P:(j + 1) * P], GQ[:, bass.ds(r * (2 * RD), 2 * RD)],
                                  start=True, stop=True).then_inc(s_pr.handle, 1)

                    def transposes(it, j, alone):
                        pe.wait_ge(s_rows.handle, s_rows.at(2 * (TB * it + j + 1)))
                        if alone and j >= 2:
                            pe.wait_ge(s_lo.handle, s_lo.at(3 * (TB * it + j - 1)))
                        out = tr_bank(j, alone)
                        for m in range(2):
                            pe.transpose(out[:, m * P:(m + 1) * P], QR[:, j % 2, m * P:(m + 1) * P], ident)
                        pe.transpose(out[:, 2 * P:3 * P], KR[:, j % 2, :], ident).then_inc(s_qkp.handle, 1)

                    for j in range(TB + 2):
                        if j < TB:
                            latent_transposes(j)
                        if 1 <= j <= TB:
                            projections(b * NP1, 0, j - 1, True)
                        if j >= 2:
                            transposes(b * NP1, j - 2, True)
                    pe.wait_ge(s_ckl.handle, s_ckl.at(2 * TB * (b + 1)))

                    def scores_of(it, n, buf, free, between=None):
                        if n == 0:
                            pe.wait_ge(s_lo.handle, s_lo.at(3 * TB * (it + 1)))
                        if not free:
                            pe.wait_ge(s_p.handle, s_p.at(NU * it + n - 1))
                        qs = slice(n // 2 * P, (n // 2 + 1) * P)
                        for c in range(2):
                            if c and between:
                                between()
                            ks = slice(c * 512, (c + 1) * 512)
                            for m, (q, k) in enumerate(((QH, KH), (QL, KH), (QH, KL))):
                                ins = pe.matmul(bank(2 * (n % 2) + c)[:, :], q[:, buf, n % 2, qs], k[:, buf, n % 2, ks], start=(m == 0), stop=(m == 2))
                        ins.then_inc(s_sc.handle, 1)

                    def probs_transposes(it, n, free):
                        pe.wait_ge(s_p.handle, s_p.at(NU * it + n + 1))
                        for c in range(2):
                            if not free:
                                pe.wait_ge(s_ptc.handle, s_ptc.at(2 * (NU * it + n) + c - 1))
                            for k in range(4):
                                ins = pe.transpose(bank(4 + c)[:, k * P:(k + 1) * P], PR[:, n % 2, (4 * c + k) * P:(4 * c + k + 1) * P], ident)
                            ins.then_inc(s_ptp.handle, 1)

                    def values_of(tile, i, half, free):
                        if half == 0:
                            pe.wait_ge(s_ptc.handle, s_ptc.at(4 * (tile + 1)))
                            if not free:
                                pe.wait_ge(s_la.handle, s_la.at(tile))
                        for k in range(4 * half, 4 * half + 4):
                            for h in range(2):
                                ins = pe.matmul(bank(6)[h * DKVL:(h + 1) * DKVL, 0:P], CN[:, k, DQL:DQL + DKVL], PT[:, i % 2, h, k, :],
                                                start=(k == 0), stop=(k == TB - 1))
                        if half == 1:
                            ins.then_inc(s_ot.handle, 1)

                    def out_rows_of(tile):
                        pe.wait_ge(s_otc.handle, s_otc.at(tile + 1))
                        pe.transpose(bank(6)[:, P:2 * P], OT[:, :], ident).then_inc(s_bt.handle, 1)

                    def pair(it, r, buf, first, last):
                        def step(s):
                            if s in steps and not last:
                                what, j = steps[s]
                                if what == "projections":
                                    projections(it + 1, r + 1, j, False)
                                else:
                                    transposes(it + 1, j, False)

                        if first:
                            scores_of(it, 0, buf, True)
                        for n in range(NU):
                            rows = None
                            if n % 2 == 0 and (n >= 4 or not first):
                                rows = lambda: out_rows_of(TB * it + n // 2 - 2)
                            if n + 1 < NU:
                                scores_of(it, n + 1, buf, first and n == 0, rows)
                            elif not last:
                                scores_of(it + 1, 0, 1 - buf, False)
                            step(2 * n)
                            probs_transposes(it, n, first and n == 0)
                            if n >= 2 or not first:
                                values_of(TB * it + n // 2 - 1, (n // 2 - 1) % TB, n % 2, first and n < 4)
                            step(2 * n + 1)
                        if last:
                            out_rows_of(TB * it + TB - 2)
                            for half in range(2):
                                values_of(TB * it + TB - 1, TB - 1, half, False)
                            out_rows_of(TB * it + TB - 1)

                    pairs_of_a_sequence(pe, b, pair)

                    def rows_t(i):
                        for c in range(2):
                            if i >= 2:
                                pe.wait_ge(s_lc.handle, s_lc.at(2 * (TB * b + i) + c - 3))
                            for k in range(4):
                                ins = pe.transpose(lt_bank(i, c)[:, k * P:(k + 1) * P], LA[:, i, (4 * c + k) * P:(4 * c + k + 1) * P], ident)
                            ins.then_inc(s_lp.handle, 1)

                    pe.wait_ge(s_la.handle, s_la.at(TB * NP1 * (b + 1)))
                    rows_t(0)
                    for i in range(TB):
                        if i + 1 < TB:
                            rows_t(i + 1)
                        pe.wait_ge(s_lc.handle, s_lc.at(2 * (TB * b + i + 1)))
                        if i >= 2:
                            pe.wait_ge(s_x.handle, s_x.at(TB * b + i - 1))
                        for k in range(NP1):
                            ins = pe.matmul(bank(6 + i % 2)[:, 0:D], LT[:, i % 2, k, :], UV[:, k, :], start=(k == 0), stop=(k == NP1 - 1))
                        ins.then_inc(s_o.handle, 1)
                    pe.wait_ge(s_x.handle, s_x.at(TB * (b + 1)))

            @block.scalar
            def _(act):
                norm_sd_act(act, g, s_mv, s_sd)
                with act.Fori(0, BATCH) as b:
                    def latents(j):
                        act.wait_ge(s_cp.handle, s_cp.at(TB * b + j + 1))
                        for m, cols in enumerate((slice(0, DQL), kv)):
                            if j >= 2:
                                act.wait_ge(s_sq.handle, s_sq.at(2 * (TB * b + j - 2) + m + 1))
                            act.activation(SQ[:, j % 2, cols], bank(2 + j % 2)[:, cols], ACT.Square, accum_out=SS[:, m, j:j + 1]).then_inc(s_sq.handle, 1)
                        act.copy(CR[:, j, :], bank(2 + j % 2)[:, 0:NL]).then_inc(s_cc.handle, 1)

                    for j in range(TB):
                        act.wait_ge(s_xtp.handle, s_xtp.at(TB * b + j + 1))
                        act.copy(XT[:, :, j * P:(j + 1) * P], bank(j % 2)[:, 0:KD * P].rearrange("p (k s) -> p k s", s=P)).then_inc(s_xtc.handle, 1)
                        if j:
                            latents(j - 1)
                    latents(TB - 1)
                    act.wait_ge(s_re.handle, s_re.at(b + 1))
                    act.activation(SD2[:, :, :], SE[:, :, :], ACT.Sqrt, bias=g.C[:, C_EPS + 1:C_EPS + 2]).then_inc(s_rd.handle, 1)
                    nc.scalar.preload_act_table(ACT.Exp)
                    def latents_t(j):
                        tok = slice(j * P, (j + 1) * P)
                        act.wait_ge(s_ctp.handle, s_ctp.at(TB * b + j + 1))
                        act.copy(CQ[:, tok], bank(4 + j % 2)[0:DQL, 0:P]).then_inc(s_cq.handle, 1)
                        act.copy(KH[DKVL:P, :, 0, tok], bcast(bank(4 + j % 2)[DKVL:P, P:2 * P], 1, 2)).then_inc(s_ckh.handle, 1)
                        act.copy(KH[0:DKVL, :, 1, tok], bcast(bank(4 + j % 2)[0:DKVL, P:2 * P], 1, 2)).then_inc(s_ckh.handle, 1)

                    def latent_queries(it, j, alone):
                        act.wait_ge(s_pr.handle, s_pr.at(TB * it + j + 1))
                        if j >= 2:
                            act.wait_ge(s_qkp.handle, s_qkp.at(TB * it + j - 1))
                        act.copy(QR[:, j % 2, RD:3 * RD], pr_bank(j, alone)[:, 4 * RD:6 * RD]).then_inc(s_ab.handle, 1)

                    def highs(it, buf, j, alone):
                        tok = slice(j * P, (j + 1) * P)
                        rows_t = tr_bank(j, alone)
                        act.wait_ge(s_qkp.handle, s_qkp.at(TB * it + j + 1))
                        act.copy(QH[:, buf, :, tok], rows_t[:, 0:2 * P].rearrange("p (m s) -> p m s", m=2)).then_inc(s_hi.handle, 1)
                        act.copy(KH[0:RD, buf, 0, tok], rows_t[0:RD, 2 * P:3 * P]).then_inc(s_hi.handle, 1)
                        act.copy(KH[RD:P, buf, 1, tok], rows_t[RD:P, 2 * P:3 * P]).then_inc(s_hi.handle, 1)

                    for j in range(TB + 2):
                        if j < TB:
                            latents_t(j)
                        if 1 <= j <= TB:
                            latent_queries(b * NP1, j - 1, True)
                        if j >= 2:
                            highs(b * NP1, 0, j - 2, True)

                    def exp_of(it, n, free):
                        act.wait_ge(s_nb.handle, s_nb.at(NU * it + n + 1))
                        if not free:
                            act.wait_ge(s_ptp.handle, s_ptp.at(2 * (NU * it + n - 1)))
                        act.activation(PR[:, n % 2, :], banks(2 * (n % 2), 2)[:, :], ACT.Exp, bias=NB[:, n:n + 1], scale=MLA_SCALE,
                                       accum_out=DN[:, n:n + 1]).then_inc(s_p.handle, 1)

                    def pair(it, r, buf, first, last):
                        def step(s):
                            if s in steps and not last:
                                what, j = steps[s]
                                if what == "projections":
                                    latent_queries(it + 1, j, False)
                                else:
                                    highs(it + 1, 1 - buf, j, False)

                        if first:
                            exp_of(it, 0, True)
                        for n in range(NU):
                            i, h = n // 2, n % 2
                            step(2 * n - 1)
                            step(2 * n)
                            for c in range(2):
                                act.wait_ge(s_ptp.handle, s_ptp.at(2 * (NU * it + n) + c + 1))
                                if h == 0 and c == 0 and (i >= 2 or not first):
                                    act.wait_ge(s_ot.handle, s_ot.at(TB * it + i - 1))
                                act.copy(PT[:, i % 2, h, 4 * c:4 * c + 4, :], bank(4 + c)[:, :].rearrange("p (k s) -> p k s", s=P)).then_inc(s_ptc.handle, 1)
                            if n + 1 < NU:
                                exp_of(it, n + 1, first and n == 0)
                            elif not last:
                                exp_of(it + 1, 0, False)

                    pairs_of_a_sequence(act, b, pair)

                    for i in range(TB):
                        for c in range(2):
                            act.wait_ge(s_lp.handle, s_lp.at(2 * (TB * b + i) + c + 1))
                            if i >= 2 and c == 0:
                                act.wait_ge(s_o.handle, s_o.at(TB * b + i - 1))
                            act.copy(LT[:, i % 2, 4 * c:4 * c + 4, :], lt_bank(i, c)[:, :].rearrange("p (k s) -> p k s", s=P)).then_inc(s_lc.handle, 1)

            @block.gpsimd
            def _(pool):
                with pool.Fori(0, BATCH * NP1) as it:
                    for j in range(TB):
                        u = j % 2
                        pool.wait_ge(s_ro.handle, s_ro.at(3 * (TB * it + j + 1)))
                        if j >= 2:
                            pool.wait_ge(s_qkp.handle, s_qkp.at(TB * it + j - 1))
                        heads = lambda ap: ap.rearrange("p (m d) -> p m d", m=2)
                        qr = QR[:, u, :].rearrange("p (m d) -> p m d", m=2)[:, :, 0:RD]
                        pool.tensor_tensor(qr, heads(T1[:, u, 0:2 * RD]), heads(T2[:, u, 0:2 * RD]), ALU.add).then_inc(s_rows.handle, 1)
                        pool.tensor_tensor(KR[:, u, :], T1[:, u, 2 * RD:4 * RD], T2[:, u, 2 * RD:4 * RD], ALU.add).then_inc(s_rows.handle, 1)

            @block.vector
            def _(dve):
                norm_stats_dve(dve, g, s_mv)
                norm_rs_dve(dve, g, s_sd, s_rs)
                with dve.Fori(0, BATCH) as b:
                    for j in range(TB):
                        if j >= 2:
                            dve.wait_ge(s_xtp.handle, s_xtp.at(TB * b + j - 1))
                        normalize(dve, g, XNS[:, j % 2, :], b * TB + j).then_inc(s_xn.handle, 1)
                    dve.wait_ge(s_cc.handle, s_cc.at(TB * (b + 1)))
                    for m, n in enumerate((DQL, DKVL)):
                        ins = dve.tensor_scalar(SE[:, m, :], SS[:, m, :], 1.0 / n, None, ALU.mult)
                    ins.then_inc(s_re.handle, 1)
                    dve.wait_ge(s_rd.handle, s_rd.at(b + 1))
                    dve.reciprocal(RS2[:, :, :], SD2[:, :, :]).then_inc(s_rr.handle, 1)
                    dve.wait_ge(s_rr.handle, s_rr.at(b + 1))
                    for j in range(TB):
                        dve.scalar_tensor_tensor(CN[:, j, 0:DQL], CR[:, j, 0:DQL], RS2[:, 0, j:j + 1], WN[:, 0:DQL], ALU.mult, ALU.mult)
                        for m in range(2):
                            ins = dve.scalar_tensor_tensor(CN[:, j, DQL + m * DKVL:DQL + (m + 1) * DKVL], CR[:, j, kv], RS2[:, 1, j:j + 1],
                                                           WN[:, kv], ALU.mult, ALU.mult)
                        ins.then_inc(s_cn2.handle, 1)

                    def latent_lows(j):
                        tok = slice(j * P, (j + 1) * P)
                        dve.wait_ge(s_ckh.handle, s_ckh.at(2 * (TB * b + j + 1)))
                        for h, rows in ((0, slice(DKVL, P)), (1, slice(0, DKVL))):
                            dve.tensor_tensor(KL[rows, :, h, tok], bcast(bank(4 + j % 2)[rows, P:2 * P], 1, 2), KH[rows, :, h, tok].bitcast(F32),
                                              ALU.subtract).then_inc(s_ckl.handle, 1)

                    def rotary(it, j, alone):
                        u = j % 2
                        dve.wait_ge(s_ab.handle, s_ab.at(TB * it + j + 1))
                        if j >= 2:
                            dve.wait_ge(s_rows.handle, s_rows.at(2 * (TB * it + j - 1)))
                        rot = pr_bank(j, alone)[:, 0:4 * RD].rearrange("p (m d) -> p m d", d=RD)
                        t1, t2 = (t[:, u, :].rearrange("p (m d) -> p m d", d=RD) for t in (T1, T2))
                        half = RD // 2
                        dve.tensor_tensor(t1, rot, bcast(RO[:, 0, j, :], 1, 4), ALU.mult).then_inc(s_ro.handle, 1)
                        dve.tensor_tensor(t2[:, :, 0:half], rot[:, :, half:RD], bcast(RO[:, 1, j, 0:half], 1, 4), ALU.mult).then_inc(s_ro.handle, 1)
                        dve.tensor_tensor(t2[:, :, half:RD], rot[:, :, 0:half], bcast(RO[:, 1, j, half:RD], 1, 4), ALU.mult).then_inc(s_ro.handle, 1)

                    def lows(it, buf, j, alone):
                        tok = slice(j * P, (j + 1) * P)
                        rows_t = tr_bank(j, alone)
                        dve.wait_ge(s_hi.handle, s_hi.at(3 * (TB * it + j + 1)))
                        dve.tensor_tensor(QL[:, buf, :, tok], rows_t[:, 0:2 * P].rearrange("p (m s) -> p m s", m=2),
                                          QH[:, buf, :, tok].bitcast(F32), ALU.subtract).then_inc(s_lo.handle, 1)
                        for h, rows in ((0, slice(0, RD)), (1, slice(RD, P))):
                            dve.tensor_tensor(KL[rows, buf, h, tok], rows_t[rows, 2 * P:3 * P], KH[rows, buf, h, tok].bitcast(F32), ALU.subtract).then_inc(s_lo.handle, 1)

                    for j in range(TB + 2):
                        if j < TB:
                            latent_lows(j)
                        if 1 <= j <= TB:
                            rotary(b * NP1, j - 1, True)
                        if j >= 2:
                            lows(b * NP1, 0, j - 2, True)

                    def max_of(it, n):
                        dve.wait_ge(s_sc.handle, s_sc.at(NU * it + n + 1))
                        dve.tensor_reduce(MX[:, n:n + 1], banks(2 * (n % 2), 2)[:, :], AX_X, ALU.max).then_inc(s_mx.handle, 1)
                        dve.wait_ge(s_mx.handle, s_mx.at(NU * it + n + 1))
                        dve.tensor_scalar(NB[:, n:n + 1], MX[:, n:n + 1], -MLA_SCALE, None, ALU.mult).then_inc(s_nb.handle, 1)

                    def out_copy(tile):
                        dve.wait_ge(s_ot.handle, s_ot.at(tile + 1))
                        dve.tensor_copy(OT[:, :], bank(6)[:, 0:P]).then_inc(s_otc.handle, 1)

                    def finish(tile, i, r):
                        dve.reciprocal(RD_[:, :], DN[:, 2 * i:2 * i + 2]).then_inc(s_dn.handle, 1)
                        dve.wait_ge(s_dn.handle, s_dn.at(tile + 1))
                        dve.wait_ge(s_bt.handle, s_bt.at(tile + 1))
                        dve.tensor_tensor(LA[:, i, bass.ds(r * P, P)].rearrange("p (h d) -> p h d", h=2),
                                          bank(6)[:, P:2 * P].rearrange("p (h d) -> p h d", h=2), bcast(RD_[:, :], 2, DKVL), ALU.mult).then_inc(s_la.handle, 1)

                    def pair(it, r, buf, first, last):
                        def step(s):
                            if s in steps and not last:
                                what, j = steps[s]
                                if what == "projections":
                                    rotary(it + 1, j, False)
                                else:
                                    lows(it + 1, 1 - buf, j, False)

                        if first:
                            max_of(it, 0)
                        for n in range(NU):
                            ends = n % 2 == 0 and (n >= 4 or not first)
                            tile, i = TB * it + n // 2 - 2, (n // 2 - 2) % TB
                            if ends:
                                out_copy(tile)
                            step(2 * n - 1)
                            if ends:
                                finish(tile, i, r if n >= 4 else r - 1)
                            if n + 1 < NU:
                                max_of(it, n + 1)
                            elif not last:
                                max_of(it + 1, 0)
                            step(2 * n)
                        if last:
                            for i in (TB - 2, TB - 1):
                                out_copy(TB * it + i)
                                finish(TB * it + i, i, r)

                    pairs_of_a_sequence(dve, b, pair)

                    for i in range(TB):
                        dve.wait_ge(s_o.handle, s_o.at(TB * b + i + 1))
                        xt = g.X[:, b * TB + i, :]
                        dve.tensor_tensor(xt, bank(6 + i % 2)[:, 0:D], xt, ALU.add).then_inc(s_x.handle, 1)
                        dve.wait_ge(s_x.handle, s_x.at(TB * b + i + 1))
                        dve.bn_stats(g.ST[:, b * TB + i, :], xt)


def store_stage(nc, g, out):
    s_out = g.sem("stored")
    with nc.Block() as block:
        @block.sync
        def _(sp):
            g.credit(sp)
            sp.dma_start(out.rearrange("b (t p) d -> p (b t) d", p=P), g.X[:, :, :]).then_inc(s_out.handle, 16)
            sp.wait_ge(s_out.handle, s_out.at(16))


def macaron_program(nc, dram, out, stages="mamlLl"):
    with ExitStack() as ctx:
        g = Core(nc, ctx)
        g.X = g.sb(ctx, "X", [P, NT, D])
        g.C = g.sb(ctx, "C", [P, C_END])
        g.ST = g.sb(ctx, "ST", [P, NT, 6])
        g.MV = g.sb(ctx, "MV", [P, NT, 2])
        g.SD = g.sb(ctx, "SD", [P, NT])
        g.Z = g.sb(ctx, "Z", [P, D])
        g.RS = g.sb(ctx, "RS", [P, NT])
        g.XG = nc.dram_tensor("slots_in", [NE * ROWS + P, D], F32, kind="Internal").ap()
        g.YG = nc.dram_tensor("slots_out", [NTILE * P, D], F32, kind="Internal").ap()
        PS = ctx.enter_context(nc.psum_tensor("PS", [P, 8, 512], F32))
        g.bank = lambda n: PS[:, n, :]
        g.banks = lambda n, m: PS[:, n:n + m, :].rearrange("p b c -> p (b c)")
        g.s_w1 = g.sem("loaded_W1")
        g.s_second = [g.sem(f"second_added{r}") for r in range(2)]
        with ExitStack() as moe:
            g.XN = g.sb(moe, "XN", [P, NT, D])
            g.W1 = g.sb(moe, "W1", [P, NE, KD, FF])
            load_stage(nc, g, dram)
            moe_stage(nc, g, dram, 0)
            if "a" in stages:
                attention_stage(nc, g, dram)
            if stages.count("m") > 1:
                moe_stage(nc, g, dram, 1)
        if "l" in stages:
            lora_stage(nc, g, dram, 0)
        if "L" in stages:
            mla_stage(nc, g, dram)
        if stages.count("l") > 1:
            lora_stage(nc, g, dram, 1)
        store_stage(nc, g, out)


def shape_constants():
    c = np.zeros((P, C_END), np.float32)
    c[:, C_ID:C_ID + P] = np.eye(P)
    c[:, C_ONE:C_ONE + P] = 1.0
    c[:, C_TRI:C_TRI + P] = np.triu(np.ones((P, P)), 1)
    c[:, C_LOW:C_LOW + P] = np.tril(np.ones((P, P)))
    c[:, C_IOTA:C_IOTA + NE] = np.arange(NE)
    c[:, C_TILE:C_TILE + NTILE + 2] = np.arange(NTILE + 2)
    c[:, C_EPS] = LN_EPS
    c[:, C_EPS + 1] = RMS_EPS
    freqs = (np.float32(1.0) / np.float32(10000.0) ** (np.arange(0, RD, 2, dtype=np.float32) / np.float32(RD))).astype(np.float32)
    ang = np.outer(np.arange(SEQ, dtype=np.float32), freqs).astype(np.float32)
    cos, sin = np.cos(ang).astype(np.float32), np.sin(ang).astype(np.float32)
    rope = np.stack([np.concatenate([cos, cos], 1), np.concatenate([-sin, sin], 1)])
    rope = rope.reshape(2, TB, P, RD).transpose(2, 0, 1, 3)
    return c, np.ascontiguousarray(rope)


def lay_out(a):
    f = np.ascontiguousarray
    chunks = lambda w: w.reshape(w.shape[0] // P, P, -1).transpose(1, 0, 2)
    const, rope = shape_constants()
    r = {"const": const, "rope": rope, "x": f(a["L0_attn_x"].reshape(BATCH * SEQ, D))}
    r["router_w"] = f(chunks(a["L0_ffn_router_w"]))
    r["W1"] = f(a["L0_ffn_W1"].reshape(NE, KD, P, FF).transpose(2, 0, 1, 3))
    r["W2"] = f(a["L0_ffn_W2"].reshape(NE, KF, P, D).transpose(2, 0, 1, 3))
    heads = lambda w: w.reshape(D, NG0, HG * DH0)
    r["Wqkv"] = f(chunks(np.concatenate([heads(a["L0_attn_Wq"]), heads(a["L0_attn_Wk"]), heads(a["L0_attn_Wv"])], 2).reshape(D, -1)))
    r["Wo"] = f(chunks(a["L0_attn_Wo"]))
    pairs = lambda w: w.reshape(D, NP1, 2, RD // 2, 2).transpose(0, 1, 2, 4, 3).reshape(D, NP1, 1, 2 * RD)
    r["Wrope"] = f(chunks(np.concatenate([pairs(a["L1_attn_Wq_rope"]), pairs(a["L1_attn_Wk_rope"])], 2).reshape(D, -1)))
    r["Wdown"] = f(chunks(np.concatenate([a["L1_attn_Wq_down"], a["L1_attn_Wkv_down"]], 1)))
    r["norms"] = f(np.concatenate([a["L1_attn_q_norm_w"], a["L1_attn_kv_norm_w"]]).reshape(1, -1))
    up = lambda w: f(w.reshape(-1, H1, HD1).transpose(2, 1, 0))
    r["WqT"], r["WkT"], r["WvT"] = up(a["L1_attn_Wq_up"]), up(a["L1_attn_Wk_up"]), up(a["L1_attn_Wv_up"])
    r["Wout"] = f(a["L1_attn_Wout"].reshape(H1, HD1, D).transpose(1, 0, 2))
    r["Wbase"] = f(chunks(np.ascontiguousarray(a["L1_ffn_base_w"].T)))
    lora = a["L1_ffn_lora_A"].transpose(1, 0, 2).reshape(D, LE * LR)
    r["Wlora"] = f(chunks(np.concatenate([lora, a["L1_ffn_router_w"].T], 1)))
    r["Blora"] = f(a["L1_ffn_lora_B"].reshape(LE * LR, D))
    r["biases"] = f(np.concatenate([a["L1_ffn_base_b"], a["L1_ffn_router_b"]]).reshape(1, -1))
    return r


def kernel(**inputs):
    import concourse.bacc as _bacc
    from concourse.bass_utils import run_bass_kernel_spmd as _run

    nc = _bacc.Bacc("TRN2", target_bir_lowering=False, num_devices=1)
    arrays, dram = {}, {}
    for name, a in lay_out({k: np.asarray(v) for k, v in inputs.items()}).items():
        arrays[f"in_{name}_dram"] = a
        dram[name] = nc.dram_tensor(f"in_{name}_dram", a.shape, F32, kind="ExternalInput").ap()
    out = nc.dram_tensor("out_0_dram", (BATCH, SEQ, D), F32, kind="ExternalOutput").ap()
    macaron_program(nc, dram, out)
    r = _run(nc, [arrays], core_ids=[0])
    return r.results[0]["out_0_dram"]
```
